# Optimizing a Trainium2 kernel written in Bass

```python
import numpy as np
import jax
import jax.numpy as jnp

def _softmax(x, axis=-1):
    return jax.nn.softmax(x, axis=axis)

def _gelu(x):
    return jax.nn.gelu(x, approximate=True)

def _silu(x):
    return jax.nn.silu(x)

def _sigmoid(x):
    return jax.nn.sigmoid(x)

def _layernorm(x, axis=-1, eps=1e-05):
    m = jnp.mean(x, axis=axis, keepdims=True)
    v = jnp.var(x, axis=axis, keepdims=True)
    return (x - m) / jnp.sqrt(v + eps)

def _scatter_add(tgt, idx, src, axis=0):
    return tgt.at[idx].add(src)

def _segment_sum(src, seg, n):
    return jax.ops.segment_sum(src, seg, n)
kernel_name = 'mk_cond_seq_d2_seqx_r8_be7c54'

def setup_inputs(seed: int=0):
    np.random.seed(seed)
    _w = jnp.asarray

    def _rec_inputs():
        import jax
        import jax.numpy as jnp
        _rk = jax.random.key(seed)
        x = 7.22e-05 + 1 * jax.random.normal(jax.random.fold_in(_rk, 1), (4, 256, 128), jnp.float32)
        _lenS = 256 - jax.random.randint(jax.random.fold_in(_rk, 7), (4,), 0, max(1, 256 // 4) + 1, jnp.int32)
        _lenS2 = 256 - jax.random.randint(jax.random.fold_in(_rk, 8), (4,), 0, max(1, 256 // 4) + 1, jnp.int32)
        cond_1024 = 0.0061147 + 1.02565 * jax.random.normal(jax.random.fold_in(_rk, 11), (4, 128), jnp.float32)
        return (x, cond_1024)
    x, cond_1024 = _rec_inputs()

    def _L0_cond_setup():
        import jax, jax.numpy as jnp
        import numpy as np
        DIM = 128
        MLP_RATIO = 4
        EPS = 1e-06

        def rmsnorm(x, w):
            return x * jax.lax.rsqrt(jnp.mean(x * x, axis=-1, keepdims=True) + EPS) * w

        def film(x, cond, w, b):
            ss = cond @ w + b
            scale, shift = jnp.split(ss, 2, axis=-1)
            return x * (1.0 + scale[:, None, :]) + shift[:, None, :]
        key = jax.random.key(seed)
        ks = jax.random.split(key, 16)
        B, N, D = (4, 256, DIM)
        H = D * MLP_RATIO
        s = lambda fan_in: 1.0 / np.sqrt(fan_in)
        return {'x': jax.random.normal(ks[0], (B, N, D), jnp.float32), 'cond': jax.random.normal(ks[1], (B, D), jnp.float32), 'norm1_w': jnp.ones((D,), jnp.float32), 'film1_w': jax.random.normal(ks[2], (D, 2 * D), jnp.float32) * s(D), 'film1_b': jnp.zeros((2 * D,), jnp.float32), 'q_w': jax.random.normal(ks[3], (D, D), jnp.float32) * s(D), 'q_b': jnp.zeros((D,), jnp.float32), 'k_w': jax.random.normal(ks[4], (D, D), jnp.float32) * s(D), 'k_b': jnp.zeros((D,), jnp.float32), 'v_w': jax.random.normal(ks[5], (D, D), jnp.float32) * s(D), 'v_b': jnp.zeros((D,), jnp.float32), 'proj_w': jax.random.normal(ks[6], (D, D), jnp.float32) * s(D), 'proj_b': jnp.zeros((D,), jnp.float32), 'norm2_w': jnp.ones((D,), jnp.float32), 'film2_w': jax.random.normal(ks[7], (D, 2 * D), jnp.float32) * s(D), 'film2_b': jnp.zeros((2 * D,), jnp.float32), 'mlp_w1': jax.random.normal(ks[8], (D, H), jnp.float32) * s(D), 'mlp_b1': jnp.zeros((H,), jnp.float32), 'mlp_w2': jax.random.normal(ks[9], (H, D), jnp.float32) * s(H), 'mlp_b2': jnp.zeros((D,), jnp.float32)}
    _L0_cond_all = _L0_cond_setup()
    _L0_cond_in = {k: v for k, v in _L0_cond_all.items() if k in ('norm1_w', 'film1_w', 'film1_b', 'q_w', 'q_b', 'k_w', 'k_b', 'v_w', 'v_b', 'proj_w', 'proj_b', 'norm2_w', 'film2_w', 'film2_b', 'mlp_w1', 'mlp_b1', 'mlp_w2', 'mlp_b2')}
    del _L0_cond_all

    def _L1_cond_setup():
        import jax, jax.numpy as jnp
        import numpy as np
        B, N, D = (2, 256, 128)
        H, HD = (16, 64)
        E, DD = (8, 512)
        EPS = 1e-05

        def _ln(x, g, b):
            m = jnp.mean(x, axis=-1, keepdims=True)
            v = jnp.var(x, axis=-1, keepdims=True)
            return (x - m) * jax.lax.rsqrt(v + EPS) * g + b
        key = jax.random.key(seed)
        ks = jax.random.split(key, 16)
        s = 0.02
        return {'x': jax.random.normal(ks[0], (B, N, D), jnp.float32), 't': jax.random.normal(ks[1], (B, 1, D), jnp.float32), 'W_ada': jax.random.normal(ks[2], (D, D), jnp.float32) * s, 'b_ada': jnp.zeros((D,), jnp.float32), 'ln1_g': jnp.ones((D,), jnp.float32), 'ln1_b': jnp.zeros((D,), jnp.float32), 'Wqkv': jax.random.normal(ks[3], (3 * H * HD, D), jnp.float32) * s, 'qn_g': jnp.ones((HD,), jnp.float32), 'qn_b': jnp.zeros((HD,), jnp.float32), 'kn_g': jnp.ones((HD,), jnp.float32), 'kn_b': jnp.zeros((HD,), jnp.float32), 'Wout': jax.random.normal(ks[4], (D, H * HD), jnp.float32) * s, 'mlp_g': jnp.ones((D,), jnp.float32), 'mlp_b': jnp.zeros((D,), jnp.float32), 'Wgate': jax.random.normal(ks[5], (E, D), jnp.float32) * s, 'fc1s': jax.random.normal(ks[6], (E, DD, D), jnp.float32) * s, 'b1s': jnp.zeros((E, DD), jnp.float32), 'fc2s': jax.random.normal(ks[7], (E, D, DD), jnp.float32) * s, 'b2s': jnp.zeros((E, D), jnp.float32)}
    _L1_cond_all = _L1_cond_setup()
    _L1_cond_in = {k: v for k, v in _L1_cond_all.items() if k in ('W_ada', 'b_ada', 'ln1_g', 'ln1_b', 'Wqkv', 'qn_g', 'qn_b', 'kn_g', 'kn_b', 'Wout', 'mlp_g', 'mlp_b', 'Wgate', 'fc1s', 'b1s', 'fc2s', 'b2s')}
    del _L1_cond_all
    return {'x': x, 'cond_1024': cond_1024, 'L0_cond_norm1_w': _L0_cond_in['norm1_w'], 'L0_cond_film1_w': _L0_cond_in['film1_w'], 'L0_cond_film1_b': _L0_cond_in['film1_b'], 'L0_cond_q_w': _L0_cond_in['q_w'], 'L0_cond_q_b': _L0_cond_in['q_b'], 'L0_cond_k_w': _L0_cond_in['k_w'], 'L0_cond_k_b': _L0_cond_in['k_b'], 'L0_cond_v_w': _L0_cond_in['v_w'], 'L0_cond_v_b': _L0_cond_in['v_b'], 'L0_cond_proj_w': _L0_cond_in['proj_w'], 'L0_cond_proj_b': _L0_cond_in['proj_b'], 'L0_cond_norm2_w': _L0_cond_in['norm2_w'], 'L0_cond_film2_w': _L0_cond_in['film2_w'], 'L0_cond_film2_b': _L0_cond_in['film2_b'], 'L0_cond_mlp_w1': _L0_cond_in['mlp_w1'], 'L0_cond_mlp_b1': _L0_cond_in['mlp_b1'], 'L0_cond_mlp_w2': _L0_cond_in['mlp_w2'], 'L0_cond_mlp_b2': _L0_cond_in['mlp_b2'], 'L1_cond_W_ada': _L1_cond_in['W_ada'], 'L1_cond_b_ada': _L1_cond_in['b_ada'], 'L1_cond_ln1_g': _L1_cond_in['ln1_g'], 'L1_cond_ln1_b': _L1_cond_in['ln1_b'], 'L1_cond_Wqkv': _L1_cond_in['Wqkv'], 'L1_cond_qn_g': _L1_cond_in['qn_g'], 'L1_cond_qn_b': _L1_cond_in['qn_b'], 'L1_cond_kn_g': _L1_cond_in['kn_g'], 'L1_cond_kn_b': _L1_cond_in['kn_b'], 'L1_cond_Wout': _L1_cond_in['Wout'], 'L1_cond_mlp_g': _L1_cond_in['mlp_g'], 'L1_cond_mlp_b': _L1_cond_in['mlp_b'], 'L1_cond_Wgate': _L1_cond_in['Wgate'], 'L1_cond_fc1s': _L1_cond_in['fc1s'], 'L1_cond_b1s': _L1_cond_in['b1s'], 'L1_cond_fc2s': _L1_cond_in['fc2s'], 'L1_cond_b2s': _L1_cond_in['b2s']}

def reference(x, cond_1024, L0_cond_norm1_w, L0_cond_film1_w, L0_cond_film1_b, L0_cond_q_w, L0_cond_q_b, L0_cond_k_w, L0_cond_k_b, L0_cond_v_w, L0_cond_v_b, L0_cond_proj_w, L0_cond_proj_b, L0_cond_norm2_w, L0_cond_film2_w, L0_cond_film2_b, L0_cond_mlp_w1, L0_cond_mlp_b1, L0_cond_mlp_w2, L0_cond_mlp_b2, L1_cond_W_ada, L1_cond_b_ada, L1_cond_ln1_g, L1_cond_ln1_b, L1_cond_Wqkv, L1_cond_qn_g, L1_cond_qn_b, L1_cond_kn_g, L1_cond_kn_b, L1_cond_Wout, L1_cond_mlp_g, L1_cond_mlp_b, L1_cond_Wgate, L1_cond_fc1s, L1_cond_b1s, L1_cond_fc2s, L1_cond_b2s):
    import jax
    import jax.numpy as jnp

    def _L0_cond_ref(x, cond, norm1_w, film1_w, film1_b, q_w, q_b, k_w, k_b, v_w, v_b, proj_w, proj_b, norm2_w, film2_w, film2_b, mlp_w1, mlp_b1, mlp_w2, mlp_b2):
        import jax, jax.numpy as jnp
        import numpy as np
        DIM = 128
        MLP_RATIO = 4
        EPS = 1e-06

        def rmsnorm(x, w):
            return x * jax.lax.rsqrt(jnp.mean(x * x, axis=-1, keepdims=True) + EPS) * w

        def film(x, cond, w, b):
            ss = cond @ w + b
            scale, shift = jnp.split(ss, 2, axis=-1)
            return x * (1.0 + scale[:, None, :]) + shift[:, None, :]
        B, N, D = x.shape
        x_in = x
        h = film(rmsnorm(x, norm1_w), cond, film1_w, film1_b)
        Q = h @ q_w + q_b
        K = h @ k_w + k_b
        V = h @ v_w + v_b
        scores = jnp.einsum('bnd,bmd->bnm', Q, K) * D ** (-0.5)
        attn = jax.nn.softmax(scores, axis=-1)
        out = jnp.einsum('bnm,bmd->bnd', attn, V)
        x = x_in + (out @ proj_w + proj_b)
        x_in = x
        h = film(rmsnorm(x, norm2_w), cond, film2_w, film2_b)
        h = jax.nn.gelu(h @ mlp_w1 + mlp_b1, approximate=False) @ mlp_w2 + mlp_b2
        return x_in + h

    def _L1_cond_ref(x, t, W_ada, b_ada, ln1_g, ln1_b, Wqkv, qn_g, qn_b, kn_g, kn_b, Wout, mlp_g, mlp_b, Wgate, fc1s, b1s, fc2s, b2s):
        import jax, jax.numpy as jnp
        import numpy as np
        B, N, D = (2, 256, 128)
        H, HD = (16, 64)
        E, DD = (8, 512)
        EPS = 1e-05

        def _ln(x, g, b):
            m = jnp.mean(x, axis=-1, keepdims=True)
            v = jnp.var(x, axis=-1, keepdims=True)
            return (x - m) * jax.lax.rsqrt(v + EPS) * g + b
        b, n, d = x.shape
        shift = jax.nn.silu(t) @ W_ada.T + b_ada
        h = _ln(x, ln1_g, ln1_b) + shift
        qkv = (h @ Wqkv.T).reshape(b, n, 3, H, HD)
        q = _ln(qkv[:, :, 0].transpose(0, 2, 1, 3), qn_g, qn_b)
        k = _ln(qkv[:, :, 1].transpose(0, 2, 1, 3), kn_g, kn_b)
        v = qkv[:, :, 2].transpose(0, 2, 1, 3)
        scores = jnp.einsum('bhnd,bhmd->bhnm', q, k) / jnp.sqrt(jnp.float32(HD))
        attn = jax.nn.softmax(scores, axis=-1)
        o = jnp.einsum('bhnm,bhmd->bhnd', attn, v)
        o = o.transpose(0, 2, 1, 3).reshape(b, n, H * HD)
        x = x + o @ Wout.T
        tok = x.reshape(-1, d)
        bs = tok.shape[0]
        gate = jax.nn.softmax(tok @ Wgate.T, axis=-1)
        k_cap = bs // E
        vals, idx = jax.lax.top_k(gate.T, k_cap)
        idx_flat = idx.T.reshape(-1)
        w = vals.T
        g = _ln(tok[idx_flat], mlp_g, mlp_b).reshape(k_cap, E, d)
        y = jnp.einsum('ked,ehd->keh', g, fc1s) + b1s
        y = jax.nn.gelu(y, approximate=True)
        y = jnp.einsum('keh,edh->ked', y, fc2s) + b2s
        y = y * w[..., None]
        tok = tok.at[idx_flat].add(y.reshape(-1, d))
        return tok.reshape(x.shape)
    x = _L0_cond_ref(x, cond_1024, L0_cond_norm1_w, L0_cond_film1_w, L0_cond_film1_b, L0_cond_q_w, L0_cond_q_b, L0_cond_k_w, L0_cond_k_b, L0_cond_v_w, L0_cond_v_b, L0_cond_proj_w, L0_cond_proj_b, L0_cond_norm2_w, L0_cond_film2_w, L0_cond_film2_b, L0_cond_mlp_w1, L0_cond_mlp_b1, L0_cond_mlp_w2, L0_cond_mlp_b2)
    x = _L1_cond_ref(x, cond_1024[:, None, :], L1_cond_W_ada, L1_cond_b_ada, L1_cond_ln1_g, L1_cond_ln1_b, L1_cond_Wqkv, L1_cond_qn_g, L1_cond_qn_b, L1_cond_kn_g, L1_cond_kn_b, L1_cond_Wout, L1_cond_mlp_g, L1_cond_mlp_b, L1_cond_Wgate, L1_cond_fc1s, L1_cond_b1s, L1_cond_fc2s, L1_cond_b2s)
    return x

_drawn_inputs = setup_inputs


def setup_inputs(seed=0):
    import zlib

    import numpy as np

    out = dict(_drawn_inputs(seed))
    spreads = {'L0_cond_norm1_w': (1.0, 0.2),
     'L0_cond_film1_b': (0.0, 0.1),
     'L0_cond_q_b': (0.0, 0.1),
     'L0_cond_k_b': (0.0, 2.0),
     'L0_cond_v_b': (0.0, 0.1),
     'L0_cond_proj_b': (0.0, 0.1),
     'L0_cond_norm2_w': (1.0, 0.2),
     'L0_cond_film2_b': (0.0, 0.1),
     'L0_cond_mlp_b1': (0.0, 0.1),
     'L0_cond_mlp_b2': (0.0, 0.1),
     'L1_cond_b_ada': (0.0, 0.8),
     'L1_cond_ln1_g': (1.0, 0.6),
     'L1_cond_ln1_b': (0.0, 0.8),
     'L1_cond_qn_g': (1.0, 0.6),
     'L1_cond_qn_b': (0.0, 2.0),
     'L1_cond_kn_g': (1.0, 0.6),
     'L1_cond_kn_b': (0.0, 2.0),
     'L1_cond_mlp_g': (1.0, 0.6),
     'L1_cond_mlp_b': (0.0, 0.8),
     'L1_cond_b1s': (0.0, 0.8),
     'L1_cond_b2s': (0.0, 0.745)}
    factors = {'L1_cond_W_ada': 5.771, 'L1_cond_Wgate': 4.696, 'L1_cond_fc1s': 8.0, 'L1_cond_fc2s': 8.0}
    for name, (base, spread) in spreads.items():
        noise = np.random.default_rng([zlib.crc32(name.encode()), seed]).standard_normal(out[name].shape)
        drawn = base * np.exp(spread * noise) if base else spread * noise
        out[name] = jnp.asarray(drawn.astype(out[name].dtype))
    for name, factor in factors.items():
        out[name] = (out[name] * factor).astype(out[name].dtype)
    return out
```

```python
import concourse.bass as bass
from concourse import mybir
from contextlib import ExitStack

B, N, D = 4, 256, 128
TOK = B * N
P = 128
NT = TOK // P
TB = N // P
FF = 4 * D
FC = FF // P
H, HD = 16, 64
NP = H // 2
UP = 2 * B
E, DD = 8, 512
EC = DD // P
CAP = TOK // E
GR = P // E
VD = HD + 1
EPS0, EPS1 = 1e-6, 1e-5
SCALE0 = float(D) ** -0.5

COLS = {}
for _name, _n in (("norm1_w", 1), ("film1_b", 2), ("q_b", 1), ("k_b", 1), ("v_b", 1), ("norm2_w", 1),
                  ("film2_b", 2), ("mlp_b1", FC), ("b_ada", 1), ("ln1_g", 1), ("ln1_b", 1), ("qn_g", 1),
                  ("qn_b", 1), ("kn_g", 1), ("kn_b", 1), ("mlp_g", 1), ("mlp_b", 1), ("b1s", E * EC)):
    COLS[_name] = sum(n for _, n in COLS.values()), _n
NCOL = sum(n for _, n in COLS.values())
SHIFTS = [28] + list(range(24, -1, -4))
NR = len(SHIFTS)
CONST32 = {"ident": (0, P), "iota": (P, P), "step": (2 * P, NR)}
NCONST = 2 * P + NR


def in_range(p, dp):
    return not isinstance(p, int) or 0 <= p + dp < NP


def has_unit(p, s):
    return not isinstance(p, int) or 0 <= UP * p + s < UP * NP


def wait(eng, semaphore, value):
    if not isinstance(value, int) or value > 0:
        eng.wait_ge(semaphore, value)


def run_pairs(eng, slot_):
    for s in range(3, 2 + UP):
        slot_(-1, s)
    with eng.Fori(0, NP - 1) as p:
        for s in range(2, 2 + UP):
            slot_(p, s)
    for s in range(2, 2 + UP):
        slot_(NP - 1, s)


def conditioned_sequence_kernel(nc, x, cols, cond, film1_w, film2_w, wqkvp0, w_ada, mlp_w1, mlp_w2, rows,
                                wqkv, wout, wgate, fc1, fc2, b2s, const32, consti, constm, out):
    f32, bf16, f16, i32 = mybir.dt.float32, mybir.dt.bfloat16, mybir.dt.float16, mybir.dt.int32
    ALU, ACT, AX = mybir.AluOpType, mybir.ActivationFunctionType, mybir.AxisListType
    ds = bass.ds
    ctx = ExitStack()
    with ctx:
        def sb(name, shape, dt=f32):
            return ctx.enter_context(nc.sbuf_tensor(name, shape, dt))

        def sem(name):
            return ctx.enter_context(nc.semaphore(name))

        PS = ctx.enter_context(nc.psum_tensor("banks", [P, 8, 512], f32))

        cols_sb = sb("cols_sb", [P, NCOL])
        cond_sb = sb("cond_sb", [P, B])
        film_w = [sb("film1_sb", [P, 2 * D]), sb("film2_sb", [P, 2 * D])]
        w0 = sb("w0", [P, 4, D])
        wada_sb = sb("wada_sb", [P, D])
        w1_sb = sb("w1_sb", [P, FF])
        w2_sb = sb("w2_sb", [P, FC, D])
        rows_sb = sb("rows_sb", [P, 2, D])
        wqkv_sb = sb("wqkv_sb", [P, NP, 3, P])
        wout_sb = sb("wout_sb", [P, NP, D])
        wgate_sb = sb("wgate_sb", [P, E])
        fc1_sb = sb("fc1_sb", [P, E, DD])
        fc2_sb = sb("fc2_sb", [P, E, EC, D])
        b2_sb = sb("b2_sb", [P, E, D])
        c32 = sb("c32", [P, NCONST])
        ci = sb("ci", [P, NR + 1], i32)
        cm = sb("cm", [P, 3, P])
        identb = sb("identb", [P, P], bf16)
        iotab = sb("iotab", [P, P], bf16)
        blockb = sb("blockb", [P, P], bf16)
        ident = c32[:, 0:P]
        mhalf = sb("mhalf", [P, 2 * 4])

        def col(name, i=0):
            o = COLS[name][0] + i
            return cols_sb[:, o:o + 1]

        x0 = y_out = sb("x0_out", [P, NT, D])
        x2 = sb("x2", [P, NT, D])
        x3 = sb("x3", [P, NT, D])
        xn = [sb(f"xn{i}", [P, NT, D]) for i in range(2)]
        hT0 = sb("hT0", [P, TOK])
        hT = [hT0, hT0, sb("hT2", [P, TOK])]
        sq = sb("sq", [P, 2, D])
        ss = [sb("ss0", [P, NT]), sb("ss1", [P, NT])]
        rs = [sb(f"rs{i}", [P, NT]) for i in range(4)]
        var = [sb(f"var{i}", [P, NT]) for i in range(4)]
        stats = sb("stats", [P, 2, NT, 6])
        mv = sb("mv", [P, 2, NT, 2])
        silu = sb("silu", [P, 4, B])
        film1c = sb("film1c", [P, 2])
        fA = [sb("fA0", [P, B]), sb("fA1", [P, B])]
        fB = [sb(f"fB{i}", [P, B]) for i in range(3)]
        qbs = sb("qbs", [P, 1])
        nm0 = sb("nm0", [P, B, TB])
        reuse_a, reuse_b, reuse_c = sb("reuse_a", [P, NP * TOK]), sb("reuse_b", [P, FC * TOK]), \
            sb("reuse_c", [P, 6 * TOK])
        p0 = reuse_a[:, 0:2 * TOK].rearrange("p (b t m) -> p b t m", b=B, t=TB)
        sum0 = sb("sum0", [P, B, TB])
        rec0 = sb("rec0", [P, B, TB])
        pn0 = reuse_a[:, 2 * TOK:4 * TOK].rearrange("p (b t m) -> p b t m", b=B, t=TB)
        pT0 = reuse_a[:, 4 * TOK:6 * TOK].rearrange("p (b t m) -> p b t m", b=B, t=TB)
        qT0 = reuse_a[:, 6 * TOK:7 * TOK]
        kT0 = reuse_a[:, 7 * TOK:8 * TOK]
        oT = reuse_a[:, :].rearrange("p (a n) -> p a n", a=NP)
        gel = reuse_b[:, :].rearrange("p (c n) -> p c n", c=FC)
        OH = reuse_b[:, :].bitcast(bf16).rearrange("p (t e c) -> p t e c", t=NT, e=E)

        def part(i):
            return reuse_c[:, i * TOK:(i + 1) * TOK]

        def rows_of(ap):
            return ap.rearrange("p (t d) -> p t d", d=D)

        v0, xpb, x1, x1b, oT0 = (rows_of(part(i)) if i < 4 else part(i) for i in range(5))
        V, x3T = part(0), part(1)
        xh = part(2).bitcast(f16).rearrange("p (j t d) -> p j t d", j=2, t=NT)
        gT = part(3).rearrange("p (e c) -> p e c", e=E)
        gx = part(4).rearrange("p (t e j) -> p t e j", t=NT, e=E)
        ohT = part(5).bitcast(bf16).rearrange("p (j n) -> p j n", j=2)

        wsum = sb("wsum", [P, NP, 4])
        wmean = sb("wmean", [P, NP, 4])
        qg8 = sb("qg8", [P, 2])
        qk_raw = sb("qk_raw", [P, NT, 2 * P])
        qk_sq = sb("qk_sq", [P, TB, 2 * P])
        qk_ss = sb("qk_ss", [P, 8])
        qk_var = sb("qk_var", [P, 8])
        qk_rs = sb("qk_rs", [P, 8])
        qT = sb("qT", [P, B, N])
        kT = sb("kT", [P, B, N])
        vv = sb("vv", [P, NT, 2, VD])
        nm = sb("nm", [P, 2, TB])
        pr = sb("pr", [P, 2, TB, N])
        pT = sb("pT", [P, 2, TB, N])
        rec = sb("rec", [P, 2, TB])
        on = xn[1]

        lmax = sb("lmax", [P, NT])
        lsub = sb("lsub", [P, NT, E])
        lexp = sb("lexp", [P, NT, E])
        lsum = sb("lsum", [P, NT])
        lrec = sb("lrec", [P, NT])
        gate = sb("gate", [P, E, NT])
        g3 = sb("g3", [P, E, NT, 3], bf16)
        gr = sb("gr", [P, 2, E, NT])
        gx2 = sb("gx2", [P, E, NT, 2])
        V2 = sb("V2", [P, P])
        ge = sb("ge", [P, TOK], bf16)
        cnt = sb("cnt", [P, 4])
        okb = sb("okb", [P, 1], bf16)
        digit = sb("digit", [P, 1], i32)
        prefix = sb("prefix", [P, 1], i32)
        thr = sb("thr", [P, 1], i32)
        gt, eq, scan1, sel, mask, scan2, slot = (
            pr[:, :, :, :].rearrange("p i t m -> p (i t m)")[:, i * P:(i + 1) * P] for i in range(7))
        zero = sb("zero", [P, P])
        need = sb("need", [P, 1])
        slotT = sb("slotT", [P, E, NT, 2])
        nmr = sb("nmr", [P, NT])
        wsel = sb("wsel", [P, E])
        hid = hT0[:, :].rearrange("p (j c n) -> p j c n", j=2, c=EC)
        ys = sb("ys", [P, 2, D])
        yr = sb("yr", [P, 2, D])
        y3 = sb("y3", [P, 2, 3, D], bf16)

        x_in = [sem(f"x_in{b}") for b in range(B)]
        film_in, l0_in, mlp_in, qkvw_in, out_in, fc_in, const_in = (
            sem(n) for n in ("film_in", "l0_in", "mlp_in", "qkvw_in", "out_in", "fc_in", "const_in"))
        film_mm, silu_exp, silu_rdy, film_rdy = (sem(n) for n in ("film_mm", "silu_exp", "silu_rdy", "film_rdy"))
        ada_mm = sem("ada_mm")
        mhalf_rdy, xpb_rdy, x1b_rdy, ones_rdy, wsum_rdy, wc_rdy = (
            sem(n) for n in ("mhalf_rdy", "xpb_rdy", "x1b_rdy", "ones_rdy", "wsum_rdy", "wc_rdy"))
        ss_rdy, rs_rdy, xn_rdy, t_done, h_rdy = ([sem(f"{n}{i}") for i in range(4)] for n in
                                                 ("ss_rdy", "rs_rdy", "xn_rdy", "t_done", "h_rdy"))
        qkv0_mm, qk0_rdy, v0_rdy, s0_mm, nm0_rdy, exp0_rdy, pn0_rdy, pt0_mm, pt0_rdy, o0_mm, o0_rdy, proj_mm, \
            x1_rdy, up_mm, gel_rdy, down_mm, x2_rdy = (sem(n) for n in (
                "qkv0_mm", "qk0_rdy", "v0_rdy", "s0_mm", "nm0_rdy", "exp0_rdy", "pn0_rdy", "pt0_mm", "pt0_rdy",
                "o0_mm", "o0_rdy", "proj_mm", "x1_rdy", "up_mm", "gel_rdy", "down_mm", "x2_rdy"))
        dve_step, pool_step = sem("dve_step"), sem("pool_step")
        qkv_mm, qkv_copied, sq_rdy, qkss_rdy, var_rdy, rs1_rdy, qkn_rdy, qkt_mm, qk_rdy = (
            sem(n) for n in ("qkv_mm", "qkv_copied", "sq_rdy", "qkss_rdy", "var_rdy", "rs1_rdy", "qkn_rdy",
                             "qkt_mm", "qk_rdy"))
        s_mm, nm_rdy, exp_rdy, pt_mm, pt_rdy, pv_mm, rec_rdy, o_rdy, ot_mm, ot_rdy = (
            sem(n) for n in ("s_mm", "nm_rdy", "exp_rdy", "pt_mm", "pt_rdy", "pv_mm", "rec_rdy", "o_rdy",
                             "ot_mm", "ot_rdy"))
        wo_mm, x3_rdy, x3t_mm, x3t_rdy, lg_mm, lsub_rdy, lexp_rdy, gx_rdy, gt_mm, v_rdy, v2_rdy, g3_rdy = (
            sem(n) for n in ("wo_mm", "x3_rdy", "x3t_mm", "x3t_rdy", "lg_mm", "lsub_rdy", "lexp_rdy", "gx_rdy",
                             "gt_mm", "v_rdy", "v2_rdy", "g3_rdy"))
        thr_rdy, cnt_rdy, ok_rdy, k_mm, dig_rdy = (sem(n) for n in ("thr_rdy", "cnt_rdy", "ok_rdy", "k_mm",
                                                                    "dig_rdy"))
        tie_rdy, tie_mm, off_rdy, off_mm, slot_rdy, slot_mm, slotT_rdy, oh_rdy, xn3_rdy, xh_rdy = (
            sem(n) for n in ("tie_rdy", "tie_mm", "off_rdy", "off_mm", "slot_rdy", "slot_mm", "slotT_rdy",
                             "oh_rdy", "xn3_rdy", "xh_rdy"))
        nmr_rdy, w_mm, w_rdy, gath_mm, g_rdy, fc1_mm, hid_rdy, oht_mm, oht_rdy, fc2_mm, ysum_rdy, y_rdy, sc_mm, \
            out_rdy, out_st, constb_rdy = (sem(n) for n in (
                "nmr_rdy", "w_mm", "w_rdy", "gath_mm", "g_rdy", "fc1_mm", "hid_rdy", "oht_mm", "oht_rdy", "fc2_mm",
                "ysum_rdy", "y_rdy", "sc_mm", "out_rdy", "out_st", "constb_rdy"))

        def tiles(t, b):
            return t[:, b * TB:(b + 1) * TB, :]

        block = ctx.enter_context(nc.Block())

        @block.sync
        def _(sp):
            xv = x.rearrange("(t p) d -> p t d", p=P)
            for b in range(B):
                sp.dma_start(tiles(x0, b), tiles(xv, b)).then_inc(x_in[b], 16)
            sp.dma_start(w0[:, :, :], wqkvp0).then_inc(l0_in, 16)
            sp.dma_start(rows_sb[:, :, :], rows).then_inc(l0_in, 16)
            sp.dma_start(w1_sb[:, :], mlp_w1).then_inc(mlp_in, 16)
            sp.dma_start(w2_sb[:, :, :], mlp_w2).then_inc(mlp_in, 16)
            sp.dma_start(wqkv_sb[:, :, :, :], wqkv).then_inc(qkvw_in, 16)
            sp.dma_start(wout_sb[:, :, :], wout).then_inc(out_in, 16)
            sp.dma_start(wgate_sb[:, :], wgate).then_inc(out_in, 16)
            sp.dma_start(ci[:, :], consti).then_inc(out_in, 16)
            sp.dma_start(cm[:, :, :], constm).then_inc(out_in, 16)
            sp.dma_start(b2_sb[:, :, :], b2s).then_inc(fc_in, 16)
            sp.dma_start(fc1_sb[:, :, :], fc1).then_inc(fc_in, 16)
            sp.dma_start(fc2_sb[:, :, :, :], fc2).then_inc(fc_in, 16)
            ov = out.rearrange("(t p) d -> p t d", p=P)
            for i in range(2):
                sp.wait_ge(out_rdy, i + 1)
                sp.dma_start(ov[:, 4 * i:4 * i + 4, :], y_out[:, 4 * i:4 * i + 4, :]).then_inc(out_st, 16)
            sp.wait_ge(out_st, 32)

        @block.gpsimd
        def _(pool):
            steps = [0]

            def rstd(dst, tmp, src, scale, eps, done):
                n = src.shape[1]
                nc.gpsimd.tensor_scalar(tmp, src, scale, eps, ALU.mult, ALU.add).then_inc(pool_step, 1)
                steps[0] += 1
                pool.wait_ge(pool_step, steps[0])
                nc.gpsimd.tensor_tensor(dst, tmp, mhalf[:, 0:n], ALU.pow).then_inc(done, 1)

            nc.gpsimd.memset(mhalf[:, :], -0.5).then_inc(mhalf_rdy, 1)
            nc.gpsimd.memset(vv[:, :, :, HD:VD], 1.0).then_inc(ones_rdy, 1)
            nc.gpsimd.memset(zero[:, :], 0.0).then_inc(ones_rdy, 1)
            pool.wait_ge(mhalf_rdy, 1)
            for b in range(B):
                pool.wait_ge(ss_rdy[0], b + 1)
                sl = slice(b * TB, (b + 1) * TB)
                rstd(rs[0][:, sl], var[0][:, sl], ss[0][:, sl], 1.0 / D, EPS0, rs_rdy[0])
            pool.wait_ge(l0_in, 32)
            for b in range(B):
                pool.wait_ge(x_in[b], 16)
                nc.gpsimd.tensor_tensor(tiles(xpb, b), tiles(x0, b),
                                        rows_sb[:, 0:1, :].broadcast_to([P, TB, D]), ALU.add).then_inc(xpb_rdy, 1)
            pool.wait_ge(wsum_rdy, 1)
            nc.gpsimd.tensor_tensor(wqkv_sb[:, :, 0:2, :].rearrange("p a g (h c) -> p a (g h) c", c=HD),
                                    wqkv_sb[:, :, 0:2, :].rearrange("p a g (h c) -> p a (g h) c", c=HD),
                                    wmean[:, :, :].unsqueeze(3).broadcast_to([P, NP, 4, HD]),
                                    ALU.add).then_inc(wc_rdy, 1)
            for b in range(B):
                sl = slice(b * TB, (b + 1) * TB)
                pool.wait_ge(ss_rdy[1], b + 1)
                rstd(rs[1][:, sl], var[1][:, sl], ss[1][:, sl], 1.0 / D, EPS0, rs_rdy[1])
                pool.wait_ge(x1_rdy, b + 1)
                nc.gpsimd.tensor_tensor(tiles(x1b, b), tiles(x1, b),
                                        rows_sb[:, 1:2, :].broadcast_to([P, TB, D]), ALU.add).then_inc(x1b_rdy, 1)
            for b in range(B):
                sl = slice(b * TB, (b + 1) * TB)
                pool.wait_ge(ss_rdy[2], b + 1)
                rstd(rs[2][:, sl], var[2][:, sl], mv[:, 0, sl, 1], 1.0, EPS1, rs_rdy[2])

            def slot_(p, s, late=True, early=True):
                for s0, dp, b in ((2, 0, 3), (4, 1, 0), (6, 1, 1), (8, 1, 2)):
                    if s != s0 or not in_range(p, dp):
                        continue
                    g = 4 * p + 4 * dp + b
                    pool.wait_ge(qkv_copied, 2 * g + 2)
                    raw = qk_raw[:, b * TB:(b + 1) * TB, :]
                    nc.gpsimd.tensor_tensor(qk_sq[:, :, :], raw, raw, ALU.mult).then_inc(sq_rdy, 1)
                    pool.wait_ge(var_rdy, g + 1)
                    nc.gpsimd.tensor_tensor(qk_rs[:, :], qk_var[:, :], mhalf[:, :], ALU.pow).then_inc(rs1_rdy, 1)
                    pool.wait_ge(rs1_rdy, g + 1)
                    nc.gpsimd.tensor_tensor(
                        raw.rearrange("p t (h c) -> p (t h) c", c=HD),
                        raw.rearrange("p t (h c) -> p (t h) c", c=HD),
                        qk_rs[:, :].unsqueeze(2).broadcast_to([P, 4 * TB, HD]), ALU.mult).then_inc(qkn_rdy, 1)

            run_pairs(pool, slot_)

            pool.wait_ge(ss_rdy[3], 1)
            rstd(rs[3][:, :], var[3][:, :], mv[:, 1, :, 1], 1.0, EPS1, rs_rdy[3])
            pool.wait_ge(xn3_rdy, 1)
            nc.gpsimd.tensor_copy(xh[:, 0, :, :], xn[1][:, :, :]).then_inc(xh_rdy, 1)
            pool.wait_ge(xh_rdy, 1)
            nc.gpsimd.tensor_tensor(xh[:, 1, :, :], xn[1][:, :, :], xh[:, 0, :, :],
                                    ALU.subtract).then_inc(xh_rdy, 1)

        def experts_pe(pe, mm, tr):
            pe.wait_ge(out_in, 64)
            pe.wait_ge(ot_rdy, 4 * NP)
            for t in range(NT):
                for a in range(NP):
                    last = mm(PS[:, t // 4, (t % 4) * P:(t % 4 + 1) * P], oT[:, a, t * P:(t + 1) * P],
                              wout_sb[:, a, :], start=(a == 0), stop=(a == NP - 1))
                if t % 4 == 3:
                    last.then_inc(wo_mm, 1)
            for i in range(2):
                pe.wait_ge(x3_rdy, i + 1)
                for t in range(4):
                    last = tr(PS[:, 2 + i, t * P:(t + 1) * P], x3[:, 4 * i + t, :], ident)
                last.then_inc(x3t_mm, 1)
            for i in range(2):
                pe.wait_ge(x3t_rdy, i + 1)
                for t in range(4 * i, 4 * i + 4):
                    last = mm(PS[:, 4, t * E:(t + 1) * E], x3T[:, t * P:(t + 1) * P], wgate_sb[:, :],
                              start=True, stop=True)
            last.then_inc(lg_mm, 1)
            pe.wait_ge(gx_rdy, 1)
            for t in range(NT):
                last = tr(PS[:, 5 + t // 4, (t % 4) * P:(t % 4 + 1) * P],
                          gx[:, t, :, :].rearrange("p e j -> p (e j)"), ident)
                if t % 4 == 3:
                    last.then_inc(gt_mm, 1)
            pe.wait_ge(gx_rdy, 2)
            tr(PS[:, 7, 0:P], gx2[:, :, :, :].rearrange("p e t j -> p (e t j)"), ident).then_inc(gt_mm, 1)

            with pe.Fori(0, NR) as r:
                pe.wait_ge(ok_rdy, r + 1)
                mm(PS[:, 4, 0:1], blockb[:, :], okb[:, :], start=True, stop=True).then_inc(k_mm, 1)
            pe.wait_ge(tie_rdy, 1)
            mm(PS[:, 5, 0:1], cm[:, 1, :], cnt[:, 1:2], start=True, stop=False)
            mm(PS[:, 5, 0:1], cm[:, 2, :], cnt[:, 2:3], start=False, stop=True).then_inc(tie_mm, 1)
            pe.wait_ge(off_rdy, 1)
            mm(PS[:, 6, 0:1], cm[:, 2, :], cnt[:, 3:4], start=True, stop=True).then_inc(off_mm, 1)
            pe.wait_ge(slot_rdy, 1)
            tr(PS[:, 7, 0:P], slot[:, :], ident).then_inc(slot_mm, 1)

            pe.wait_ge(xh_rdy, 2)
            pe.wait_ge(oh_rdy, NT)
            for i in range(2):
                for t in range(NT):
                    for j in range(2):
                        last = mm(PS[:, i, :], xh[:, j, t, :], OH[:, t, 4 * i:4 * i + 4, :],
                                  start=(t == 0 and j == 0), stop=(t == NT - 1 and j == 1))
                last.then_inc(gath_mm, 1)
            pe.wait_ge(g3_rdy, 3)
            for e in range(E):
                for t in range(NT):
                    last = mm(PS[:, 4, 3 * e:3 * e + 3], OH[:, t, e, :], g3[:, e, t, :],
                              start=(t == 0), stop=(t == NT - 1))
            last.then_inc(w_mm, 1)
            pe.wait_ge(fc_in, 48)
            for e in range(E + 2):
                if e < E:
                    if e == 0:
                        pe.wait_ge(g_rdy, 2)
                    if e >= 2:
                        pe.wait_ge(hid_rdy, e - 1)
                    for c in range(EC):
                        last = mm(PS[:, e % 2, c * CAP:(c + 1) * CAP], fc1_sb[:, e, c * P:(c + 1) * P],
                                  gT[:, e, :], start=True, stop=True)
                    last.then_inc(fc1_mm, 1)
                    if e >= 2:
                        pe.wait_ge(oht_rdy, e - 1)
                    for t in range(NT):
                        last = tr(PS[:, 2 + e % 2, t * 64:(t + 1) * 64].bitcast(bf16), OH[:, t, e, :],
                                  identb[:, :])
                    last.then_inc(oht_mm, 1)
                if 1 <= e <= E:
                    f = e - 1
                    pe.wait_ge(hid_rdy, f + 1)
                    if f == 0:
                        pe.wait_ge(w_rdy, 1)
                    if f >= 2:
                        pe.wait_ge(ysum_rdy, f - 1)
                    for c in range(EC):
                        last = mm(PS[:, 4 + f % 2, 0:D], hid[:, f % 2, c, :], fc2_sb[:, f, c, :],
                                  start=(c == 0), stop=(c == EC - 1))
                    last.then_inc(fc2_mm, 1)
                if e >= 2:
                    f = e - 2
                    pe.wait_ge(y_rdy, f + 1)
                    pe.wait_ge(oht_rdy, f + 1)
                    for t in range(NT):
                        for j in range(3):
                            last = mm(PS[:, 6 + t // 4, (t % 4) * D:(t % 4 + 1) * D],
                                      ohT[:, f % 2, t * P:(t + 1) * P], y3[:, f % 2, j, :],
                                      start=(f == 0 and t % 4 == 0 and j == 0), stop=(f == E - 1 and j == 2),
                                      skip_group_check=True)
                    last.then_inc(sc_mm, 1)

        @block.tensor
        def _(pe):
            mm, tr = nc.tensor.matmul, nc.tensor.transpose
            pe.wait_ge(film_in, 64)
            for i in range(2):
                for j in range(2):
                    o = 4 * (2 * i + j)
                    last = mm(PS[:, 7, o:o + B], film_w[i][:, j * D:(j + 1) * D], cond_sb[:, :],
                              start=True, stop=True)
            last.then_inc(film_mm, 1)
            pe.wait_ge(const_in, 32)

            def transposes(i, src, bank):
                for b in range(B):
                    pe.wait_ge(xn_rdy[i], b + 1)
                    for t in range(TB):
                        last = tr(PS[:, bank(b), t * P:(t + 1) * P], src[:, b * TB + t, :], ident)
                    last.then_inc(t_done[i], 1)

            transposes(0, xn[0], lambda b: b)
            pe.wait_ge(silu_rdy, 1)
            pe.wait_ge(film_rdy, 1)
            mm(PS[:, 7, 0:B], wada_sb[:, :], silu[:, 3, :], start=True, stop=True).then_inc(ada_mm, 1)
            pe.wait_ge(l0_in, 32)
            for b in range(B):
                pe.wait_ge(h_rdy[0], b + 1)
                if b == B - 1:
                    pe.wait_ge(film_rdy, 2)
                h = hT[0][:, b * N:(b + 1) * N]
                mm(PS[:, 4 + b, 0:N], w0[:, 0, :], h, start=True, stop=True)
                mm(PS[:, 4 + b, N:2 * N], w0[:, 1, :], h, start=True, stop=True)
                for t in range(TB):
                    last = mm(PS[:, b, t * P:(t + 1) * P], h[:, t * P:(t + 1) * P], w0[:, 2, :],
                              start=True, stop=True)
                last.then_inc(qkv0_mm, 1)
            for b in range(B):
                pe.wait_ge(qk0_rdy, b + 1)
                for t in range(TB):
                    last = mm(PS[:, 4 + b, t * N:(t + 1) * N], qT0[:, b * N + t * P:b * N + (t + 1) * P],
                              kT0[:, b * N:(b + 1) * N], start=True, stop=True)
                last.then_inc(s0_mm, 1)
            for b in range(B):
                pe.wait_ge(pn0_rdy, b + 1)
                pe.wait_ge(v0_rdy, b + 1)
                for m in range(TB):
                    for t in range(TB):
                        last = tr(PS[:, b, m * N + t * P:m * N + (t + 1) * P], pn0[:, b, t, m * P:(m + 1) * P],
                                  ident)
                last.then_inc(pt0_mm, 1)
            for b in range(B):
                pe.wait_ge(pt0_rdy, b + 1)
                for m in range(TB):
                    last = mm(PS[:, 4 + b, 0:N], v0[:, b * TB + m, :], pT0[:, b, m, :],
                              start=(m == 0), stop=(m == TB - 1))
                last.then_inc(o0_mm, 1)
            for b in range(B):
                pe.wait_ge(o0_rdy, b + 1)
                for t in range(TB):
                    last = mm(PS[:, b, t * P:(t + 1) * P], oT0[:, b * N + t * P:b * N + (t + 1) * P], w0[:, 3, :],
                              start=True, stop=True)
                last.then_inc(proj_mm, 1)
            transposes(1, xn[1], lambda b: 4 + b)
            pe.wait_ge(mlp_in, 32)
            for b in range(B):
                pe.wait_ge(h_rdy[1], b + 1)
                for c in range(FC):
                    last = mm(PS[:, b + 4 * (c // 2), (c % 2) * N:(c % 2 + 1) * N], w1_sb[:, c * P:(c + 1) * P],
                              hT[1][:, b * N:(b + 1) * N], start=True, stop=True)
                    if c % 2:
                        last.then_inc(up_mm, 1)
            for b in range(B):
                pe.wait_ge(gel_rdy, b + 1)
                for t in range(TB):
                    for c in range(FC):
                        last = mm(PS[:, b, t * P:(t + 1) * P],
                                  gel[:, c, b * N + t * P:b * N + (t + 1) * P], w2_sb[:, c, :],
                                  start=(c == 0), stop=(c == FC - 1))
                last.then_inc(down_mm, 1)
            transposes(2, xn[0], lambda b: 4 + b)

            pe.wait_ge(wc_rdy, 1)
            pe.wait_ge(qkvw_in, 16)
            pe.wait_ge(h_rdy[2], B)

            def scores(p, s, b, hh):
                u = UP * p + s
                pe.wait_ge(qk_rdy, 4 * (p + s // UP) + b + 1)
                wait(pe, exp_rdy, u - 1)
                hs = slice(hh * HD, (hh + 1) * HD)
                for t in range(TB):
                    last = mm(PS[:, s % 2, t * N:(t + 1) * N], qT[hs, b, t * P:(t + 1) * P], kT[hs, b, :],
                              start=True, stop=True)
                last.then_inc(s_mm, 1)

            def make_qkv(p, t):
                g = 8 * p + t
                wait(pe, qkv_copied, g)
                h = hT[2][:, t * P:(t + 1) * P]
                pp = slice(p, p + 1) if isinstance(p, int) else ds(p, 1)
                mm(PS[:, 4, 0:2 * P], h, wqkv_sb[:, pp, 0:2, :], start=True, stop=True)
                mm(PS[:, 4, 2 * P:3 * P], h, wqkv_sb[:, pp, 2, :], start=True, stop=True).then_inc(qkv_mm, 1)

            def turn_probs(p, s):
                u = UP * p + s
                pe.wait_ge(exp_rdy, u + 1)
                wait(pe, pt_rdy, u - 1)
                for m in range(TB):
                    for t in range(TB):
                        last = tr(PS[:, 2 + s % 2, m * N + t * P:m * N + (t + 1) * P],
                                  pr[:, s % 2, t, m * P:(m + 1) * P], ident)
                last.then_inc(pt_mm, 1)

            def turn_qk(p, b):
                g = 4 * p + b
                pe.wait_ge(qkn_rdy, g + 1)
                wait(pe, qk_rdy, g)
                for i in range(2):
                    for t in range(TB):
                        last = tr(PS[:, 5, i * N + t * P:i * N + (t + 1) * P], qk_raw[:, b * TB + t, i * P:(i + 1) * P],
                                  ident)
                last.then_inc(qkt_mm, 1)

            def values(p, s):
                u, b, hh = UP * p + s, (s % UP) // 2, s % 2
                pe.wait_ge(pt_rdy, u + 1)
                wait(pe, o_rdy, u)
                for t in range(TB):
                    for m in range(TB):
                        last = mm(PS[:, 6, t * VD:(t + 1) * VD], pT[:, s % 2, m, t * P:(t + 1) * P],
                                  vv[:, b * TB + m, hh, :], start=(m == 0), stop=(m == TB - 1))
                last.then_inc(pv_mm, 1)

            def turn_out(p, b):
                g = 4 * p + b
                pe.wait_ge(o_rdy, 2 * g + 2)
                if isinstance(p, int):
                    wait(pe, ot_rdy, g)
                for t in range(TB):
                    last = tr(PS[:, 7, t * P:(t + 1) * P], on[:, b * TB + t, :], ident)
                last.then_inc(ot_mm, 1)

            pe.wait_ge(ones_rdy, 2)

            def slot_(p, s):
                if has_unit(p, s + 1):
                    scores(p, s + 1, (s + 1) % UP // 2, (s + 1) % 2)
                if s >= 3 and in_range(p, 1):
                    make_qkv(p + 1, s - 3)
                if s == 2 and in_range(p, 0):
                    make_qkv(p, UP - 1)
                if has_unit(p, s):
                    turn_probs(p, s)
                for s0, dp, b in ((2, 0, 2), (4, 0, 3), (6, 1, 0), (8, 1, 1)):
                    if s == s0 and in_range(p, dp):
                        turn_qk(p + dp, b)
                if has_unit(p, s - 1):
                    values(p, s - 1)
                if s in (3, 5, 7, 9) and in_range(p, 0):
                    turn_out(p, (s - 3) // 2)

            run_pairs(pe, slot_)
            experts_pe(pe, mm, tr)

        @block.scalar
        def _(act):
            av = nc.scalar.activation
            act.dma_start(cols_sb[:, :], cols).then_inc(film_in, 16)
            act.dma_start(cond_sb[:, :], cond).then_inc(film_in, 16)
            act.dma_start(film_w[0][:, :], film1_w).then_inc(film_in, 16)
            act.dma_start(film_w[1][:, :], film2_w).then_inc(film_in, 16)
            act.dma_start(c32[:, :], const32).then_inc(const_in, 16)
            act.dma_start(wada_sb[:, :], w_ada).then_inc(const_in, 16)
            act.wait_ge(film_in, 64)
            av(silu[:, 0, :], cond_sb[:, :], ACT.Exp, scale=-1.0).then_inc(silu_exp, 1)

            def turned(i, bank, scale, bias):
                for b in range(B):
                    act.wait_ge(t_done[i], b + 1)
                    av(hT[i][:, b * N:(b + 1) * N], PS[:, bank(b), 0:N], ACT.Identity, scale=scale(b),
                       bias=bias(b)).then_inc(h_rdy[i], 1)

            act.wait_ge(film_rdy, 1)
            turned(0, lambda b: b, lambda b: fA[0][:, b:b + 1], lambda b: fB[0][:, b:b + 1])
            for b in range(B):
                act.wait_ge(qkv0_mm, b + 1)
                av(qT0[:, b * N:(b + 1) * N], PS[:, 4 + b, 0:N], ACT.Identity, scale=SCALE0, bias=qbs[:, :])
                av(kT0[:, b * N:(b + 1) * N], PS[:, 4 + b, N:2 * N], ACT.Identity,
                   bias=col("k_b")).then_inc(qk0_rdy, 1)
            for b in range(B):
                act.wait_ge(nm0_rdy, b + 1)
                for t in range(TB):
                    last = av(p0[:, b, t, :], PS[:, 4 + b, t * N:(t + 1) * N], ACT.Exp, bias=nm0[:, b, t:t + 1],
                              accum_out=sum0[:, b, t:t + 1])
                last.then_inc(exp0_rdy, 1)
            for b in range(B):
                act.wait_ge(o0_mm, b + 1)
                av(oT0[:, b * N:(b + 1) * N], PS[:, 4 + b, 0:N], ACT.Identity, bias=col("v_b")).then_inc(o0_rdy, 1)
            turned(1, lambda b: 4 + b, lambda b: fA[1][:, b:b + 1], lambda b: fB[1][:, b:b + 1])
            for b in range(B):
                for c in range(FC):
                    if c % 2 == 0:
                        act.wait_ge(up_mm, 2 * b + c // 2 + 1)
                    last = av(gel[:, c, b * N:(b + 1) * N], PS[:, b + 4 * (c // 2), (c % 2) * N:(c % 2 + 1) * N],
                              ACT.Gelu, bias=col("mlp_b1", c))
                last.then_inc(gel_rdy, 1)
            act.wait_ge(film_rdy, 3)
            turned(2, lambda b: 4 + b, lambda b: col("ln1_g"), lambda b: fB[2][:, b:b + 1])

            def copy_qkv(p, t):
                g = 8 * p + t
                act.wait_ge(qkv_mm, g + 1)
                av(qk_raw[:, t, :], PS[:, 4, 0:2 * P], ACT.Copy)
                av(vv[:, t, :, 0:HD], PS[:, 4, 2 * P:3 * P].rearrange("p (h c) -> p h c", c=HD),
                   ACT.Copy).then_inc(qkv_copied, 1)

            def exps(p, s):
                u = UP * p + s
                act.wait_ge(nm_rdy, u + 1)
                wait(act, pt_mm, u - 1)
                for t in range(TB):
                    last = av(pr[:, s % 2, t, :], PS[:, s % 2, t * N:(t + 1) * N], ACT.Exp,
                              bias=nm[:, s % 2, t:t + 1])
                last.then_inc(exp_rdy, 1)

            def norm_qk(p, b):
                g = 4 * p + b
                act.wait_ge(qkt_mm, g + 1)
                av(qT[:, b, :], PS[:, 5, 0:N], ACT.Identity, scale=qg8[:, 0:1], bias=qg8[:, 1:2])
                av(kT[:, b, :], PS[:, 5, N:2 * N], ACT.Identity, scale=col("kn_g"),
                   bias=col("kn_b")).then_inc(qk_rdy, 1)

            def copy_out(p, b):
                g = 4 * p + b
                act.wait_ge(ot_mm, g + 1)
                pp = slice(p, p + 1) if isinstance(p, int) else ds(p, 1)
                av(oT[:, pp, b * N:(b + 1) * N], PS[:, 7, 0:N], ACT.Copy).then_inc(ot_rdy, 1)

            def slot_(p, s):
                if s >= 3 and in_range(p, 1):
                    copy_qkv(p + 1, s - 3)
                if s == 2 and in_range(p, 0):
                    copy_qkv(p, UP - 1)
                if has_unit(p, s + 1):
                    exps(p, s + 1)
                for s0, dp, b in ((2, 0, 2), (4, 0, 3), (6, 1, 0), (8, 1, 1)):
                    if s == s0 and in_range(p, dp):
                        norm_qk(p + dp, b)
                if s in (3, 5, 7, 9) and in_range(p, 0):
                    copy_out(p, (s - 3) // 2)

            act.wait_ge(ones_rdy, 2)
            run_pairs(act, slot_)
            for i in range(2):
                act.wait_ge(x3t_mm, i + 1)
                av(x3T[:, 512 * i:512 * (i + 1)], PS[:, 2 + i, :], ACT.Copy).then_inc(x3t_rdy, 1)
            act.wait_ge(lsub_rdy, 1)
            av(lexp[:, :, :], lsub[:, :, :], ACT.Exp).then_inc(lexp_rdy, 1)
            for i in range(2):
                act.wait_ge(gt_mm, i + 1)
                av(V[:, 512 * i:512 * (i + 1)], PS[:, 5 + i, :], ACT.Copy).then_inc(v_rdy, 1)
            act.wait_ge(nmr_rdy, 1)
            for t in range(NT):
                last = av(xn[1][:, t, :], x3[:, t, :], ACT.Identity, scale=rs[3][:, t:t + 1], bias=nmr[:, t:t + 1])
            last.then_inc(xn3_rdy, 1)
            for i in range(2):
                act.wait_ge(gath_mm, i + 1)
                av(gT[:, 4 * i:4 * i + 4, :], PS[:, i, :].rearrange("p (e c) -> p e c", c=CAP), ACT.Identity,
                   scale=col("mlp_g"), bias=col("mlp_b")).then_inc(g_rdy, 1)
            for e in range(E):
                act.wait_ge(fc1_mm, e + 1)
                if e >= 2:
                    act.wait_ge(fc2_mm, e - 1)
                for c in range(EC):
                    last = av(hid[:, e % 2, c, :], PS[:, e % 2, c * CAP:(c + 1) * CAP], ACT.Gelu_apprx_tanh,
                              bias=col("b1s", e * EC + c))
                last.then_inc(hid_rdy, 1)

        @block.vector
        def _(dve):
            ts, tt, stt = nc.vector.tensor_scalar, nc.vector.tensor_tensor, nc.vector.scalar_tensor_tensor
            red, cp = nc.vector.tensor_reduce, nc.vector.tensor_copy
            steps = [0]

            def link(ins):
                ins.then_inc(dve_step, 1)
                steps[0] += 1
                dve.wait_ge(dve_step, steps[0])

            def squares(i, src, b):
                for t in range(TB):
                    n = b * TB + t
                    if n >= 2 or i:
                        dve.wait_ge(dve_step, steps[0])
                    last = nc.vector.tensor_tensor_reduce(out=sq[:, t, :], in0=src[:, n, :], in1=src[:, n, :],
                                                          scale=1.0, scalar=0.0, op0=ALU.mult, op1=ALU.add,
                                                          accum_out=ss[i][:, n:n + 1])
                last.then_inc(ss_rdy[i], 1)

            def scaled(i, src, dst, b):
                dve.wait_ge(rs_rdy[i], b + 1)
                for t in range(TB):
                    n = b * TB + t
                    last = ts(dst[:, n, :], src[:, n, :], rs[i][:, n:n + 1], None, ALU.mult)
                last.then_inc(xn_rdy[i], 1)

            for b in range(B):
                dve.wait_ge(x_in[b], 16)
                if b:
                    dve.wait_ge(ss_rdy[0], b)
                squares(0, x0, b)
            dve.wait_ge(silu_exp, 1)
            link(ts(silu[:, 1, :], silu[:, 0, :], 1.0, None, ALU.add))
            link(nc.vector.reciprocal(silu[:, 2, :], silu[:, 1, :]))
            tt(silu[:, 3, :], cond_sb[:, :], silu[:, 2, :], ALU.mult).then_inc(silu_rdy, 1)
            ts(film1c[:, 0:1], col("film1_b", 0), 1.0, None, ALU.add)
            ts(film1c[:, 1:2], col("film2_b", 0), 1.0, None, ALU.add)
            link(ts(qbs[:, :], col("q_b"), SCALE0, None, ALU.mult))
            dve.wait_ge(film_mm, 1)
            for i in range(2):
                ts(fA[i][:, :], PS[:, 7, 8 * i:8 * i + B], film1c[:, i:i + 1], col(f"norm{i + 1}_w"), ALU.add,
                   ALU.mult)
                last = ts(fB[i][:, :], PS[:, 7, 8 * i + 4:8 * i + 4 + B], col(f"film{i + 1}_b", 1), None, ALU.add)
            last.then_inc(film_rdy, 1)
            for b in range(B):
                scaled(0, x0, xn[0], b)
            dve.wait_ge(ada_mm, 1)
            ts(fB[2][:, :], PS[:, 7, 0:B], col("b_ada"), col("ln1_b"), ALU.add, ALU.add).then_inc(film_rdy, 1)
            for b in range(B):
                dve.wait_ge(qkv0_mm, b + 1)
                cp(tiles(v0, b), PS[:, b, 0:N].rearrange("p (t d) -> p t d", d=D)).then_inc(v0_rdy, 1)
            for b in range(B):
                dve.wait_ge(s0_mm, b + 1)
                red(nm0[:, b, :], PS[:, 4 + b, :].rearrange("p (t m) -> p t m", m=N), AX.X, ALU.max,
                    negate=True).then_inc(nm0_rdy, 1)
            for b in range(B):
                dve.wait_ge(exp0_rdy, b + 1)
                link(nc.vector.reciprocal(rec0[:, b, :], sum0[:, b, :]))
                for t in range(TB):
                    last = ts(pn0[:, b, t, :], p0[:, b, t, :], rec0[:, b, t:t + 1], None, ALU.mult)
                last.then_inc(pn0_rdy, 1)
            for b in range(B):
                dve.wait_ge(pt0_mm, b + 1)
                cp(pT0[:, b, :, :], PS[:, b, :].rearrange("p (t m) -> p t m", m=N)).then_inc(pt0_rdy, 1)
            dve.wait_ge(qkvw_in, 16)
            link(red(wsum[:, :, :], wqkv_sb[:, :, 0:2, :].rearrange("p a g (h c) -> p a (g h) c", c=HD), AX.X,
                     ALU.add))
            ts(wmean[:, :, :], wsum[:, :, :], -1.0 / HD, None, ALU.mult).then_inc(wsum_rdy, 1)
            for b in range(B):
                dve.wait_ge(proj_mm, b + 1)
                dve.wait_ge(xpb_rdy, b + 1)
                tt(tiles(x1, b), PS[:, b, 0:N].rearrange("p (t d) -> p t d", d=D), tiles(xpb, b),
                   ALU.add).then_inc(x1_rdy, 1)
                dve.wait_ge(x1_rdy, b + 1)
                if b:
                    dve.wait_ge(ss_rdy[1], b)
                else:
                    dve.wait_ge(ss_rdy[0], B)
                squares(1, x1, b)
            for b in range(B):
                scaled(1, x1, xn[1], b)
            ts(qg8[:, 0:1], col("qn_g"), HD ** -0.5, None, ALU.mult)
            ts(qg8[:, 1:2], col("qn_b"), HD ** -0.5, None, ALU.mult).then_inc(film_rdy, 1)

            def row_stats(i, src, n):
                link(nc.vector.bn_stats(stats[:, i, n, :], src[:, n, :]))
                return nc.vector.bn_aggr(mv[:, i, n, :], stats[:, i, n, :])

            for b in range(B):
                dve.wait_ge(down_mm, b + 1)
                dve.wait_ge(x1b_rdy, b + 1)
                tt(tiles(x2, b), PS[:, b, 0:N].rearrange("p (t d) -> p t d", d=D), tiles(x1b, b),
                   ALU.add).then_inc(x2_rdy, 1)
                dve.wait_ge(x2_rdy, b + 1)
                for t in range(TB):
                    last = row_stats(0, x2, b * TB + t)
                last.then_inc(ss_rdy[2], 1)
            for b in range(B):
                dve.wait_ge(rs_rdy[2], b + 1)
                dve.wait_ge(t_done[0], b + 1)
                for t in range(TB):
                    n = b * TB + t
                    last = ts(xn[0][:, n, :], x2[:, n, :], mv[:, 0, n, 0:1], rs[2][:, n:n + 1], ALU.subtract,
                              ALU.mult)
                last.then_inc(xn_rdy[2], 1)

            def row_max(p, s):
                u = UP * p + s
                dve.wait_ge(s_mm, u + 1)
                wait(dve, exp_rdy, u - 1)
                red(nm[:, s % 2, :], PS[:, s % 2, :].rearrange("p (t m) -> p t m", m=N), AX.X, ALU.max,
                    negate=True).then_inc(nm_rdy, 1)

            def copy_probs(p, s):
                u = UP * p + s
                dve.wait_ge(pt_mm, u + 1)
                wait(dve, pv_mm, u - 1)
                cp(pT[:, s % 2, :, :], PS[:, 2 + s % 2, :].rearrange("p (m n) -> p m n", n=N)).then_inc(pt_rdy, 1)

            def sum_squares(p, b):
                g = 4 * p + b
                dve.wait_ge(sq_rdy, g + 1)
                red(qk_ss[:, :], qk_sq[:, :, :].rearrange("p t (h c) -> p (t h) c", c=HD), AX.X,
                    ALU.add).then_inc(qkss_rdy, 1)
                dve.wait_ge(qkss_rdy, g + 1)
                wait(dve, rs1_rdy, g)
                ts(qk_var[:, :], qk_ss[:, :], 1.0 / HD, EPS1, ALU.mult, ALU.add).then_inc(var_rdy, 1)

            def normalize(p, s):
                u, b, hh = UP * p + s, (s % UP) // 2, s % 2
                dve.wait_ge(pv_mm, u + 1)
                o = PS[:, 6, 0:TB * VD].rearrange("p (t c) -> p t c", c=VD)
                nc.vector.reciprocal(rec[:, s % 2, :], o[:, :, HD]).then_inc(rec_rdy, 1)
                dve.wait_ge(rec_rdy, u + 1)
                tt(on[:, b * TB:(b + 1) * TB, hh * HD:(hh + 1) * HD], o[:, :, 0:HD],
                   rec[:, s % 2, :].unsqueeze(2).broadcast_to([P, TB, HD]), ALU.mult).then_inc(o_rdy, 1)

            def slot_(p, s):
                if has_unit(p, s + 1):
                    row_max(p, s + 1)
                for s0, dp, b in ((3, 0, 3), (5, 1, 0), (7, 1, 1), (9, 1, 2)):
                    if s == s0 and in_range(p, dp):
                        sum_squares(p + dp, b)
                if has_unit(p, s):
                    copy_probs(p, s)
                if has_unit(p, s - 1):
                    normalize(p, s - 1)

            run_pairs(dve, slot_)

            for i in range(2):
                dve.wait_ge(wo_mm, i + 1)
                tt(x3[:, 4 * i:4 * i + 4, :], PS[:, i, :].rearrange("p (t d) -> p t d", d=D),
                   x2[:, 4 * i:4 * i + 4, :], ALU.add).then_inc(x3_rdy, 1)
                dve.wait_ge(x3_rdy, i + 1)
                for t in range(4):
                    last = row_stats(1, x3, 4 * i + t)
            last.then_inc(ss_rdy[3], 1)
            dve.wait_ge(lg_mm, 1)
            lg = PS[:, 4, 0:NT * E].rearrange("p (t e) -> p t e", e=E)
            link(red(lmax[:, :], lg, AX.X, ALU.max))
            tt(lsub[:, :, :], lg, lmax[:, :].unsqueeze(2).broadcast_to([P, NT, E]), ALU.subtract).then_inc(lsub_rdy, 1)
            dve.wait_ge(lexp_rdy, 1)
            link(red(lsum[:, :], lexp[:, :, :], AX.X, ALU.add))
            link(nc.vector.reciprocal(lrec[:, :], lsum[:, :]))
            link(tt(gate[:, :, :].rearrange("p e t -> p t e"), lexp[:, :, :],
                    lrec[:, :].unsqueeze(2).broadcast_to([P, NT, E]), ALU.mult))
            cp(gx[:, :, :, :], gate[:, :, :].rearrange("p e t -> p t e").unsqueeze(3).broadcast_to([P, NT, E, GR]))\
                .then_inc(gx_rdy, 1)
            cp(gx2[:, :, :, :], gate[:, :, :].unsqueeze(3).broadcast_to([P, E, NT, 2])).then_inc(gx_rdy, 1)
            cp(g3[:, :, :, 0], gate[:, :, :]).then_inc(g3_rdy, 1)
            dve.wait_ge(g3_rdy, 1)
            link(tt(gr[:, 0, :, :], gate[:, :, :], g3[:, :, :, 0], ALU.subtract))
            cp(g3[:, :, :, 1], gr[:, 0, :, :]).then_inc(g3_rdy, 1)
            dve.wait_ge(g3_rdy, 2)
            link(tt(gr[:, 1, :, :], gr[:, 0, :, :], g3[:, :, :, 1], ALU.subtract))
            cp(g3[:, :, :, 2], gr[:, 1, :, :]).then_inc(g3_rdy, 1)
            cp(iotab[:, :], c32[:, P:2 * P]).then_inc(constb_rdy, 1)
            cp(identb[:, :], ident).then_inc(constb_rdy, 1)
            dve.wait_ge(out_in, 64)
            link(cp(blockb[:, :], cm[:, 0, :]))
            dve.wait_ge(rs_rdy[3], 1)
            stt(nmr[:, :], mv[:, 1, :, 0], -1.0, rs[3][:, :], ALU.mult, ALU.mult).then_inc(nmr_rdy, 1)

            dve.wait_ge(gt_mm, 3)
            link(cp(V2[:, :], PS[:, 7, 0:P]))
            link(nc.vector.memset(prefix[:, :], 0))
            cp(thr[:, :], ci[:, 0:1]).then_inc(thr_rdy, 1)
            dve.wait_ge(v_rdy, 2)
            with dve.Fori(0, NR) as r:
                dve.wait_ge(thr_rdy, r + 1)
                ts(ge[:, :], V[:, :], thr[:, :].bitcast(f32), None, ALU.is_ge, ALU.add,
                   accum_out=cnt[:, 0:1]).then_inc(cnt_rdy, 1)
                dve.wait_ge(cnt_rdy, r + 1)
                ts(okb[:, :], cnt[:, 0:1], float(CAP), None, ALU.is_ge).then_inc(ok_rdy, 1)
                dve.wait_ge(k_mm, r + 1)
                ts(digit[:, :], PS[:, 4, 0:1], -1.0, c32[:, ds(r + 2 * P, 1)], ALU.add, ALU.mult)\
                    .then_inc(dig_rdy, 1)
                dve.wait_ge(dig_rdy, 2 * r + 1)
                tt(prefix[:, :], prefix[:, :], digit[:, :], ALU.bitwise_or).then_inc(dig_rdy, 1)
                dve.wait_ge(dig_rdy, 2 * r + 2)
                tt(thr[:, :], prefix[:, :], ci[:, ds(r + 1, 1)], ALU.bitwise_or).then_inc(thr_rdy, 1)
            dve.wait_ge(thr_rdy, NR + 1)

            kth = thr[:, :].bitcast(f32)
            link(ts(gt[:, :], V2[:, :], kth, None, ALU.is_gt, ALU.add, accum_out=cnt[:, 1:2]))
            ts(eq[:, :], V2[:, :], kth, None, ALU.is_equal, ALU.add, accum_out=cnt[:, 2:3]).then_inc(tie_rdy, 1)
            dve.wait_ge(tie_rdy, 1)
            nc.vector.tensor_tensor_scan(scan1[:, :], eq[:, :], zero[:, :], 0.0, ALU.add, ALU.add)
            dve.wait_ge(tie_mm, 1)
            link(ts(need[:, :], PS[:, 5, 0:1], -1.0, float(CAP), ALU.mult, ALU.add))
            link(stt(sel[:, :], scan1[:, :], need[:, :], eq[:, :], ALU.is_le, ALU.mult))
            stt(mask[:, :], gt[:, :], 0.0, sel[:, :], ALU.add, ALU.add, accum_out=cnt[:, 3:4]).then_inc(off_rdy, 1)
            dve.wait_ge(off_rdy, 1)
            link(nc.vector.tensor_tensor_scan(scan2[:, :], mask[:, :], zero[:, :], 0.0, ALU.add, ALU.add))
            dve.wait_ge(off_mm, 1)
            stt(slot[:, :], scan2[:, :], PS[:, 6, 0:1], mask[:, :], ALU.add, ALU.mult).then_inc(slot_rdy, 1)
            dve.wait_ge(slot_mm, 1)
            link(cp(slotT[:, :, :, :], PS[:, 7, 0:P].rearrange("p (e t j) -> p e t j", t=NT, j=2)))
            dve.wait_ge(constb_rdy, 2)
            for t in range(NT):
                for e in range(E):
                    last = ts(OH[:, t, e, :], iotab[:, :], slotT[:, e, t, 0:1], None, ALU.is_equal)
                last.then_inc(oh_rdy, 1)
            dve.wait_ge(w_mm, 1)
            red(wsel[:, :], PS[:, 4, 0:3 * E].rearrange("p (e j) -> p e j", j=3), AX.X, ALU.add).then_inc(w_rdy, 1)
            dve.wait_ge(w_rdy, 1)
            dve.wait_ge(fc_in, 48)
            for e in range(E + 1):
                if e < E:
                    dve.wait_ge(oht_mm, e + 1)
                    if e >= 2:
                        dve.wait_ge(sc_mm, e - 1)
                    cp(ohT[:, e % 2, :], PS[:, 2 + e % 2, :].bitcast(bf16)).then_inc(oht_rdy, 1)
                if e >= 1:
                    f = e - 1
                    y, z, parts = ys[:, f % 2, :], yr[:, f % 2, :], y3[:, f % 2, :, :]
                    dve.wait_ge(fc2_mm, f + 1)
                    if f >= 1:
                        dve.wait_ge(y_rdy, f)
                    if f >= 2:
                        dve.wait_ge(sc_mm, f - 1)
                    tt(y, PS[:, 4 + f % 2, 0:D], b2_sb[:, f, :], ALU.add).then_inc(ysum_rdy, 1)
                    dve.wait_ge(ysum_rdy, f + 1)
                    link(ts(z, y, wsel[:, f:f + 1], None, ALU.mult))
                    link(cp(parts[:, 0, :], z))
                    link(tt(y, z, parts[:, 0, :], ALU.subtract))
                    link(cp(parts[:, 1, :], y))
                    link(tt(z, y, parts[:, 1, :], ALU.subtract))
                    cp(parts[:, 2, :], z).then_inc(y_rdy, 1)
            dve.wait_ge(sc_mm, E)
            for i in range(2):
                tt(y_out[:, 4 * i:4 * i + 4, :], PS[:, 6 + i, :].rearrange("p (t d) -> p t d", d=D),
                   x3[:, 4 * i:4 * i + 4, :], ALU.add).then_inc(out_rdy, 1)


def kernel(**inputs):
    import numpy as np
    import concourse.bacc as bacc
    from concourse.bass_utils import run_bass_kernel_spmd as run

    a = {k: np.asarray(v) for k, v in inputs.items()}
    g0 = lambda n: a["L0_cond_" + n]
    g1 = lambda n: a["L1_cond_" + n]
    columns = {n: g0(n) for n in ("norm1_w", "film1_b", "q_b", "k_b", "v_b", "norm2_w", "film2_b", "mlp_b1")}
    columns.update({n: g1(n) for n in ("b_ada", "ln1_g", "ln1_b", "mlp_g", "mlp_b", "b1s")})
    for n in ("qn_g", "qn_b", "kn_g", "kn_b"):
        columns[n] = np.tile(g1(n), 2)
    cols = np.concatenate([columns[n].reshape(-1, P).T for n in COLS], axis=1)
    part = np.arange(P)
    const32 = np.concatenate([np.eye(P), np.broadcast_to(part + 1, (P, P)),
                              np.broadcast_to(2.0 ** np.array(SHIFTS), (P, NR))], axis=1).astype(np.float32)
    digits = [np.minimum(part % GR, 4) << 28] + [(part % GR) << s for s in SHIFTS[1:]] + [part * 0]
    consti = np.stack(digits, axis=1).astype(np.int32)
    same = (part[:, None] // GR == part[None, :] // GR)
    tile_of, first = part % GR // 2, (part % 2 == 0)[:, None]
    constm = np.stack([same, same & first, same & first & (tile_of[:, None] < tile_of[None, :])],
                      axis=1).astype(np.float32)
    arrays = {
        "x": a["x"].reshape(TOK, D), "cols": cols, "cond": a["cond_1024"].T, "film1_w": g0("film1_w"),
        "film2_w": g0("film2_w"),
        "wqkvp0": np.stack([g0(n) for n in ("q_w", "k_w", "v_w", "proj_w")], axis=1),
        "w_ada": g1("W_ada").T, "mlp_w1": g0("mlp_w1"), "mlp_w2": g0("mlp_w2").reshape(FC, P, D).transpose(1, 0, 2),
        "rows": np.broadcast_to(np.stack([g0("proj_b"), g0("mlp_b2")]), (P, 2, D)),
        "wqkv": g1("Wqkv").reshape(3, NP, P, D).transpose(3, 1, 0, 2),
        "wout": g1("Wout").reshape(D, NP, P).transpose(2, 1, 0), "wgate": g1("Wgate").T,
        "fc1": g1("fc1s").transpose(2, 0, 1), "fc2": g1("fc2s").reshape(E, D, EC, P).transpose(3, 0, 2, 1),
        "b2s": np.broadcast_to(g1("b2s"), (P, E, D)), "const32": const32, "consti": consti, "constm": constm,
    }
    nc = bacc.Bacc("TRN2", target_bir_lowering=False, num_devices=1)
    arrays = {f"in_{k}": np.ascontiguousarray(v) for k, v in arrays.items()}
    args = [nc.dram_tensor(k, v.shape, mybir.dt.from_np(v.dtype), kind="ExternalInput").ap()
            for k, v in arrays.items()]
    args.append(nc.dram_tensor("out_0", (TOK, D), mybir.dt.float32, kind="ExternalOutput").ap())
    conditioned_sequence_kernel(nc, *args)
    r = run(nc, [arrays], core_ids=[0])
    return r.results[0]["out_0"].reshape(B, N, D)
```

```python
import concourse.bass as bass
from concourse import mybir
from contextlib import ExitStack

B, N, D = 4, 256, 128
TOK = B * N
P = 128
NT = TOK // P
TB = N // P
FF = 4 * D
FC = FF // P
H, HD = 16, 64
NP = H // 2
UP = 2 * B
E, DD = 8, 512
EC = DD // P
CAP = TOK // E
GR = P // E
VD = HD + 1
EPS0, EPS1 = 1e-6, 1e-5
SCALE0 = float(D) ** -0.5

COLS = {}
for _name, _n in (("norm1_w", 1), ("film1_b", 2), ("q_b", 1), ("k_b", 1), ("v_b", 1), ("norm2_w", 1),
                  ("film2_b", 2), ("mlp_b1", FC), ("b_ada", 1), ("ln1_g", 1), ("ln1_b", 1), ("qn_g", 1),
                  ("qn_b", 1), ("kn_g", 1), ("kn_b", 1), ("mlp_g", 1), ("mlp_b", 1), ("b1s", E * EC)):
    COLS[_name] = sum(n for _, n in COLS.values()), _n
NCOL = sum(n for _, n in COLS.values())
SHIFTS = [28] + list(range(24, -1, -4))
NR = len(SHIFTS)
CONST32 = {"ident": (0, P), "iota": (P, P), "step": (2 * P, NR)}
NCONST = 2 * P + NR


NORM_SLOTS = [(2 * b + 2, 1, b) for b in range(B)]
SUM_SLOTS = [(2 * b + 3, 1, b) for b in range(B)]
TURN_SLOTS = [(2 * b + 5, 1, b) for b in range(B - 1)] + [(3, 0, B - 1)]


WOUT_PARTS = {3: [(0, 0), (0, 1)], 9: [(1, 5), (1, 6)], **{s: [(1, s - 4), (0, s - 2)] for s in range(4, 9)}}


HALVES = ((0, 0), (0, 1), (1, 0))


def in_range(p, dp):
    return not isinstance(p, int) or 0 <= p + dp < NP


def has_unit(p, s):
    return not isinstance(p, int) or 0 <= UP * p + s < UP * NP


def wait(eng, semaphore, value):
    if not isinstance(value, int) or value > 0:
        eng.wait_ge(semaphore, value)


def run_pairs(eng, slot_):
    for s in range(2, 2 + UP):
        slot_(-1, s)
    with eng.Fori(0, NP - 2) as p:
        for s in range(2, 2 + UP):
            slot_(p, s)
    for p in range(NP - 2, NP):
        for s in range(2, 2 + UP):
            slot_(p, s)


def conditioned_sequence_kernel(nc, x, cols, cond, film1_w, film2_w, wqkvp0, w_ada, mlp_w1, mlp_w2, rows,
                                wqkv, wout, wgate, fc1, fc2, b2s, const32, consti, constm, out):
    f32, bf16, f16, i32 = mybir.dt.float32, mybir.dt.bfloat16, mybir.dt.float16, mybir.dt.int32
    ALU, ACT, AX = mybir.AluOpType, mybir.ActivationFunctionType, mybir.AxisListType
    ds = bass.ds
    ctx = ExitStack()
    with ctx:
        def sb(name, shape, dt=f32):
            return ctx.enter_context(nc.sbuf_tensor(name, shape, dt))

        def sem(name):
            return ctx.enter_context(nc.semaphore(name))

        PS = ctx.enter_context(nc.psum_tensor("banks", [P, 8, 512], f32))

        cols_sb = sb("cols_sb", [P, NCOL])
        cond_sb = sb("cond_sb", [P, B])
        film_w = [sb("film1_sb", [P, 2 * D]), sb("film2_sb", [P, 2 * D])]
        w0 = sb("w0", [P, 4, D])
        wada_sb = sb("wada_sb", [P, D])
        w1_sb = sb("w1_sb", [P, FF])
        w2_sb = sb("w2_sb", [P, FC, D])
        rows_sb = sb("rows_sb", [P, 2, D])
        wout_sb = sb("wout_sb", [P, NP, D])
        wgate_sb = sb("wgate_sb", [P, E])
        fc1_sb = sb("fc1_sb", [P, E, DD])
        wqkv_sb = fc1_sb[:, :, :].rearrange("p e c -> p (e c)")[:, 0:NP * 3 * P].rearrange(
            "p (a g c) -> p a g c", a=NP, g=3)
        wqkv16 = sb("wqkv16", [P, 2, NP, 3 * P], f16)
        fc2_sb = sb("fc2_sb", [P, E, EC, D])
        b2_sb = sb("b2_sb", [P, E, D])
        c32 = sb("c32", [P, NCONST])
        ci = sb("ci", [P, NR + 1], i32)
        cm = sb("cm", [P, 3, P])
        identb = sb("identb", [P, P], bf16)
        iotab = sb("iotab", [P, P], bf16)
        blockb = sb("blockb", [P, P], bf16)
        ident = c32[:, 0:P]
        mhalf = sb("mhalf", [P, 2 * 4])

        def col(name, i=0):
            o = COLS[name][0] + i
            return cols_sb[:, o:o + 1]

        x0 = y_out = sb("x0_out", [P, NT, D])
        x2 = sb("x2", [P, NT, D])
        x3 = sb("x3", [P, NT, D])
        xn = [sb(f"xn{i}", [P, NT, D]) for i in range(2)]
        hT0 = sb("hT0", [P, TOK])
        hT = [hT0, hT0, hT0]
        h16 = sb("h16", [P, 2, TOK], f16)
        sq = sb("sq", [P, 2, D])
        ss = [sb("ss0", [P, NT]), sb("ss1", [P, NT])]
        rs = [sb(f"rs{i}", [P, NT]) for i in range(4)]
        var = [sb(f"var{i}", [P, NT]) for i in range(4)]
        stats = sb("stats", [P, 2, NT, 6])
        mv = sb("mv", [P, 2, NT, 2])
        silu = sb("silu", [P, 4, B])
        film1c = sb("film1c", [P, 2])
        fA = [sb("fA0", [P, B]), sb("fA1", [P, B])]
        fB = [sb(f"fB{i}", [P, B]) for i in range(3)]
        qbs = sb("qbs", [P, 1])
        nm0 = sb("nm0", [P, B, TB])
        reuse_a, reuse_b, reuse_c = sb("reuse_a", [P, NP * TOK]), sb("reuse_b", [P, FC * TOK]), \
            sb("reuse_c", [P, 5 * TOK])
        p0 = reuse_a[:, 0:2 * TOK].rearrange("p (b t m) -> p b t m", b=B, t=TB)
        sum0 = sb("sum0", [P, B, TB])
        rec0 = sb("rec0", [P, B, TB])
        pn0 = reuse_a[:, 2 * TOK:4 * TOK].rearrange("p (b t m) -> p b t m", b=B, t=TB)
        pT0 = reuse_a[:, 4 * TOK:6 * TOK].rearrange("p (b t m) -> p b t m", b=B, t=TB)
        qT0 = reuse_a[:, 6 * TOK:7 * TOK]
        kT0 = reuse_a[:, 7 * TOK:8 * TOK]
        oT = reuse_a[:, :].rearrange("p (a n) -> p a n", a=NP)
        gel = reuse_b[:, :].rearrange("p (c n) -> p c n", c=FC)
        OH = reuse_b[:, :].bitcast(bf16).rearrange("p (t e c) -> p t e c", t=NT, e=E)

        def part(i):
            return reuse_c[:, i * TOK:(i + 1) * TOK]

        def rows_of(ap):
            return ap.rearrange("p (t d) -> p t d", d=D)

        v0, xpb, x1, x1b, oT0 = (rows_of(part(i)) if i < 4 else part(i) for i in range(5))
        V, x3T = part(0), part(1)
        xh = part(2).bitcast(f16).rearrange("p (j t d) -> p j t d", j=2, t=NT)
        gT = part(3).rearrange("p (e c) -> p e c", e=E)
        gx = part(4).rearrange("p (t e j) -> p t e j", t=NT, e=E)
        ohT = reuse_a[:, 0:4 * TOK].bitcast(bf16).rearrange("p (e n) -> p e n", e=E)

        wsum = sb("wsum", [P, NP, 4])
        wmean = sb("wmean", [P, NP, 4])
        qg8 = sb("qg8", [P, 2])
        qk_raw = sb("qk_raw", [P, NT, 2 * P])
        qk_sq = sb("qk_sq", [P, TB, 2 * P])
        qk_ss = sb("qk_ss", [P, 8])
        qk_var = sb("qk_var", [P, 8])
        qk_rs = sb("qk_rs", [P, 8])
        qT = sb("qT", [P, B, N])
        kT = sb("kT", [P, B, N])
        vv = sb("vv", [P, 2, NT, 2, VD], f16)
        nm = sb("nm", [P, 2, TB])
        pr = sb("pr", [P, 2, TB, N])
        pT = sb("pT", [P, 2, 2, TB, N], f16)
        rec = sb("rec", [P, 2, TB])
        on = xn[1]

        lmax = sb("lmax", [P, NT])
        lsub = sb("lsub", [P, NT, E])
        lexp = sb("lexp", [P, NT, E])
        lsum = sb("lsum", [P, NT])
        lrec = sb("lrec", [P, NT])
        gate = sb("gate", [P, E, NT])
        g3 = sb("g3", [P, E, NT, 3], bf16)
        gr = sb("gr", [P, 2, E, NT])
        gx2 = sb("gx2", [P, E, NT, 2])
        V2 = sb("V2", [P, P])
        ge = sb("ge", [P, TOK], bf16)
        cnt = sb("cnt", [P, 4])
        okb = sb("okb", [P, 1], bf16)
        digit = sb("digit", [P, 1], i32)
        prefix = sb("prefix", [P, 1], i32)
        trial = sb("trial", [P, 1], i32)
        thr = sb("thr", [P, 1], i32)
        gt, eq, scan1, sel, mask, scan2, slot = (
            pr[:, :, :, :].rearrange("p i t m -> p (i t m)")[:, i * P:(i + 1) * P] for i in range(7))
        zero = sb("zero", [P, P])
        need = sb("need", [P, 1])
        slotT = sb("slotT", [P, E, NT, 2])
        nmr = sb("nmr", [P, NT])
        wsel = sb("wsel", [P, E])
        hid = hT0[:, :].rearrange("p (j c n) -> p j c n", j=2, c=EC)
        ys = sb("ys", [P, 2, D])
        y2 = sb("y2", [P, 2, 2, D], f16)

        x_in = [sem(f"x_in{b}") for b in range(B)]
        film_in, l0_in, mlp_in, qkvw_in, out_in, fc_in, const_in = (
            sem(n) for n in ("film_in", "l0_in", "mlp_in", "qkvw_in", "out_in", "fc_in", "const_in"))
        film_mm, silu_exp, silu_rdy, film_rdy = (sem(n) for n in ("film_mm", "silu_exp", "silu_rdy", "film_rdy"))
        ada_mm = sem("ada_mm")
        mhalf_rdy, xpb_rdy, x1b_rdy, ones_rdy, wsum_rdy, wc_rdy, w16_rdy, h16_rdy = (
            sem(n) for n in ("mhalf_rdy", "xpb_rdy", "x1b_rdy", "ones_rdy", "wsum_rdy", "wc_rdy", "w16_rdy",
                             "h16_rdy"))
        ph_rdy, v_copied = sem("ph_rdy"), sem("v_copied")
        ss_rdy, rs_rdy, xn_rdy, t_done, h_rdy = ([sem(f"{n}{i}") for i in range(4)] for n in
                                                 ("ss_rdy", "rs_rdy", "xn_rdy", "t_done", "h_rdy"))
        qkv0_mm, qk0_rdy, v0_rdy, s0_mm, nm0_rdy, exp0_rdy, pn0_rdy, pt0_mm, pt0_rdy, o0_mm, o0_rdy, proj_mm, \
            x1_rdy, up_mm, gel_rdy, down_mm, x2_rdy = (sem(n) for n in (
                "qkv0_mm", "qk0_rdy", "v0_rdy", "s0_mm", "nm0_rdy", "exp0_rdy", "pn0_rdy", "pt0_mm", "pt0_rdy",
                "o0_mm", "o0_rdy", "proj_mm", "x1_rdy", "up_mm", "gel_rdy", "down_mm", "x2_rdy"))
        dve_step, pool_step = sem("dve_step"), sem("pool_step")
        qkv_mm, qkv_copied, sq_rdy, qkss_rdy, var_rdy, rs1_rdy, qkn_rdy, qkt_mm, qk_rdy = (
            sem(n) for n in ("qkv_mm", "qkv_copied", "sq_rdy", "qkss_rdy", "var_rdy", "rs1_rdy", "qkn_rdy",
                             "qkt_mm", "qk_rdy"))
        s_mm, nm_rdy, exp_rdy, pt_mm, pt_rdy, pv_mm, rec_rdy, o_rdy, ot_mm, ot_rdy = (
            sem(n) for n in ("s_mm", "nm_rdy", "exp_rdy", "pt_mm", "pt_rdy", "pv_mm", "rec_rdy", "o_rdy",
                             "ot_mm", "ot_rdy"))
        wo_mm, x3_rdy, x3t_mm, x3t_rdy, lg_mm, lsub_rdy, lexp_rdy, gx_rdy, gt_mm, v_rdy, v2_rdy, g3_rdy = (
            sem(n) for n in ("wo_mm", "x3_rdy", "x3t_mm", "x3t_rdy", "lg_mm", "lsub_rdy", "lexp_rdy", "gx_rdy",
                             "gt_mm", "v_rdy", "v2_rdy", "g3_rdy"))
        thr_rdy, cnt_rdy, ok_rdy, k_mm, dig_rdy, prefix_rdy, trial_rdy = (
            sem(n) for n in ("thr_rdy", "cnt_rdy", "ok_rdy", "k_mm", "dig_rdy", "prefix_rdy", "trial_rdy"))
        tie_rdy, tie_mm, off_rdy, off_mm, slot_rdy, slot_mm, slotT_rdy, oh_rdy, xn3_rdy, xh_rdy = (
            sem(n) for n in ("tie_rdy", "tie_mm", "off_rdy", "off_mm", "slot_rdy", "slot_mm", "slotT_rdy",
                             "oh_rdy", "xn3_rdy", "xh_rdy"))
        nmr_rdy, w_mm, b2w_rdy, gath_mm, g_rdy, fc1_mm, hid_rdy, oht_mm, oht_rdy, fc2_mm, sum_mm, y_rdy, sc_mm, \
            out_rdy, out_st, constb_rdy = (sem(n) for n in (
                "nmr_rdy", "w_mm", "b2w_rdy", "gath_mm", "g_rdy", "fc1_mm", "hid_rdy", "oht_mm", "oht_rdy", "fc2_mm",
                "sum_mm", "y_rdy", "sc_mm", "out_rdy", "out_st", "constb_rdy"))

        def tiles(t, b):
            return t[:, b * TB:(b + 1) * TB, :]

        w_all = wqkv_sb.rearrange("p a g c -> p (a g c)")
        w_half = [wqkv16[:, i, :, :].rearrange("p a c -> p (a c)") for i in range(2)]

        block = ctx.enter_context(nc.Block())

        @block.sync
        def _(sp):
            xv = x.rearrange("(t p) d -> p t d", p=P)
            for b in range(B):
                sp.dma_start(tiles(x0, b), tiles(xv, b)).then_inc(x_in[b], 16)
            sp.dma_start(w0[:, :, :], wqkvp0).then_inc(l0_in, 16)
            sp.dma_start(rows_sb[:, :, :], rows).then_inc(l0_in, 16)
            sp.dma_start(w1_sb[:, :], mlp_w1).then_inc(mlp_in, 16)
            sp.dma_start(w2_sb[:, :, :], mlp_w2).then_inc(mlp_in, 16)
            sp.dma_start(wqkv_sb[:, :, :, :], wqkv).then_inc(qkvw_in, 16)
            sp.dma_start(wout_sb[:, :, :], wout).then_inc(out_in, 16)
            sp.dma_start(wgate_sb[:, :], wgate).then_inc(out_in, 16)
            sp.dma_start(ci[:, :], consti).then_inc(out_in, 16)
            sp.dma_start(cm[:, :, :], constm).then_inc(out_in, 16)
            sp.dma_start(b2_sb[:, :, :], b2s).then_inc(fc_in, 16)
            sp.dma_start(fc2_sb[:, :, :, :], fc2).then_inc(fc_in, 16)
            sp.wait_ge(w16_rdy, 2)
            sp.dma_start(fc1_sb[:, :, :], fc1).then_inc(fc_in, 16)
            ov = out.rearrange("(t p) d -> p t d", p=P)
            for i in range(2):
                sp.wait_ge(out_rdy, i + 1)
                sp.dma_start(ov[:, 4 * i:4 * i + 4, :], y_out[:, 4 * i:4 * i + 4, :]).then_inc(out_st, 16)
            sp.wait_ge(out_st, 32)

        @block.gpsimd
        def _(pool):
            steps = [0]

            def rstd(dst, tmp, src, scale, eps, done):
                n = src.shape[1]
                nc.gpsimd.tensor_scalar(tmp, src, scale, eps, ALU.mult, ALU.add).then_inc(pool_step, 1)
                steps[0] += 1
                pool.wait_ge(pool_step, steps[0])
                nc.gpsimd.tensor_tensor(dst, tmp, mhalf[:, 0:n], ALU.pow).then_inc(done, 1)

            nc.gpsimd.memset(mhalf[:, :], -0.5).then_inc(mhalf_rdy, 1)
            nc.gpsimd.memset(vv[:, 0, :, :, HD:VD], 1.0).then_inc(ones_rdy, 1)
            nc.gpsimd.memset(vv[:, 1, :, :, HD:VD], 0.0).then_inc(ones_rdy, 1)
            nc.gpsimd.memset(zero[:, :], 0.0).then_inc(ones_rdy, 1)
            pool.wait_ge(mhalf_rdy, 1)
            for b in range(B):
                pool.wait_ge(ss_rdy[0], b + 1)
                sl = slice(b * TB, (b + 1) * TB)
                rstd(rs[0][:, sl], var[0][:, sl], ss[0][:, sl], 1.0 / D, EPS0, rs_rdy[0])
            pool.wait_ge(l0_in, 32)
            for b in range(B):
                pool.wait_ge(x_in[b], 16)
                nc.gpsimd.tensor_tensor(tiles(xpb, b), tiles(x0, b),
                                        rows_sb[:, 0:1, :].broadcast_to([P, TB, D]), ALU.add).then_inc(xpb_rdy, 1)
            pool.wait_ge(wsum_rdy, 1)
            nc.gpsimd.tensor_tensor(wqkv_sb[:, :, 0:2, :].rearrange("p a g (h c) -> p a (g h) c", c=HD),
                                    wqkv_sb[:, :, 0:2, :].rearrange("p a g (h c) -> p a (g h) c", c=HD),
                                    wmean[:, :, :].unsqueeze(3).broadcast_to([P, NP, 4, HD]),
                                    ALU.add).then_inc(wc_rdy, 1)
            for b in range(B):
                sl = slice(b * TB, (b + 1) * TB)
                pool.wait_ge(ss_rdy[1], b + 1)
                rstd(rs[1][:, sl], var[1][:, sl], ss[1][:, sl], 1.0 / D, EPS0, rs_rdy[1])
                pool.wait_ge(x1_rdy, b + 1)
                nc.gpsimd.tensor_tensor(tiles(x1b, b), tiles(x1, b),
                                        rows_sb[:, 1:2, :].broadcast_to([P, TB, D]), ALU.add).then_inc(x1b_rdy, 1)
            for b in range(B):
                sl = slice(b * TB, (b + 1) * TB)
                pool.wait_ge(ss_rdy[2], b + 1)
                rstd(rs[2][:, sl], var[2][:, sl], mv[:, 0, sl, 1], 1.0, EPS1, rs_rdy[2])

            def slot_(p, s, late=True, early=True):
                for s0, dp, b in NORM_SLOTS:
                    if s != s0 or not in_range(p, dp):
                        continue
                    g = 4 * p + 4 * dp + b
                    pool.wait_ge(qkv_copied, 2 * g + 2)
                    raw = qk_raw[:, b * TB:(b + 1) * TB, :]
                    nc.gpsimd.tensor_tensor(qk_sq[:, :, :], raw, raw, ALU.mult).then_inc(sq_rdy, 1)
                    pool.wait_ge(var_rdy, g + 1)
                    nc.gpsimd.tensor_tensor(qk_rs[:, :], qk_var[:, :], mhalf[:, :], ALU.pow).then_inc(rs1_rdy, 1)
                    pool.wait_ge(rs1_rdy, g + 1)
                    nc.gpsimd.tensor_tensor(
                        raw.rearrange("p t (h c) -> p (t h) c", c=HD),
                        raw.rearrange("p t (h c) -> p (t h) c", c=HD),
                        qk_rs[:, :].unsqueeze(2).broadcast_to([P, 4 * TB, HD]), ALU.mult).then_inc(qkn_rdy, 1)

            run_pairs(pool, slot_)

            pool.wait_ge(ss_rdy[3], 1)
            rstd(rs[3][:, :], var[3][:, :], mv[:, 1, :, 1], 1.0, EPS1, rs_rdy[3])
            pool.wait_ge(xn3_rdy, 1)
            nc.gpsimd.tensor_copy(xh[:, 0, :, :], xn[1][:, :, :]).then_inc(xh_rdy, 1)
            pool.wait_ge(xh_rdy, 1)
            nc.gpsimd.tensor_tensor(xh[:, 1, :, :], xn[1][:, :, :], xh[:, 0, :, :],
                                    ALU.subtract).then_inc(xh_rdy, 1)

        def wout_product(pe, mm, i, a):
            for t in range(4 * i, 4 * i + 4):
                pe.wait_ge(ot_rdy, 4 * a + t // TB + 1)
                last = mm(PS[:, 4 + i, (t % 4) * P:(t % 4 + 1) * P], oT[:, a, t * P:(t + 1) * P],
                          wout_sb[:, a, :], start=(a == 0 and t % 4 == 0), stop=(a == NP - 1),
                          skip_group_check=True)
            return last

        def experts_pe(pe, mm, tr):
            for i in range(2):
                wout_product(pe, mm, i, NP - 1).then_inc(wo_mm, 1)
            for i in range(2):
                pe.wait_ge(x3_rdy, i + 1)
                for t in range(4):
                    last = tr(PS[:, 2 + i, t * P:(t + 1) * P], x3[:, 4 * i + t, :], ident)
                last.then_inc(x3t_mm, 1)
            for i in range(2):
                pe.wait_ge(x3t_rdy, i + 1)
                for t in range(4 * i, 4 * i + 4):
                    last = mm(PS[:, 0, t * E:(t + 1) * E], x3T[:, t * P:(t + 1) * P], wgate_sb[:, :],
                              start=True, stop=True)
            last.then_inc(lg_mm, 1)
            pe.wait_ge(gx_rdy, 1)
            for t in range(NT):
                last = tr(PS[:, 5 + t // 4, (t % 4) * P:(t % 4 + 1) * P],
                          gx[:, t, :, :].rearrange("p e j -> p (e j)"), ident)
                if t % 4 == 3:
                    last.then_inc(gt_mm, 1)
            pe.wait_ge(gx_rdy, 2)
            tr(PS[:, 7, 0:P], gx2[:, :, :, :].rearrange("p e t j -> p (e t j)"), ident).then_inc(gt_mm, 1)

            with pe.Fori(0, NR) as r:
                pe.wait_ge(ok_rdy, r + 1)
                mm(PS[:, 4, 0:1], blockb[:, :], okb[:, :], start=True, stop=True).then_inc(k_mm, 1)
            pe.wait_ge(tie_rdy, 1)
            mm(PS[:, 5, 0:1], cm[:, 1, :], cnt[:, 1:2], start=True, stop=False)
            mm(PS[:, 5, 0:1], cm[:, 2, :], cnt[:, 2:3], start=False, stop=True).then_inc(tie_mm, 1)
            pe.wait_ge(off_rdy, 1)
            mm(PS[:, 6, 0:1], cm[:, 2, :], cnt[:, 3:4], start=True, stop=True).then_inc(off_mm, 1)
            pe.wait_ge(slot_rdy, 1)
            tr(PS[:, 7, 0:P], slot[:, :], ident).then_inc(slot_mm, 1)

            pe.wait_ge(xh_rdy, 2)
            for t in range(NT):
                pe.wait_ge(oh_rdy, t + 1)
                for i in range(2):
                    for j in range(2):
                        last = mm(PS[:, i, :], xh[:, j, t, :], OH[:, t, 4 * i:4 * i + 4, :],
                                  start=(t == 0 and j == 0), stop=(t == NT - 1 and j == 1))
                    if t == NT - 1:
                        last.then_inc(gath_mm, 1)
                if t >= 4:
                    pe.wait_ge(oht_rdy, t - 3)
                for e in range(E):
                    last = tr(PS[:, 2 + t % 4, e * 64:(e + 1) * 64].bitcast(bf16), OH[:, t, e, :], identb[:, :])
                last.then_inc(oht_mm, 1)
            pe.wait_ge(g3_rdy, 3)
            for e in range(E):
                for t in range(NT):
                    last = mm(PS[:, 7, 3 * e:3 * e + 3], OH[:, t, e, :], g3[:, e, t, :],
                              start=(t == 0), stop=(t == NT - 1))
            last.then_inc(w_mm, 1)
            pe.wait_ge(fc_in, 48)
            pe.wait_ge(g_rdy, 2)
            for e in range(E + 2):
                if e < E:
                    if e >= 2:
                        pe.wait_ge(hid_rdy, e - 1)
                    for c in range(EC):
                        last = mm(PS[:, e % 2, c * CAP:(c + 1) * CAP], fc1_sb[:, e, c * P:(c + 1) * P],
                                  gT[:, e, :], start=True, stop=True)
                    last.then_inc(fc1_mm, 1)
                if 1 <= e <= E:
                    f = e - 1
                    pe.wait_ge(hid_rdy, f + 1)
                    if f == 0:
                        pe.wait_ge(oht_rdy, NT)
                    if f >= 2:
                        pe.wait_ge(y_rdy, f - 1)
                    for c in range(EC):
                        last = mm(PS[:, 4 + f % 2, 0:D], hid[:, f % 2, c, :], fc2_sb[:, f, c, :],
                                  start=(c == 0), stop=(c == EC - 1))
                    last.then_inc(fc2_mm, 1)
                if e >= 2:
                    f = e - 2
                    pe.wait_ge(y_rdy, f + 1)
                    for t in range(NT):
                        for j in range(2):
                            last = mm(PS[:, 6 + t // 4, (t % 4) * D:(t % 4 + 1) * D],
                                      ohT[:, f, t * P:(t + 1) * P], y2[:, f % 2, j, :],
                                      start=(f == 0 and t % 4 == 0 and j == 0), stop=(f == E - 1 and j == 1),
                                      skip_group_check=True)
                        if f == E - 1 and t % 4 == 3:
                            last.then_inc(sum_mm, 1)
                        elif t == NT - 1:
                            last.then_inc(sc_mm, 1)

        @block.tensor
        def _(pe):
            mm, tr = nc.tensor.matmul, nc.tensor.transpose
            pe.wait_ge(film_in, 64)
            for i in range(2):
                for j in range(2):
                    o = 4 * (2 * i + j)
                    last = mm(PS[:, 7, o:o + B], film_w[i][:, j * D:(j + 1) * D], cond_sb[:, :],
                              start=True, stop=True)
            last.then_inc(film_mm, 1)
            pe.wait_ge(const_in, 32)

            def transposes(i, src, bank):
                for b in range(B):
                    pe.wait_ge(xn_rdy[i], b + 1)
                    for t in range(TB):
                        last = tr(PS[:, bank(b), t * P:(t + 1) * P], src[:, b * TB + t, :], ident)
                    last.then_inc(t_done[i], 1)

            transposes(0, xn[0], lambda b: b)
            pe.wait_ge(silu_rdy, 1)
            pe.wait_ge(film_rdy, 1)
            mm(PS[:, 7, 0:B], wada_sb[:, :], silu[:, 3, :], start=True, stop=True).then_inc(ada_mm, 1)
            pe.wait_ge(l0_in, 32)
            for b in range(B):
                pe.wait_ge(h_rdy[0], b + 1)
                if b == B - 1:
                    pe.wait_ge(film_rdy, 2)
                h = hT[0][:, b * N:(b + 1) * N]
                mm(PS[:, 4 + b, 0:N], w0[:, 0, :], h, start=True, stop=True)
                mm(PS[:, 4 + b, N:2 * N], w0[:, 1, :], h, start=True, stop=True)
                for t in range(TB):
                    last = mm(PS[:, b, t * P:(t + 1) * P], h[:, t * P:(t + 1) * P], w0[:, 2, :],
                              start=True, stop=True)
                last.then_inc(qkv0_mm, 1)
            for b in range(B):
                pe.wait_ge(qk0_rdy, b + 1)
                for t in range(TB):
                    last = mm(PS[:, 4 + b, t * N:(t + 1) * N], qT0[:, b * N + t * P:b * N + (t + 1) * P],
                              kT0[:, b * N:(b + 1) * N], start=True, stop=True)
                last.then_inc(s0_mm, 1)
            for b in range(B):
                pe.wait_ge(pn0_rdy, b + 1)
                pe.wait_ge(v0_rdy, b + 1)
                for m in range(TB):
                    for t in range(TB):
                        last = tr(PS[:, b, m * N + t * P:m * N + (t + 1) * P], pn0[:, b, t, m * P:(m + 1) * P],
                                  ident)
                last.then_inc(pt0_mm, 1)
            for b in range(B):
                pe.wait_ge(pt0_rdy, b + 1)
                for m in range(TB):
                    last = mm(PS[:, 4 + b, 0:N], v0[:, b * TB + m, :], pT0[:, b, m, :],
                              start=(m == 0), stop=(m == TB - 1))
                last.then_inc(o0_mm, 1)
            for b in range(B):
                pe.wait_ge(o0_rdy, b + 1)
                for t in range(TB):
                    last = mm(PS[:, b, t * P:(t + 1) * P], oT0[:, b * N + t * P:b * N + (t + 1) * P], w0[:, 3, :],
                              start=True, stop=True)
                last.then_inc(proj_mm, 1)
            transposes(1, xn[1], lambda b: 4 + b)
            pe.wait_ge(mlp_in, 32)
            for b in range(B):
                pe.wait_ge(h_rdy[1], b + 1)
                for c in range(FC):
                    last = mm(PS[:, b + 4 * (c // 2), (c % 2) * N:(c % 2 + 1) * N], w1_sb[:, c * P:(c + 1) * P],
                              hT[1][:, b * N:(b + 1) * N], start=True, stop=True)
                    if c % 2:
                        last.then_inc(up_mm, 1)
            for b in range(B):
                pe.wait_ge(gel_rdy, b + 1)
                for t in range(TB):
                    for c in range(FC):
                        last = mm(PS[:, b, t * P:(t + 1) * P],
                                  gel[:, c, b * N + t * P:b * N + (t + 1) * P], w2_sb[:, c, :],
                                  start=(c == 0), stop=(c == FC - 1))
                last.then_inc(down_mm, 1)
            transposes(2, xn[0], lambda b: 4 + b)

            pe.wait_ge(w16_rdy, 2)
            pe.wait_ge(h16_rdy, 2 * B)

            def scores(p, s, b, hh):
                u = UP * p + s
                pe.wait_ge(qk_rdy, 4 * (p + s // UP) + b + 1)
                wait(pe, exp_rdy, u - 1)
                hs = slice(hh * HD, (hh + 1) * HD)
                for t in range(TB):
                    last = mm(PS[:, s % 2, t * N:(t + 1) * N], qT[hs, b, t * P:(t + 1) * P], kT[hs, b, :],
                              start=True, stop=True)
                last.then_inc(s_mm, 1)

            def one(p):
                return slice(p, p + 1) if isinstance(p, int) else ds(p, 1)

            def make_qkv(p, t):
                g = NT * p + t
                wait(pe, v_copied, g)
                if isinstance(p, int) and g == 0:
                    pe.wait_ge(qkv_copied, 1)
                nt, np_ = (t + 1) % NT, p + (t + 1) // NT
                if in_range(np_, 0):
                    for n, (i, j) in enumerate(HALVES):
                        last = mm(PS[:, 4, 0:2 * P], h16[:, i, nt * P:(nt + 1) * P],
                                  wqkv16[:, j, one(np_), 0:2 * P], start=(n == 0), stop=(n == 2))
                if in_range(p, 0):
                    for n, (i, j) in enumerate(HALVES):
                        last = mm(PS[:, 4, 2 * P:3 * P], h16[:, i, t * P:(t + 1) * P],
                                  wqkv16[:, j, one(p), 2 * P:3 * P], start=(n == 0), stop=(n == 2))
                last.then_inc(qkv_mm, 1)

            def turn_probs(p, s):
                u = UP * p + s
                pe.wait_ge(exp_rdy, u + 1)
                wait(pe, pt_rdy, u - 1)
                for m in range(TB):
                    for t in range(TB):
                        last = tr(PS[:, 2 + s % 2, m * N + t * P:m * N + (t + 1) * P],
                                  pr[:, s % 2, t, m * P:(m + 1) * P], ident)
                last.then_inc(pt_mm, 1)

            def turn_qk(p, b):
                g = 4 * p + b
                pe.wait_ge(qkn_rdy, g + 1)
                wait(pe, qk_rdy, g)
                for i in range(2):
                    for t in range(TB):
                        last = tr(PS[:, 5, i * N + t * P:i * N + (t + 1) * P], qk_raw[:, b * TB + t, i * P:(i + 1) * P],
                                  ident)
                last.then_inc(qkt_mm, 1)

            def values(p, s):
                u, b, hh = UP * p + s, (s % UP) // 2, s % 2
                pe.wait_ge(pt_rdy, u + 1)
                wait(pe, o_rdy, u)
                for t in range(TB):
                    for m in range(TB):
                        for n, (i, j) in enumerate(HALVES):
                            last = mm(PS[:, 6, t * VD:(t + 1) * VD], pT[:, s % 2, i, m, t * P:(t + 1) * P],
                                      vv[:, j, b * TB + m, hh, :], start=(m == 0 and n == 0),
                                      stop=(m == TB - 1 and n == 2))
                last.then_inc(pv_mm, 1)

            def turn_out(p, b):
                g = 4 * p + b
                pe.wait_ge(o_rdy, 2 * g + 2)
                if isinstance(p, int):
                    wait(pe, ot_rdy, g)
                for t in range(TB):
                    last = tr(PS[:, 7, t * P:(t + 1) * P], on[:, b * TB + t, :], ident)
                last.then_inc(ot_mm, 1)

            pe.wait_ge(ones_rdy, 3)
            make_qkv(-1, NT - 1)

            def slot_(p, s):
                if has_unit(p, s + 1):
                    scores(p, s + 1, (s + 1) % UP // 2, (s + 1) % 2)
                if has_unit(p, s):
                    turn_probs(p, s)
                for s0, dp, b in TURN_SLOTS:
                    if s == s0 and in_range(p, dp):
                        turn_qk(p + dp, b)
                if s in (3, 5, 7, 9) and in_range(p, 0):
                    turn_out(p, (s - 3) // 2)
                if has_unit(p, s - 1):
                    values(p, s - 1)
                if in_range(p, 1):
                    make_qkv(p + 1, s - 2)
                elif s > 2:
                    pe.wait_ge(out_in, 64)
                    pe.wait_ge(v_copied, NT * NP)
                    if s > 3:
                        pe.wait_ge(qk_rdy, 4 * NP)
                    for i, a in WOUT_PARTS[s]:
                        wout_product(pe, mm, i, a)

            run_pairs(pe, slot_)
            experts_pe(pe, mm, tr)

        @block.scalar
        def _(act):
            av = nc.scalar.activation
            act.dma_start(cols_sb[:, :], cols).then_inc(film_in, 16)
            act.dma_start(cond_sb[:, :], cond).then_inc(film_in, 16)
            act.dma_start(film_w[0][:, :], film1_w).then_inc(film_in, 16)
            act.dma_start(film_w[1][:, :], film2_w).then_inc(film_in, 16)
            act.dma_start(c32[:, :], const32).then_inc(const_in, 16)
            act.dma_start(wada_sb[:, :], w_ada).then_inc(const_in, 16)
            act.wait_ge(film_in, 64)
            av(silu[:, 0, :], cond_sb[:, :], ACT.Exp, scale=-1.0).then_inc(silu_exp, 1)

            def turned(i, bank, scale, bias):
                for b in range(B):
                    act.wait_ge(t_done[i], b + 1)
                    av(hT[i][:, b * N:(b + 1) * N], PS[:, bank(b), 0:N], ACT.Identity, scale=scale(b),
                       bias=bias(b)).then_inc(h_rdy[i], 1)

            act.wait_ge(film_rdy, 1)
            turned(0, lambda b: b, lambda b: fA[0][:, b:b + 1], lambda b: fB[0][:, b:b + 1])
            for b in range(B):
                act.wait_ge(qkv0_mm, b + 1)
                av(qT0[:, b * N:(b + 1) * N], PS[:, 4 + b, 0:N], ACT.Identity, scale=SCALE0, bias=qbs[:, :])
                av(kT0[:, b * N:(b + 1) * N], PS[:, 4 + b, N:2 * N], ACT.Identity,
                   bias=col("k_b")).then_inc(qk0_rdy, 1)
            for b in range(B):
                act.wait_ge(nm0_rdy, b + 1)
                for t in range(TB):
                    last = av(p0[:, b, t, :], PS[:, 4 + b, t * N:(t + 1) * N], ACT.Exp, bias=nm0[:, b, t:t + 1],
                              accum_out=sum0[:, b, t:t + 1])
                last.then_inc(exp0_rdy, 1)
            for b in range(B):
                act.wait_ge(o0_mm, b + 1)
                av(oT0[:, b * N:(b + 1) * N], PS[:, 4 + b, 0:N], ACT.Identity, bias=col("v_b")).then_inc(o0_rdy, 1)
            act.wait_ge(wc_rdy, 1)
            av(w_half[0], w_all, ACT.Copy).then_inc(w16_rdy, 1)
            turned(1, lambda b: 4 + b, lambda b: fA[1][:, b:b + 1], lambda b: fB[1][:, b:b + 1])
            for b in range(B):
                for c in range(FC):
                    if c % 2 == 0:
                        act.wait_ge(up_mm, 2 * b + c // 2 + 1)
                    last = av(gel[:, c, b * N:(b + 1) * N], PS[:, b + 4 * (c // 2), (c % 2) * N:(c % 2 + 1) * N],
                              ACT.Gelu, bias=col("mlp_b1", c))
                last.then_inc(gel_rdy, 1)
            act.wait_ge(film_rdy, 3)
            turned(2, lambda b: 4 + b, lambda b: col("ln1_g"), lambda b: fB[2][:, b:b + 1])

            def copy_qkv(p, t):
                g = NT * p + t
                act.wait_ge(qkv_mm, g + 2)
                nt, np_ = (t + 1) % NT, p + (t + 1) // NT
                if in_range(np_, 0):
                    last = av(qk_raw[:, nt, :], PS[:, 4, 0:2 * P], ACT.Copy)
                if not in_range(p, 0):
                    last.then_inc(qkv_copied, 1)
                    return
                av(vv[:, 0, t, :, 0:HD], PS[:, 4, 2 * P:3 * P].rearrange("p (h c) -> p h c", c=HD),
                   ACT.Copy).then_inc(qkv_copied, 1)

            def exps(p, s):
                u = UP * p + s
                act.wait_ge(nm_rdy, u + 1)
                wait(act, pt_mm, u - 1)
                for t in range(TB):
                    last = av(pr[:, s % 2, t, :], PS[:, s % 2, t * N:(t + 1) * N], ACT.Exp,
                              bias=nm[:, s % 2, t:t + 1])
                last.then_inc(exp_rdy, 1)

            def norm_qk(p, b):
                g = 4 * p + b
                act.wait_ge(qkt_mm, g + 1)
                av(qT[:, b, :], PS[:, 5, 0:N], ACT.Identity, scale=qg8[:, 0:1], bias=qg8[:, 1:2])
                av(kT[:, b, :], PS[:, 5, N:2 * N], ACT.Identity, scale=col("kn_g"),
                   bias=col("kn_b")).then_inc(qk_rdy, 1)

            def copy_out(p, b):
                g = 4 * p + b
                act.wait_ge(ot_mm, g + 1)
                pp = slice(p, p + 1) if isinstance(p, int) else ds(p, 1)
                av(oT[:, pp, b * N:(b + 1) * N], PS[:, 7, 0:N], ACT.Copy).then_inc(ot_rdy, 1)

            def copy_high(p, s):
                u = UP * p + s
                act.wait_ge(pt_mm, u + 1)
                wait(act, pv_mm, u - 1)
                av(pT[:, s % 2, 0, :, :], PS[:, 2 + s % 2, :].rearrange("p (m n) -> p m n", n=N),
                   ACT.Copy).then_inc(ph_rdy, 1)

            def slot_(p, s):
                if has_unit(p, s):
                    copy_high(p, s)
                if has_unit(p, s + 1):
                    exps(p, s + 1)
                if in_range(p, 1):
                    copy_qkv(p + 1, s - 2)
                for s0, dp, b in TURN_SLOTS:
                    if s == s0 and in_range(p, dp):
                        norm_qk(p + dp, b)
                if s in (3, 5, 7, 9) and in_range(p, 0):
                    copy_out(p, (s - 3) // 2)

            act.wait_ge(ones_rdy, 3)
            copy_qkv(-1, NT - 1)
            run_pairs(act, slot_)
            for i in range(2):
                act.wait_ge(x3t_mm, i + 1)
                av(x3T[:, 512 * i:512 * (i + 1)], PS[:, 2 + i, :], ACT.Copy).then_inc(x3t_rdy, 1)
            act.wait_ge(lsub_rdy, 1)
            av(lexp[:, :, :], lsub[:, :, :], ACT.Exp).then_inc(lexp_rdy, 1)
            for i in range(2):
                act.wait_ge(gt_mm, i + 1)
                av(V[:, 512 * i:512 * (i + 1)], PS[:, 5 + i, :], ACT.Copy).then_inc(v_rdy, 1)
            act.wait_ge(nmr_rdy, 1)
            for t in range(NT):
                last = av(xn[1][:, t, :], x3[:, t, :], ACT.Identity, scale=rs[3][:, t:t + 1], bias=nmr[:, t:t + 1])
            last.then_inc(xn3_rdy, 1)
            def copy_slots(t):
                act.wait_ge(oht_mm, t + 1)
                av(ohT[:, :, t * P:(t + 1) * P], PS[:, 2 + t % 4, :].bitcast(bf16).rearrange(
                    "p (e n) -> p e n", e=E), ACT.Copy).then_inc(oht_rdy, 1)

            for t in range(NT - 1):
                copy_slots(t)
            for i in range(2):
                act.wait_ge(gath_mm, i + 1)
                av(gT[:, 4 * i:4 * i + 4, :], PS[:, i, :].rearrange("p (e c) -> p e c", c=CAP), ACT.Identity,
                   scale=col("mlp_g"), bias=col("mlp_b")).then_inc(g_rdy, 1)
            copy_slots(NT - 1)
            for e in range(E):
                act.wait_ge(fc1_mm, e + 1)
                if e >= 2:
                    act.wait_ge(fc2_mm, e - 1)
                for c in range(EC):
                    last = av(hid[:, e % 2, c, :], PS[:, e % 2, c * CAP:(c + 1) * CAP], ACT.Gelu_apprx_tanh,
                              bias=col("b1s", e * EC + c))
                last.then_inc(hid_rdy, 1)

        @block.vector
        def _(dve):
            ts, tt, stt = nc.vector.tensor_scalar, nc.vector.tensor_tensor, nc.vector.scalar_tensor_tensor
            red, cp = nc.vector.tensor_reduce, nc.vector.tensor_copy
            steps = [0]

            def link(ins):
                ins.then_inc(dve_step, 1)
                steps[0] += 1
                dve.wait_ge(dve_step, steps[0])

            def squares(i, src, b):
                for t in range(TB):
                    n = b * TB + t
                    if n >= 2 or i:
                        dve.wait_ge(dve_step, steps[0])
                    last = nc.vector.tensor_tensor_reduce(out=sq[:, t, :], in0=src[:, n, :], in1=src[:, n, :],
                                                          scale=1.0, scalar=0.0, op0=ALU.mult, op1=ALU.add,
                                                          accum_out=ss[i][:, n:n + 1])
                last.then_inc(ss_rdy[i], 1)

            def scaled(i, src, dst, b):
                dve.wait_ge(rs_rdy[i], b + 1)
                for t in range(TB):
                    n = b * TB + t
                    last = ts(dst[:, n, :], src[:, n, :], rs[i][:, n:n + 1], None, ALU.mult)
                last.then_inc(xn_rdy[i], 1)

            for b in range(B):
                dve.wait_ge(x_in[b], 16)
                if b:
                    dve.wait_ge(ss_rdy[0], b)
                squares(0, x0, b)
            dve.wait_ge(silu_exp, 1)
            link(ts(silu[:, 1, :], silu[:, 0, :], 1.0, None, ALU.add))
            link(nc.vector.reciprocal(silu[:, 2, :], silu[:, 1, :]))
            tt(silu[:, 3, :], cond_sb[:, :], silu[:, 2, :], ALU.mult).then_inc(silu_rdy, 1)
            ts(film1c[:, 0:1], col("film1_b", 0), 1.0, None, ALU.add)
            ts(film1c[:, 1:2], col("film2_b", 0), 1.0, None, ALU.add)
            link(ts(qbs[:, :], col("q_b"), SCALE0, None, ALU.mult))
            dve.wait_ge(film_mm, 1)
            for i in range(2):
                ts(fA[i][:, :], PS[:, 7, 8 * i:8 * i + B], film1c[:, i:i + 1], col(f"norm{i + 1}_w"), ALU.add,
                   ALU.mult)
                last = ts(fB[i][:, :], PS[:, 7, 8 * i + 4:8 * i + 4 + B], col(f"film{i + 1}_b", 1), None, ALU.add)
            last.then_inc(film_rdy, 1)
            for b in range(B):
                scaled(0, x0, xn[0], b)
            dve.wait_ge(ada_mm, 1)
            ts(fB[2][:, :], PS[:, 7, 0:B], col("b_ada"), col("ln1_b"), ALU.add, ALU.add).then_inc(film_rdy, 1)
            for b in range(B):
                dve.wait_ge(qkv0_mm, b + 1)
                cp(tiles(v0, b), PS[:, b, 0:N].rearrange("p (t d) -> p t d", d=D)).then_inc(v0_rdy, 1)
            for b in range(B):
                dve.wait_ge(s0_mm, b + 1)
                red(nm0[:, b, :], PS[:, 4 + b, :].rearrange("p (t m) -> p t m", m=N), AX.X, ALU.max,
                    negate=True).then_inc(nm0_rdy, 1)
            for b in range(B):
                dve.wait_ge(exp0_rdy, b + 1)
                link(nc.vector.reciprocal(rec0[:, b, :], sum0[:, b, :]))
                for t in range(TB):
                    last = ts(pn0[:, b, t, :], p0[:, b, t, :], rec0[:, b, t:t + 1], None, ALU.mult)
                last.then_inc(pn0_rdy, 1)
            for b in range(B):
                dve.wait_ge(pt0_mm, b + 1)
                cp(pT0[:, b, :, :], PS[:, b, :].rearrange("p (t m) -> p t m", m=N)).then_inc(pt0_rdy, 1)
            dve.wait_ge(qkvw_in, 16)
            link(red(wsum[:, :, :], wqkv_sb[:, :, 0:2, :].rearrange("p a g (h c) -> p a (g h) c", c=HD), AX.X,
                     ALU.add))
            ts(wmean[:, :, :], wsum[:, :, :], -1.0 / HD, None, ALU.mult).then_inc(wsum_rdy, 1)
            for b in range(B):
                dve.wait_ge(proj_mm, b + 1)
                dve.wait_ge(xpb_rdy, b + 1)
                tt(tiles(x1, b), PS[:, b, 0:N].rearrange("p (t d) -> p t d", d=D), tiles(xpb, b),
                   ALU.add).then_inc(x1_rdy, 1)
                dve.wait_ge(x1_rdy, b + 1)
                if b:
                    dve.wait_ge(ss_rdy[1], b)
                else:
                    dve.wait_ge(ss_rdy[0], B)
                squares(1, x1, b)
            for b in range(B):
                scaled(1, x1, xn[1], b)
            ts(qg8[:, 0:1], col("qn_g"), HD ** -0.5, None, ALU.mult)
            ts(qg8[:, 1:2], col("qn_b"), HD ** -0.5, None, ALU.mult).then_inc(film_rdy, 1)

            dve.wait_ge(w16_rdy, 1)
            tt(w_half[1], w_all, w_half[0], ALU.subtract).then_inc(w16_rdy, 1)

            def row_stats(i, src, n):
                link(nc.vector.bn_stats(stats[:, i, n, :], src[:, n, :]))
                return nc.vector.bn_aggr(mv[:, i, n, :], stats[:, i, n, :])

            for b in range(B):
                dve.wait_ge(down_mm, b + 1)
                dve.wait_ge(x1b_rdy, b + 1)
                tt(tiles(x2, b), PS[:, b, 0:N].rearrange("p (t d) -> p t d", d=D), tiles(x1b, b),
                   ALU.add).then_inc(x2_rdy, 1)
                dve.wait_ge(x2_rdy, b + 1)
                for t in range(TB):
                    last = row_stats(0, x2, b * TB + t)
                last.then_inc(ss_rdy[2], 1)
            for b in range(B):
                dve.wait_ge(rs_rdy[2], b + 1)
                dve.wait_ge(t_done[0], b + 1)
                for t in range(TB):
                    n = b * TB + t
                    last = ts(xn[0][:, n, :], x2[:, n, :], mv[:, 0, n, 0:1], rs[2][:, n:n + 1], ALU.subtract,
                              ALU.mult)
                last.then_inc(xn_rdy[2], 1)
            for b in range(B):
                dve.wait_ge(h_rdy[2], b + 1)
                h = hT[2][:, b * N:(b + 1) * N]
                cp(h16[:, 0, b * N:(b + 1) * N], h).then_inc(h16_rdy, 1)
                dve.wait_ge(h16_rdy, 2 * b + 1)
                tt(h16[:, 1, b * N:(b + 1) * N], h, h16[:, 0, b * N:(b + 1) * N], ALU.subtract).then_inc(h16_rdy, 1)

            def row_max(p, s):
                u = UP * p + s
                dve.wait_ge(s_mm, u + 1)
                wait(dve, exp_rdy, u - 1)
                red(nm[:, s % 2, :], PS[:, s % 2, :].rearrange("p (t m) -> p t m", m=N), AX.X, ALU.max,
                    negate=True).then_inc(nm_rdy, 1)

            def copy_low(p, s):
                u = UP * p + s
                dve.wait_ge(ph_rdy, u + 1)
                tt(pT[:, s % 2, 1, :, :], PS[:, 2 + s % 2, :].rearrange("p (m n) -> p m n", n=N),
                   pT[:, s % 2, 0, :, :], ALU.subtract).then_inc(pt_rdy, 1)

            def copy_v_low(p, t):
                g = NT * p + t
                dve.wait_ge(qkv_copied, g + 2)
                tt(vv[:, 1, t, :, 0:HD], PS[:, 4, 2 * P:3 * P].rearrange("p (h c) -> p h c", c=HD),
                   vv[:, 0, t, :, 0:HD], ALU.subtract).then_inc(v_copied, 1)

            def sum_squares(p, b):
                g = 4 * p + b
                dve.wait_ge(sq_rdy, g + 1)
                red(qk_ss[:, :], qk_sq[:, :, :].rearrange("p t (h c) -> p (t h) c", c=HD), AX.X,
                    ALU.add).then_inc(qkss_rdy, 1)
                dve.wait_ge(qkss_rdy, g + 1)
                wait(dve, rs1_rdy, g)
                ts(qk_var[:, :], qk_ss[:, :], 1.0 / HD, EPS1, ALU.mult, ALU.add).then_inc(var_rdy, 1)

            def normalize(p, s):
                u, b, hh = UP * p + s, (s % UP) // 2, s % 2
                dve.wait_ge(pv_mm, u + 1)
                o = PS[:, 6, 0:TB * VD].rearrange("p (t c) -> p t c", c=VD)
                nc.vector.reciprocal(rec[:, s % 2, :], o[:, :, HD]).then_inc(rec_rdy, 1)
                dve.wait_ge(rec_rdy, u + 1)
                tt(on[:, b * TB:(b + 1) * TB, hh * HD:(hh + 1) * HD], o[:, :, 0:HD],
                   rec[:, s % 2, :].unsqueeze(2).broadcast_to([P, TB, HD]), ALU.mult).then_inc(o_rdy, 1)

            def slot_(p, s):
                if has_unit(p, s + 1):
                    row_max(p, s + 1)
                for s0, dp, b in SUM_SLOTS:
                    if s == s0 and in_range(p, dp):
                        sum_squares(p + dp, b)
                if has_unit(p, s - 1):
                    normalize(p, s - 1)
                if has_unit(p, s):
                    copy_low(p, s)
                if in_range(p, 1):
                    copy_v_low(p + 1, s - 2)

            run_pairs(dve, slot_)

            for i in range(2):
                dve.wait_ge(wo_mm, i + 1)
                tt(x3[:, 4 * i:4 * i + 4, :], PS[:, 4 + i, :].rearrange("p (t d) -> p t d", d=D),
                   x2[:, 4 * i:4 * i + 4, :], ALU.add).then_inc(x3_rdy, 1)
            dve.wait_ge(x3_rdy, 2)
            for t in range(NT):
                last = row_stats(1, x3, t)
            last.then_inc(ss_rdy[3], 1)
            dve.wait_ge(lg_mm, 1)
            lg = PS[:, 0, 0:NT * E].rearrange("p (t e) -> p t e", e=E)
            link(red(lmax[:, :], lg, AX.X, ALU.max))
            tt(lsub[:, :, :], lg, lmax[:, :].unsqueeze(2).broadcast_to([P, NT, E]), ALU.subtract).then_inc(lsub_rdy, 1)
            dve.wait_ge(lexp_rdy, 1)
            link(red(lsum[:, :], lexp[:, :, :], AX.X, ALU.add))
            link(nc.vector.reciprocal(lrec[:, :], lsum[:, :]))
            link(tt(gate[:, :, :].rearrange("p e t -> p t e"), lexp[:, :, :],
                    lrec[:, :].unsqueeze(2).broadcast_to([P, NT, E]), ALU.mult))
            cp(gx[:, :, :, :], gate[:, :, :].rearrange("p e t -> p t e").unsqueeze(3).broadcast_to([P, NT, E, GR]))\
                .then_inc(gx_rdy, 1)
            cp(gx2[:, :, :, :], gate[:, :, :].unsqueeze(3).broadcast_to([P, E, NT, 2])).then_inc(gx_rdy, 1)
            cp(g3[:, :, :, 0], gate[:, :, :]).then_inc(g3_rdy, 1)
            dve.wait_ge(g3_rdy, 1)
            link(tt(gr[:, 0, :, :], gate[:, :, :], g3[:, :, :, 0], ALU.subtract))
            cp(g3[:, :, :, 1], gr[:, 0, :, :]).then_inc(g3_rdy, 1)
            dve.wait_ge(g3_rdy, 2)
            link(tt(gr[:, 1, :, :], gr[:, 0, :, :], g3[:, :, :, 1], ALU.subtract))
            cp(g3[:, :, :, 2], gr[:, 1, :, :]).then_inc(g3_rdy, 1)
            cp(iotab[:, :], c32[:, P:2 * P]).then_inc(constb_rdy, 1)
            cp(identb[:, :], ident).then_inc(constb_rdy, 1)
            dve.wait_ge(out_in, 64)
            link(cp(blockb[:, :], cm[:, 0, :]))
            dve.wait_ge(rs_rdy[3], 1)
            stt(nmr[:, :], mv[:, 1, :, 0], -1.0, rs[3][:, :], ALU.mult, ALU.mult).then_inc(nmr_rdy, 1)

            dve.wait_ge(gt_mm, 3)
            link(cp(V2[:, :], PS[:, 7, 0:P]))
            nc.vector.memset(digit[:, :], 0)
            link(nc.vector.memset(prefix[:, :], 0))
            cp(thr[:, :], ci[:, 0:1]).then_inc(thr_rdy, 1)
            dve.wait_ge(v_rdy, 2)
            with dve.Fori(0, NR) as r:
                dve.wait_ge(thr_rdy, r + 1)
                ts(ge[:, :], V[:, :], thr[:, :].bitcast(f32), None, ALU.is_ge, ALU.add,
                   accum_out=cnt[:, 0:1]).then_inc(cnt_rdy, 1)
                dve.wait_ge(cnt_rdy, r + 1)
                ts(okb[:, :], cnt[:, 0:1], float(CAP), None, ALU.is_ge).then_inc(ok_rdy, 1)
                tt(prefix[:, :], prefix[:, :], digit[:, :], ALU.bitwise_or).then_inc(prefix_rdy, 1)
                dve.wait_ge(prefix_rdy, r + 1)
                tt(trial[:, :], prefix[:, :], ci[:, ds(r + 1, 1)], ALU.bitwise_or).then_inc(trial_rdy, 1)
                dve.wait_ge(k_mm, r + 1)
                ts(digit[:, :], PS[:, 4, 0:1], -1.0, c32[:, ds(r + 2 * P, 1)], ALU.add, ALU.mult)\
                    .then_inc(dig_rdy, 1)
                dve.wait_ge(dig_rdy, r + 1)
                dve.wait_ge(trial_rdy, r + 1)
                tt(thr[:, :], trial[:, :], digit[:, :], ALU.bitwise_or).then_inc(thr_rdy, 1)
            dve.wait_ge(thr_rdy, NR + 1)

            kth = thr[:, :].bitcast(f32)
            link(ts(gt[:, :], V2[:, :], kth, None, ALU.is_gt, ALU.add, accum_out=cnt[:, 1:2]))
            ts(eq[:, :], V2[:, :], kth, None, ALU.is_equal, ALU.add, accum_out=cnt[:, 2:3]).then_inc(tie_rdy, 1)
            dve.wait_ge(tie_rdy, 1)
            nc.vector.tensor_tensor_scan(scan1[:, :], eq[:, :], zero[:, :], 0.0, ALU.add, ALU.add)
            dve.wait_ge(tie_mm, 1)
            link(ts(need[:, :], PS[:, 5, 0:1], -1.0, float(CAP), ALU.mult, ALU.add))
            link(stt(sel[:, :], scan1[:, :], need[:, :], eq[:, :], ALU.is_le, ALU.mult))
            stt(mask[:, :], gt[:, :], 0.0, sel[:, :], ALU.add, ALU.add, accum_out=cnt[:, 3:4]).then_inc(off_rdy, 1)
            dve.wait_ge(off_rdy, 1)
            link(nc.vector.tensor_tensor_scan(scan2[:, :], mask[:, :], zero[:, :], 0.0, ALU.add, ALU.add))
            dve.wait_ge(off_mm, 1)
            stt(slot[:, :], scan2[:, :], PS[:, 6, 0:1], mask[:, :], ALU.add, ALU.mult).then_inc(slot_rdy, 1)
            dve.wait_ge(slot_mm, 1)
            link(cp(slotT[:, :, :, :], PS[:, 7, 0:P].rearrange("p (e t j) -> p e t j", t=NT, j=2)))
            dve.wait_ge(constb_rdy, 2)
            for t in range(NT):
                for e in range(E):
                    last = ts(OH[:, t, e, :], iotab[:, :], slotT[:, e, t, 0:1], None, ALU.is_equal)
                last.then_inc(oh_rdy, 1)
            dve.wait_ge(w_mm, 1)
            link(red(wsel[:, :], PS[:, 7, 0:3 * E].rearrange("p (e j) -> p e j", j=3), AX.X, ALU.add))
            dve.wait_ge(fc_in, 48)
            tt(b2_sb[:, :, :], b2_sb[:, :, :], wsel[:, :].unsqueeze(2).broadcast_to([P, E, D]),
               ALU.mult).then_inc(b2w_rdy, 1)
            dve.wait_ge(b2w_rdy, 1)
            for f in range(E):
                y = ys[:, f % 2, :]
                dve.wait_ge(fc2_mm, f + 1)
                if f >= 1:
                    dve.wait_ge(y_rdy, f)
                if f >= 2:
                    dve.wait_ge(sc_mm, f - 1)
                link(stt(y, PS[:, 4 + f % 2, 0:D], wsel[:, f:f + 1], b2_sb[:, f, :], ALU.mult, ALU.add))
                link(cp(y2[:, f % 2, 0, :], y))
                tt(y2[:, f % 2, 1, :], y, y2[:, f % 2, 0, :], ALU.subtract).then_inc(y_rdy, 1)
            for i in range(2):
                dve.wait_ge(sum_mm, i + 1)
                tt(y_out[:, 4 * i:4 * i + 4, :], PS[:, 6 + i, :].rearrange("p (t d) -> p t d", d=D),
                   x3[:, 4 * i:4 * i + 4, :], ALU.add).then_inc(out_rdy, 1)


def kernel(**inputs):
    import numpy as np
    import concourse.bacc as bacc
    from concourse.bass_utils import run_bass_kernel_spmd as run

    a = {k: np.asarray(v) for k, v in inputs.items()}
    g0 = lambda n: a["L0_cond_" + n]
    g1 = lambda n: a["L1_cond_" + n]
    columns = {n: g0(n) for n in ("norm1_w", "film1_b", "q_b", "k_b", "v_b", "norm2_w", "film2_b", "mlp_b1")}
    columns.update({n: g1(n) for n in ("b_ada", "ln1_g", "ln1_b", "mlp_g", "mlp_b", "b1s")})
    for n in ("qn_g", "qn_b", "kn_g", "kn_b"):
        columns[n] = np.tile(g1(n), 2)
    cols = np.concatenate([columns[n].reshape(-1, P).T for n in COLS], axis=1)
    part = np.arange(P)
    const32 = np.concatenate([np.eye(P), np.broadcast_to(part + 1, (P, P)),
                              np.broadcast_to(2.0 ** np.array(SHIFTS), (P, NR))], axis=1).astype(np.float32)
    digits = [np.minimum(part % GR, 4) << 28] + [(part % GR) << s for s in SHIFTS[1:]] + [part * 0]
    consti = np.stack(digits, axis=1).astype(np.int32)
    same = (part[:, None] // GR == part[None, :] // GR)
    tile_of, first = part % GR // 2, (part % 2 == 0)[:, None]
    constm = np.stack([same, same & first, same & first & (tile_of[:, None] < tile_of[None, :])],
                      axis=1).astype(np.float32)
    arrays = {
        "x": a["x"].reshape(TOK, D), "cols": cols, "cond": a["cond_1024"].T, "film1_w": g0("film1_w"),
        "film2_w": g0("film2_w"),
        "wqkvp0": np.stack([g0(n) for n in ("q_w", "k_w", "v_w", "proj_w")], axis=1),
        "w_ada": g1("W_ada").T, "mlp_w1": g0("mlp_w1"), "mlp_w2": g0("mlp_w2").reshape(FC, P, D).transpose(1, 0, 2),
        "rows": np.broadcast_to(np.stack([g0("proj_b"), g0("mlp_b2")]), (P, 2, D)),
        "wqkv": g1("Wqkv").reshape(3, NP, P, D).transpose(3, 1, 0, 2),
        "wout": g1("Wout").reshape(D, NP, P).transpose(2, 1, 0), "wgate": g1("Wgate").T,
        "fc1": g1("fc1s").transpose(2, 0, 1), "fc2": g1("fc2s").reshape(E, D, EC, P).transpose(3, 0, 2, 1),
        "b2s": np.broadcast_to(g1("b2s"), (P, E, D)), "const32": const32, "consti": consti, "constm": constm,
    }
    nc = bacc.Bacc("TRN2", target_bir_lowering=False, num_devices=1)
    arrays = {f"in_{k}": np.ascontiguousarray(v) for k, v in arrays.items()}
    args = [nc.dram_tensor(k, v.shape, mybir.dt.from_np(v.dtype), kind="ExternalInput").ap()
            for k, v in arrays.items()]
    args.append(nc.dram_tensor("out_0", (TOK, D), mybir.dt.float32, kind="ExternalOutput").ap())
    conditioned_sequence_kernel(nc, *args)
    r = run(nc, [arrays], core_ids=[0])
    return r.results[0]["out_0"].reshape(B, N, D)
```

```python
import concourse.bass as bass
from concourse import mybir
from contextlib import ExitStack

B, N, D = 4, 256, 128
TOK = B * N
P = 128
NT = TOK // P
TB = N // P
FF = 4 * D
FC = FF // P
H, HD = 16, 64
NP = H // 2
UP = 2 * B
E, DD = 8, 512
EC = DD // P
CAP = TOK // E
HC = CAP // 2
GR = P // E
VD = HD + 1
EPS0, EPS1 = 1e-6, 1e-5
SCALE0 = float(D) ** -0.5
WS = 64.0

COLS = {}
for _name, _n in (("norm1_w", 1), ("film1_b", 2), ("q_b", 1), ("k_b", 1), ("v_b", 1), ("norm2_w", 1),
                  ("film2_b", 2), ("mlp_b1", FC), ("b_ada", 1), ("ln1_g", 1), ("ln1_b", 1), ("qn_g", 1),
                  ("qn_b", 1), ("kn_g", 1), ("kn_b", 1), ("mlp_g", 1), ("mlp_b", 1), ("b1s", E * EC)):
    COLS[_name] = sum(n for _, n in COLS.values()), _n
NCOL = sum(n for _, n in COLS.values())
SHIFTS = [28] + list(range(24, -1, -4))
NR = len(SHIFTS)
NCONST = 2 * P + NR


STAGES = 30
FILM_WAVE, ADA_WAVE = 2, 6
MEAN_WAVE, CENTRE_WAVE, HIGH_WAVE, LOW_WAVE = 7, 8, 12, 22
WAVES = STAGES + UP - 2
NORM_SLOTS = [(2 * b + 2, 1, b) for b in range(B)]
SUM_SLOTS = [(2 * b + 3, 1, b) for b in range(B)]
TURN_SLOTS = [(2 * b + 5, 1, b) for b in range(B - 1)] + [(3, 0, B - 1)]


WOUT_PARTS = {3: [(0, 0), (0, 1)], 9: [(1, 5), (1, 6)], **{s: [(1, s - 4), (0, s - 2)] for s in range(4, 9)}}


HALVES = ((0, 0), (0, 1), (1, 0))


WARM_TIE, WARM_SLOT = 10, 8


def in_range(p, dp):
    return not isinstance(p, int) or 0 <= p + dp < NP


def has_unit(p, s):
    return not isinstance(p, int) or 0 <= UP * p + s < UP * NP


def qkv_bank(p, t):
    return (0, 1, 2, 3, 6, 7, 4, 4)[t] if isinstance(p, int) and p == 0 else 4


def wait(eng, semaphore, value):
    if not isinstance(value, int) or value > 0:
        eng.wait_ge(semaphore, value)


def run_layers(eng, stages, once, first_slot, slot_):
    for w in range(WAVES):
        for k, work in reversed(stages):
            if 0 <= w - k < B:
                work(w - k)
        if w in once:
            once[w]()
        if w >= STAGES:
            first_slot(w - STAGES + 2)
    with eng.Fori(0, NP - 2) as p:
        for s in range(2, 2 + UP):
            slot_(p, s)
    for p in range(NP - 2, NP):
        for s in range(2, 2 + UP):
            slot_(p, s)


def conditioned_sequence_kernel(nc, x, cols, cond, film1_w, film2_w, wqkvp0, w_ada, mlp_w1, mlp_w2, rows,
                                wqkv, wout, wgate, fc1, fc2, b2s, const32, consti, constm, out):
    f32, bf16, f16, i32, u16 = (mybir.dt.float32, mybir.dt.bfloat16, mybir.dt.float16, mybir.dt.int32,
                                mybir.dt.uint16)
    ALU, ACT, AX = mybir.AluOpType, mybir.ActivationFunctionType, mybir.AxisListType
    ds = bass.ds
    ctx = ExitStack()
    with ctx:
        def sb(name, shape, dt=f32):
            return ctx.enter_context(nc.sbuf_tensor(name, shape, dt))

        def sem(name):
            return ctx.enter_context(nc.semaphore(name))

        PS = ctx.enter_context(nc.psum_tensor("banks", [P, 8, 512], f32))

        cols_sb = sb("cols_sb", [P, NCOL])
        cond_sb = sb("cond_sb", [P, B])
        film_w = [sb("film1_sb", [P, 2 * D]), sb("film2_sb", [P, 2 * D])]
        w0 = sb("w0", [P, 4, D])
        wada_sb = sb("wada_sb", [P, D])
        w1_sb = sb("w1_sb", [P, FF])
        w2_sb = sb("w2_sb", [P, FC, D])
        rows_sb = sb("rows_sb", [P, 2, D])
        wout_sb = sb("wout_sb", [P, NP, D])
        wgate_sb = sb("wgate_sb", [P, E])
        fc1_sb = sb("fc1_sb", [P, E, DD])
        wqkv_sb = fc1_sb[:, :, :].rearrange("p e c -> p (e c)")[:, 0:NP * 3 * P].rearrange(
            "p (a g c) -> p a g c", a=NP, g=3)
        wqkv16 = sb("wqkv16", [P, 2, NP, 3 * P], f16)
        fc2_sb = sb("fc2_sb", [P, E, EC, D])
        b2_sb = sb("b2_sb", [P, E, D])
        c32 = sb("c32", [P, NCONST])
        ci = sb("ci", [P, NR + 1], i32)
        cm = sb("cm", [P, 3, P])
        identb = sb("identb", [P, P], bf16)
        iotab = sb("iotab", [P, CAP, E], bf16)
        blockb = sb("blockb", [P, P], bf16)
        ident = c32[:, 0:P]
        mhalf = sb("mhalf", [P, 2 * 4])

        def col(name, i=0):
            o = COLS[name][0] + i
            return cols_sb[:, o:o + 1]

        x0 = y_out = sb("x0_out", [P, NT, D])
        x2 = sb("x2", [P, NT, D])
        x3 = sb("x3", [P, NT, D])
        xn = [sb(f"xn{i}", [P, NT, D]) for i in range(2)]
        hT0 = sb("hT0", [P, TOK])
        hT = [hT0, hT0, hT0]
        h16 = sb("h16", [P, 2, TOK], f16)
        sq = sb("sq", [P, 2, D])
        ss = [sb("ss0", [P, NT]), sb("ss1", [P, NT])]
        rs = [sb(f"rs{i}", [P, NT]) for i in range(4)]
        var = [sb(f"var{i}", [P, NT]) for i in range(4)]
        stats = sb("stats", [P, 2, NT, 6])
        mv = sb("mv", [P, 2, NT, 2])
        silu = sb("silu", [P, 4, B])
        film1c = sb("film1c", [P, 2])
        fA = [sb("fA0", [P, B]), sb("fA1", [P, B])]
        fB = [sb(f"fB{i}", [P, B]) for i in range(3)]
        qbs = sb("qbs", [P, 1])
        nm0 = sb("nm0", [P, B, TB])
        reuse_a, reuse_b, reuse_c = sb("reuse_a", [P, NP * TOK]), sb("reuse_b", [P, FC * TOK]), \
            sb("reuse_c", [P, 5 * TOK])
        p0 = reuse_a[:, 0:2 * TOK].rearrange("p (b t m) -> p b t m", b=B, t=TB)
        sum0 = sb("sum0", [P, B, TB])
        rec0 = sb("rec0", [P, B, TB])
        pn0 = reuse_a[:, 2 * TOK:4 * TOK].rearrange("p (b t m) -> p b t m", b=B, t=TB)
        pT0 = reuse_a[:, 4 * TOK:6 * TOK].rearrange("p (b t m) -> p b t m", b=B, t=TB)
        qT0 = reuse_a[:, 6 * TOK:7 * TOK]
        kT0 = reuse_a[:, 7 * TOK:8 * TOK]
        oT = reuse_a[:, :].rearrange("p (a n) -> p a n", a=NP)
        gel = reuse_b[:, :].rearrange("p (c n) -> p c n", c=FC)
        OH = reuse_b[:, :].bitcast(bf16).rearrange("p (t c e) -> p t c e", t=NT, e=E)

        def part(i):
            return reuse_c[:, i * TOK:(i + 1) * TOK]

        def rows_of(ap):
            return ap.rearrange("p (t d) -> p t d", d=D)

        v0, xpb, x1, x1b, oT0 = (rows_of(part(i)) if i < 4 else part(i) for i in range(5))
        V, x3T = part(0), part(1)
        xh = part(2).bitcast(f16).rearrange("p (j t d) -> p j t d", j=2, t=NT)
        gT = part(3).rearrange("p (e c) -> p e c", e=E)
        gx = part(4).rearrange("p (t e j) -> p t e j", t=NT, e=E)
        ohT = reuse_a[:, 0:4 * TOK].bitcast(bf16).rearrange("p (e n) -> p e n", e=E)

        wsum = sb("wsum", [P, NP, 4])
        wmean = sb("wmean", [P, NP, 4])
        qg8 = sb("qg8", [P, 2])
        qk_raw = sb("qk_raw", [P, NT, 2 * P])
        qk_sq = sb("qk_sq", [P, TB, 2 * P])
        qk_ss = sb("qk_ss", [P, 8])
        qk_var = sb("qk_var", [P, 8])
        qk_rs = sb("qk_rs", [P, 8])
        qT = sb("qT", [P, B, N])
        kT = sb("kT", [P, B, N])
        vv = sb("vv", [P, 2, NT, 2, VD], f16)
        nm = sb("nm", [P, 2, TB])
        pr = sb("pr", [P, 2, TB, N])
        pT = sb("pT", [P, 2, 2, TB, N], f16)
        rec = sb("rec", [P, 2, TB])
        on = xn[1]

        lmax = sb("lmax", [P, NT])
        lsub = sb("lsub", [P, NT, E])
        lexp = sb("lexp", [P, NT, E])
        lsum = sb("lsum", [P, NT])
        lrec = sb("lrec", [P, NT])
        gate = sb("gate", [P, E, NT])
        g3 = sb("g3", [P, E, NT, 3], bf16)
        gr = sb("gr", [P, 2, E, NT])
        gx2 = sb("gx2", [P, E, NT, 2])
        V2 = sb("V2", [P, P])
        ge = sb("ge", [P, TOK], bf16)
        upper = sb("upper", [P, TOK], u16)
        cnt = sb("cnt", [P, 4])
        okb = sb("okb", [P, 1], bf16)
        digit = sb("digit", [P, 1], i32)
        prefix = sb("prefix", [P, 1], i32)
        trial = sb("trial", [P, 1], i32)
        thr = sb("thr", [P, 1], i32)
        gt, eq, scan1, sel, mask, scan2, slot = (
            pr[:, :, :, :].rearrange("p i t m -> p (i t m)")[:, i * P:(i + 1) * P] for i in range(7))
        zero = sb("zero", [P, P])
        need = sb("need", [P, 1])
        slotT = sb("slotT", [P, NT, E], bf16)
        nmr = sb("nmr", [P, NT])
        wsel = sb("wsel", [P, E])
        hid = hT0[:, :].rearrange("p (j c n) -> p j c n", j=2, c=EC)
        ys = sb("ys", [P, 2, D])
        y2 = sb("y2", [P, 2, 2, D], f16)

        x_in = [sem(f"x_in{b}") for b in range(B)]
        film_in, l0_in, mlp_in, qkvw_in, out_in, fc_in, const_in, ident_in, film2_in = (
            sem(n) for n in (
                "film_in", "l0_in", "mlp_in", "qkvw_in", "out_in", "fc_in", "const_in", "ident_in", "film2_in"))
        film_mm, silu_exp, silu_rdy, film_rdy = (sem(n) for n in ("film_mm", "silu_exp", "silu_rdy", "film_rdy"))
        ada_mm = sem("ada_mm")
        mhalf_rdy, xpb_rdy, x1b_rdy, ones_rdy, wsum_rdy, wc_rdy, w16_rdy, h16_rdy = (
            sem(n) for n in ("mhalf_rdy", "xpb_rdy", "x1b_rdy", "ones_rdy", "wsum_rdy", "wc_rdy", "w16_rdy",
                             "h16_rdy"))
        ph_rdy, v_copied = sem("ph_rdy"), sem("v_copied")
        ss_rdy, rs_rdy, xn_rdy, t_done, h_rdy = ([sem(f"{n}{i}") for i in range(4)] for n in
                                                 ("ss_rdy", "rs_rdy", "xn_rdy", "t_done", "h_rdy"))
        qkv0_mm, qk0_rdy, v0_rdy, s0_mm, nm0_rdy, exp0_rdy, pn0_rdy, pt0_mm, pt0_rdy, o0_mm, o0_rdy, proj_mm, \
            x1_rdy, up_mm, gel_rdy, down_mm, x2_rdy = (sem(n) for n in (
                "qkv0_mm", "qk0_rdy", "v0_rdy", "s0_mm", "nm0_rdy", "exp0_rdy", "pn0_rdy", "pt0_mm", "pt0_rdy",
                "o0_mm", "o0_rdy", "proj_mm", "x1_rdy", "up_mm", "gel_rdy", "down_mm", "x2_rdy"))
        dve_step, pool_step = sem("dve_step"), sem("pool_step")
        qkv_mm, qkv_copied, sq_rdy, qkss_rdy, var_rdy, rs1_rdy, qkn_rdy, qkt_mm, qk_rdy = (
            sem(n) for n in ("qkv_mm", "qkv_copied", "sq_rdy", "qkss_rdy", "var_rdy", "rs1_rdy", "qkn_rdy",
                             "qkt_mm", "qk_rdy"))
        s_mm, nm_rdy, exp_rdy, pt_mm, pt_rdy, pv_mm, rec_rdy, o_rdy, ot_mm, ot_rdy = (
            sem(n) for n in ("s_mm", "nm_rdy", "exp_rdy", "pt_mm", "pt_rdy", "pv_mm", "rec_rdy", "o_rdy",
                             "ot_mm", "ot_rdy"))
        wo_mm, x3_rdy, x3t_mm, x3t_rdy, lg_mm, lsub_rdy, lexp_rdy, gx_rdy, gt_mm, v_rdy, g3_rdy = (
            sem(n) for n in ("wo_mm", "x3_rdy", "x3t_mm", "x3t_rdy", "lg_mm", "lsub_rdy", "lexp_rdy", "gx_rdy",
                             "gt_mm", "v_rdy", "g3_rdy"))
        upper_rdy = sem("upper_rdy")
        thr_rdy, cnt_rdy, ok_rdy, k_mm, dig_rdy, prefix_rdy, trial_rdy = (
            sem(n) for n in ("thr_rdy", "cnt_rdy", "ok_rdy", "k_mm", "dig_rdy", "prefix_rdy", "trial_rdy"))
        tie_rdy, tie_mm, off_rdy, off_mm, slot_rdy, slot_mm, oh_rdy, xn3_rdy, xh_rdy = (
            sem(n) for n in ("tie_rdy", "tie_mm", "off_rdy", "off_mm", "slot_rdy", "slot_mm",
                             "oh_rdy", "xn3_rdy", "xh_rdy"))
        nmr_rdy, w_mm, b2w_rdy, gath_mm, g_rdy, fc1_mm, hid_rdy, oht_mm, oht_rdy, fc2_mm, sum_mm, y_rdy, sc_mm, \
            out_rdy, out_st, constb_rdy = (sem(n) for n in (
                "nmr_rdy", "w_mm", "b2w_rdy", "gath_mm", "g_rdy", "fc1_mm", "hid_rdy", "oht_mm", "oht_rdy", "fc2_mm",
                "sum_mm", "y_rdy", "sc_mm", "out_rdy", "out_st", "constb_rdy"))

        def tiles(t, b):
            return t[:, b * TB:(b + 1) * TB, :]

        w_all = wqkv_sb.rearrange("p a g c -> p (a g c)")
        w_half = [wqkv16[:, i, :, :].rearrange("p a c -> p (a c)") for i in range(2)]

        block = ctx.enter_context(nc.Block())

        @block.sync
        def _(sp):
            xv = x.rearrange("(t p) d -> p t d", p=P)
            for b in range(2):
                sp.dma_start(tiles(x0, b), tiles(xv, b)).then_inc(x_in[b], 16)
            sp.dma_start(w0[:, :, :], wqkvp0).then_inc(l0_in, 16)
            for b in range(2, B):
                sp.dma_start(tiles(x0, b), tiles(xv, b)).then_inc(x_in[b], 16)
            sp.dma_start(rows_sb[:, :, :], rows).then_inc(l0_in, 16)
            sp.dma_start(wqkv_sb[:, :, :, :], wqkv).then_inc(qkvw_in, 16)
            sp.dma_start(w1_sb[:, :], mlp_w1).then_inc(mlp_in, 16)
            sp.dma_start(w2_sb[:, :, :], mlp_w2).then_inc(mlp_in, 16)
            sp.dma_start(wout_sb[:, :, :], wout).then_inc(out_in, 16)
            sp.dma_start(wgate_sb[:, :], wgate).then_inc(out_in, 16)
            sp.dma_start(ci[:, :], consti).then_inc(out_in, 16)
            sp.dma_start(cm[:, :, :], constm).then_inc(out_in, 16)
            sp.dma_start(b2_sb[:, :, :], b2s).then_inc(fc_in, 16)
            sp.dma_start(fc2_sb[:, :, :, :], fc2).then_inc(fc_in, 16)
            sp.wait_ge(w16_rdy, 2)
            sp.dma_start(fc1_sb[:, :, :], fc1).then_inc(fc_in, 16)
            ov = out.rearrange("(t p) d -> p t d", p=P)
            for i in range(2):
                sp.wait_ge(out_rdy, i + 1)
                sp.dma_start(ov[:, 4 * i:4 * i + 4, :], y_out[:, 4 * i:4 * i + 4, :]).then_inc(out_st, 16)
            sp.wait_ge(out_st, 32)

        @block.gpsimd
        def _(pool):
            steps = [0]

            def rstd(dst, tmp, src, scale, eps, done):
                n = src.shape[1]
                nc.gpsimd.tensor_scalar(tmp, src, scale, eps, ALU.mult, ALU.add).then_inc(pool_step, 1)
                steps[0] += 1
                pool.wait_ge(pool_step, steps[0])
                nc.gpsimd.tensor_tensor(dst, tmp, mhalf[:, 0:n], ALU.pow).then_inc(done, 1)

            nc.gpsimd.memset(mhalf[:, :], -0.5).then_inc(mhalf_rdy, 1)
            nc.gpsimd.memset(vv[:, 0, :, :, HD:VD], WS).then_inc(ones_rdy, 1)
            nc.gpsimd.memset(vv[:, 1, :, :, HD:VD], 0.0).then_inc(ones_rdy, 1)
            nc.gpsimd.memset(zero[:, :], 0.0).then_inc(ones_rdy, 1)
            pool.wait_ge(mhalf_rdy, 1)

            def norm0(b):
                pool.wait_ge(ss_rdy[0], b + 1)
                sl = slice(b * TB, (b + 1) * TB)
                rstd(rs[0][:, sl], var[0][:, sl], ss[0][:, sl], 1.0 / D, EPS0, rs_rdy[0])

            def add_proj_b(b):
                pool.wait_ge(l0_in, 32)
                pool.wait_ge(x_in[b], 16)
                nc.gpsimd.tensor_tensor(tiles(xpb, b), tiles(x0, b),
                                        rows_sb[:, 0:1, :].broadcast_to([P, TB, D]), ALU.add).then_inc(xpb_rdy, 1)

            def centre_weights():
                pool.wait_ge(wsum_rdy, 1)
                nc.gpsimd.tensor_tensor(wqkv_sb[:, :, 0:2, :].rearrange("p a g (h c) -> p a (g h) c", c=HD),
                                        wqkv_sb[:, :, 0:2, :].rearrange("p a g (h c) -> p a (g h) c", c=HD),
                                        wmean[:, :, :].unsqueeze(3).broadcast_to([P, NP, 4, HD]),
                                        ALU.add).then_inc(wc_rdy, 1)

            def norm1(b):
                sl = slice(b * TB, (b + 1) * TB)
                pool.wait_ge(ss_rdy[1], b + 1)
                rstd(rs[1][:, sl], var[1][:, sl], ss[1][:, sl], 1.0 / D, EPS0, rs_rdy[1])

            def add_mlp_b2(b):
                pool.wait_ge(x1_rdy, b + 1)
                nc.gpsimd.tensor_tensor(tiles(x1b, b), tiles(x1, b),
                                        rows_sb[:, 1:2, :].broadcast_to([P, TB, D]), ALU.add).then_inc(x1b_rdy, 1)

            def norm2(b):
                sl = slice(b * TB, (b + 1) * TB)
                pool.wait_ge(ss_rdy[2], b + 1)
                rstd(rs[2][:, sl], var[2][:, sl], mv[:, 0, sl, 1], 1.0, EPS1, rs_rdy[2])

            def first_slot(s):
                b = s - 2
                if b < B:
                    pool.wait_ge(var_rdy, b + 1)
                    if b:
                        pool.wait_ge(qkn_rdy, b)
                    nc.gpsimd.tensor_tensor(qk_rs[:, :], qk_var[:, :], mhalf[:, :], ALU.pow).then_inc(rs1_rdy, 1)

            def slot_(p, s):
                for s0, dp, b in NORM_SLOTS:
                    if s != s0 or not in_range(p, dp):
                        continue
                    g = 4 * p + 4 * dp + b
                    raw = qk_raw[:, b * TB:(b + 1) * TB, :]
                    pool.wait_ge(qkv_copied, 2 * g + 2)
                    nc.gpsimd.tensor_tensor(qk_sq[:, :, :], raw, raw, ALU.mult).then_inc(sq_rdy, 1)
                    pool.wait_ge(var_rdy, g + 1)
                    nc.gpsimd.tensor_tensor(qk_rs[:, :], qk_var[:, :], mhalf[:, :], ALU.pow).then_inc(rs1_rdy, 1)
                    pool.wait_ge(rs1_rdy, g + 1)
                    nc.gpsimd.tensor_tensor(
                        raw.rearrange("p t (h c) -> p (t h) c", c=HD),
                        raw.rearrange("p t (h c) -> p (t h) c", c=HD),
                        qk_rs[:, :].unsqueeze(2).broadcast_to([P, 4 * TB, HD]), ALU.mult).then_inc(qkn_rdy, 1)

            run_layers(pool, ((1, norm0), (5, add_proj_b), (17, norm1), (20, add_mlp_b2), (25, norm2)),
                       {CENTRE_WAVE: centre_weights}, first_slot, slot_)

            pool.wait_ge(ss_rdy[3], 1)
            rstd(rs[3][:, :], var[3][:, :], mv[:, 1, :, 1], 1.0, EPS1, rs_rdy[3])
            pool.wait_ge(xn3_rdy, 1)
            nc.gpsimd.tensor_copy(xh[:, 0, :, :], xn[1][:, :, :]).then_inc(xh_rdy, 1)
            pool.wait_ge(xh_rdy, 1)
            nc.gpsimd.tensor_tensor(xh[:, 1, :, :], xn[1][:, :, :], xh[:, 0, :, :],
                                    ALU.subtract).then_inc(xh_rdy, 1)

        def wout_product(pe, mm, i, a):
            for t in range(4 * i, 4 * i + 4):
                pe.wait_ge(ot_rdy, 4 * a + t // TB + 1)
                last = mm(PS[:, 4 + i, (t % 4) * P:(t % 4 + 1) * P], oT[:, a, t * P:(t + 1) * P],
                          wout_sb[:, a, :], start=(a == 0 and t % 4 == 0), stop=(a == NP - 1),
                          skip_group_check=True)
            return last

        def experts_pe(pe, mm, tr):
            def warm(n):
                for _ in range(n):
                    mm(PS[:, 3, 0:P], blockb[:, :], blockb[:, :], start=True, stop=True)

            for i in range(2):
                wout_product(pe, mm, i, NP - 1).then_inc(wo_mm, 1)
            for i in range(2):
                pe.wait_ge(x3_rdy, i + 1)
                for t in range(4):
                    last = tr(PS[:, 2 + i, t * P:(t + 1) * P], x3[:, 4 * i + t, :], ident)
                last.then_inc(x3t_mm, 1)
            for i in range(2):
                pe.wait_ge(x3t_rdy, i + 1)
                for t in range(4 * i, 4 * i + 4):
                    last = mm(PS[:, 0, t * E:(t + 1) * E], x3T[:, t * P:(t + 1) * P], wgate_sb[:, :],
                              start=True, stop=True)
            last.then_inc(lg_mm, 1)
            pe.wait_ge(gx_rdy, 1)
            for t in range(NT):
                last = tr(PS[:, 5 + t // 4, (t % 4) * P:(t % 4 + 1) * P],
                          gx[:, t, :, :].rearrange("p e j -> p (e j)"), ident)
                if t % 4 == 3:
                    last.then_inc(gt_mm, 1)
            pe.wait_ge(gx_rdy, 2)
            tr(PS[:, 7, 0:P], gx2[:, :, :, :].rearrange("p e t j -> p (e t j)"), ident).then_inc(gt_mm, 1)

            for r in range(NR):
                pe.wait_ge(ok_rdy, r + 1)
                mm(PS[:, 4, 0:1], blockb[:, :], okb[:, :], start=True, stop=True).then_inc(k_mm, 1)
            pe.wait_ge(tie_rdy, 1)
            mm(PS[:, 5, 0:1], cm[:, 1, :], cnt[:, 1:2], start=True, stop=False)
            mm(PS[:, 5, 0:1], cm[:, 2, :], cnt[:, 2:3], start=False, stop=True).then_inc(tie_mm, 1)
            warm(WARM_TIE)
            pe.wait_ge(off_rdy, 1)
            mm(PS[:, 6, 0:1], cm[:, 2, :], cnt[:, 3:4], start=True, stop=True).then_inc(off_mm, 1)
            warm(WARM_SLOT)
            pe.wait_ge(slot_rdy, 1)
            tr(PS[:, 7, 0:P], slot[:, :], ident).then_inc(slot_mm, 1)
            warm(WARM_SLOT)

            pe.wait_ge(xh_rdy, 2)
            for t in range(NT):
                pe.wait_ge(oh_rdy, t + 1)
                for i in range(2):
                    for j in range(2):
                        last = mm(PS[:, i, :], xh[:, j, t, :], OH[:, t, i * HC:(i + 1) * HC, :],
                                  start=(t == 0 and j == 0), stop=(t == NT - 1 and j == 1))
                    if t == NT - 1:
                        last.then_inc(gath_mm, 1)
                if t >= 4:
                    pe.wait_ge(oht_rdy, t - 3)
                for e in range(E):
                    last = tr(PS[:, 2 + t % 4, e * 64:(e + 1) * 64].bitcast(bf16), OH[:, t, :, e], identb[:, :])
                last.then_inc(oht_mm, 1)
            pe.wait_ge(g3_rdy, 3)
            for e in range(E):
                for t in range(NT):
                    last = mm(PS[:, 7, 3 * e:3 * e + 3], OH[:, t, :, e], g3[:, e, t, :],
                              start=(t == 0), stop=(t == NT - 1))
            last.then_inc(w_mm, 1)
            pe.wait_ge(fc_in, 48)
            for e in range(E + 2):
                if e < E:
                    if e == 0:
                        pe.wait_ge(g_rdy, 2)
                    if e >= 2:
                        pe.wait_ge(hid_rdy, e - 1)
                    for c in range(EC):
                        last = mm(PS[:, e % 2, c * CAP:(c + 1) * CAP], fc1_sb[:, e, c * P:(c + 1) * P],
                                  gT[:, e, :], start=True, stop=True)
                    last.then_inc(fc1_mm, 1)
                if 1 <= e <= E:
                    f = e - 1
                    pe.wait_ge(hid_rdy, f + 1)
                    if f == 0:
                        pe.wait_ge(oht_rdy, NT)
                    if f >= 2:
                        pe.wait_ge(y_rdy, f - 1)
                    for c in range(EC):
                        last = mm(PS[:, 4 + f % 2, 0:D], hid[:, f % 2, c, :], fc2_sb[:, f, c, :],
                                  start=(c == 0), stop=(c == EC - 1))
                    last.then_inc(fc2_mm, 1)
                if e >= 2:
                    f = e - 2
                    pe.wait_ge(y_rdy, f + 1)
                    for t in range(NT):
                        for j in range(2):
                            last = mm(PS[:, 6 + t // 4, (t % 4) * D:(t % 4 + 1) * D],
                                      ohT[:, f, t * P:(t + 1) * P], y2[:, f % 2, j, :],
                                      start=(f == 0 and t % 4 == 0 and j == 0), stop=(f == E - 1 and j == 1),
                                      skip_group_check=True)
                        if f == E - 1 and t % 4 == 3:
                            last.then_inc(sum_mm, 1)
                        elif t == NT - 1:
                            last.then_inc(sc_mm, 1)

        @block.tensor
        def _(pe):
            mm, tr = nc.tensor.matmul, nc.tensor.transpose

            def film(i):
                for j in range(2):
                    o = 4 * (2 * i + j)
                    last = mm(PS[:, 7, o:o + B], film_w[i][:, j * D:(j + 1) * D], cond_sb[:, :],
                              start=True, stop=True)
                last.then_inc(film_mm, 1)

            pe.wait_ge(film_in, 48)
            film(0)
            pe.wait_ge(ident_in, 16)

            def transposes(i, src, bank0, b):
                pe.wait_ge(xn_rdy[i], b + 1)
                for t in range(TB):
                    last = tr(PS[:, bank0 + b, t * P:(t + 1) * P], src[:, b * TB + t, :], ident)
                last.then_inc(t_done[i], 1)

            def ada():
                pe.wait_ge(film2_in, 32)
                pe.wait_ge(film_rdy, 1)
                film(1)
                pe.wait_ge(silu_rdy, 1)
                pe.wait_ge(film_rdy, 2)
                mm(PS[:, 7, 0:B], wada_sb[:, :], silu[:, 3, :], start=True, stop=True).then_inc(ada_mm, 1)

            def qkv0(b):
                pe.wait_ge(l0_in, 32)
                pe.wait_ge(h_rdy[0], b + 1)
                if b == B - 1:
                    pe.wait_ge(film_rdy, 3)
                h = hT[0][:, b * N:(b + 1) * N]
                mm(PS[:, 4 + b, 0:N], w0[:, 0, :], h, start=True, stop=True)
                mm(PS[:, 4 + b, N:2 * N], w0[:, 1, :], h, start=True, stop=True)
                for t in range(TB):
                    last = mm(PS[:, b, t * P:(t + 1) * P], h[:, t * P:(t + 1) * P], w0[:, 2, :],
                              start=True, stop=True)
                last.then_inc(qkv0_mm, 1)

            def scores0(b):
                pe.wait_ge(qk0_rdy, b + 1)
                for t in range(TB):
                    last = mm(PS[:, 4 + b, t * N:(t + 1) * N], qT0[:, b * N + t * P:b * N + (t + 1) * P],
                              kT0[:, b * N:(b + 1) * N], start=True, stop=True)
                last.then_inc(s0_mm, 1)

            def turn_probs0(b):
                pe.wait_ge(pn0_rdy, b + 1)
                pe.wait_ge(v0_rdy, b + 1)
                for m in range(TB):
                    for t in range(TB):
                        last = tr(PS[:, b, m * N + t * P:m * N + (t + 1) * P], pn0[:, b, t, m * P:(m + 1) * P],
                                  ident)
                last.then_inc(pt0_mm, 1)

            def values0(b):
                pe.wait_ge(pt0_rdy, b + 1)
                for m in range(TB):
                    last = mm(PS[:, 4 + b, 0:N], v0[:, b * TB + m, :], pT0[:, b, m, :],
                              start=(m == 0), stop=(m == TB - 1))
                last.then_inc(o0_mm, 1)

            def project0(b):
                pe.wait_ge(o0_rdy, b + 1)
                for t in range(TB):
                    last = mm(PS[:, b, t * P:(t + 1) * P], oT0[:, b * N + t * P:b * N + (t + 1) * P], w0[:, 3, :],
                              start=True, stop=True)
                last.then_inc(proj_mm, 1)

            def mlp_up(b):
                pe.wait_ge(mlp_in, 32)
                pe.wait_ge(h_rdy[1], b + 1)
                for c in range(FC):
                    last = mm(PS[:, b + 4 * (c // 2), (c % 2) * N:(c % 2 + 1) * N], w1_sb[:, c * P:(c + 1) * P],
                              hT[1][:, b * N:(b + 1) * N], start=True, stop=True)
                    if c % 2:
                        last.then_inc(up_mm, 1)

            def mlp_down(b):
                pe.wait_ge(gel_rdy, b + 1)
                for t in range(TB):
                    for c in range(FC):
                        last = mm(PS[:, b, t * P:(t + 1) * P],
                                  gel[:, c, b * N + t * P:b * N + (t + 1) * P], w2_sb[:, c, :],
                                  start=(c == 0), stop=(c == FC - 1))
                last.then_inc(down_mm, 1)

            def scores(p, s, b, hh):
                u = UP * p + s
                pe.wait_ge(qk_rdy, 4 * (p + s // UP) + b + 1)
                wait(pe, exp_rdy, u - 1)
                hs = slice(hh * HD, (hh + 1) * HD)
                for t in range(TB):
                    last = mm(PS[:, s % 2, t * N:(t + 1) * N], qT[hs, b, t * P:(t + 1) * P], kT[hs, b, :],
                              start=True, stop=True)
                last.then_inc(s_mm, 1)

            def one(p):
                return slice(p, p + 1) if isinstance(p, int) else ds(p, 1)

            def make_qkv(p, t):
                g = NT * p + t
                nt, np_ = (t + 1) % NT, p + (t + 1) // NT
                first = isinstance(p, int) and p <= 0
                if first:
                    if g == NT - 1:
                        pe.wait_ge(v_copied, NT - 1)
                    elif g == NT - 2:
                        pe.wait_ge(qkv_copied, 1)
                    if np_ == 0:
                        pe.wait_ge(h16_rdy, 2 * (nt // TB) + 2)
                else:
                    wait(pe, v_copied, g)
                bank = qkv_bank(p, t)
                if in_range(np_, 0):
                    for n, (i, j) in enumerate(HALVES):
                        last = mm(PS[:, bank, 0:2 * P], h16[:, i, nt * P:(nt + 1) * P],
                                  wqkv16[:, j, one(np_), 0:2 * P], start=(n == 0), stop=(n == 2))
                if in_range(p, 0):
                    for n, (i, j) in enumerate(HALVES):
                        last = mm(PS[:, bank, 2 * P:3 * P], h16[:, i, t * P:(t + 1) * P],
                                  wqkv16[:, j, one(p), 2 * P:3 * P], start=(n == 0), stop=(n == 2))
                last.then_inc(qkv_mm, 1)

            def turn_probs(p, s):
                u = UP * p + s
                pe.wait_ge(exp_rdy, u + 1)
                wait(pe, pt_rdy, u - 1)
                for m in range(TB):
                    for t in range(TB):
                        last = tr(PS[:, 2 + s % 2, m * N + t * P:m * N + (t + 1) * P],
                                  pr[:, s % 2, t, m * P:(m + 1) * P], ident)
                last.then_inc(pt_mm, 1)

            def turn_qk(p, b):
                g = 4 * p + b
                pe.wait_ge(qkn_rdy, g + 1)
                wait(pe, qk_rdy, g)
                for i in range(2):
                    for t in range(TB):
                        last = tr(PS[:, 5, i * N + t * P:i * N + (t + 1) * P], qk_raw[:, b * TB + t, i * P:(i + 1) * P],
                                  ident)
                last.then_inc(qkt_mm, 1)

            def values(p, s):
                u, b, hh = UP * p + s, (s % UP) // 2, s % 2
                pe.wait_ge(pt_rdy, u + 1)
                wait(pe, o_rdy, u)
                for t in range(TB):
                    for m in range(TB):
                        for n, (i, j) in enumerate(HALVES):
                            last = mm(PS[:, 6, t * VD:(t + 1) * VD], pT[:, s % 2, i, m, t * P:(t + 1) * P],
                                      vv[:, j, b * TB + m, hh, :], start=(m == 0 and n == 0),
                                      stop=(m == TB - 1 and n == 2))
                last.then_inc(pv_mm, 1)

            def turn_out(p, b):
                g = 4 * p + b
                pe.wait_ge(o_rdy, 2 * g + 2)
                if isinstance(p, int):
                    wait(pe, ot_rdy, g)
                for t in range(TB):
                    last = tr(PS[:, 7, t * P:(t + 1) * P], on[:, b * TB + t, :], ident)
                last.then_inc(ot_mm, 1)

            def first_qk():
                pe.wait_ge(w16_rdy, 2)
                pe.wait_ge(x2_rdy, B)
                make_qkv(-1, NT - 1)

            def first_slot(s):
                b = s - 2
                if b < B:
                    make_qkv(0, TB * b)
                    if b < B - 1:
                        make_qkv(0, TB * b + 1)
                if 0 <= b - 3 < B - 1:
                    turn_qk(0, b - 3)
                u = s - 5
                if u >= 0:
                    pe.wait_ge(v_copied, u + 1)
                    scores(-1, u + UP, u // 2, u % 2)
                if u >= 1:
                    pe.wait_ge(v_copied, u + 2)
                    turn_probs(-1, u - 1 + UP)
                if b == B:
                    make_qkv(0, NT - 1)
                if u >= 2:
                    pe.wait_ge(ones_rdy, 3)
                    pe.wait_ge(v_copied, 5)
                    values(-1, u - 2 + UP)

            def slot_(p, s):
                if has_unit(p, s + 1):
                    scores(p, s + 1, (s + 1) % UP // 2, (s + 1) % 2)
                if has_unit(p, s):
                    turn_probs(p, s)
                for s0, dp, b in TURN_SLOTS:
                    if s == s0 and in_range(p, dp):
                        turn_qk(p + dp, b)
                if s in (3, 5, 7, 9) and in_range(p, 0):
                    turn_out(p, (s - 3) // 2)
                if has_unit(p, s - 1):
                    values(p, s - 1)
                if in_range(p, 1):
                    make_qkv(p + 1, s - 2)
                elif s > 2:
                    pe.wait_ge(out_in, 64)
                    pe.wait_ge(v_copied, NT * NP)
                    if s > 3:
                        pe.wait_ge(qk_rdy, 4 * NP)
                    for i, a in WOUT_PARTS[s]:
                        wout_product(pe, mm, i, a)

            run_layers(pe, ((3, lambda b: transposes(0, xn[0], 0, b)), (5, qkv0), (7, scores0), (11, turn_probs0),
                            (13, values0), (15, project0), (19, lambda b: transposes(1, xn[1], 4, b)),
                            (21, mlp_up), (23, mlp_down), (27, lambda b: transposes(2, xn[0], 4, b))),
                       {ADA_WAVE: ada, STAGES - 1: first_qk}, first_slot, slot_)
            experts_pe(pe, mm, tr)

        @block.scalar
        def _(act):
            av = nc.scalar.activation
            act.dma_start(film_w[0][:, :], film1_w).then_inc(film_in, 16)
            act.dma_start(cond_sb[:, :], cond).then_inc(film_in, 16)
            act.dma_start(cols_sb[:, :], cols).then_inc(film_in, 16)
            act.dma_start(ident, const32[:, 0:P]).then_inc(ident_in, 16)
            act.dma_start(film_w[1][:, :], film2_w).then_inc(film2_in, 16)
            act.dma_start(wada_sb[:, :], w_ada).then_inc(film2_in, 16)
            act.dma_start(c32[:, P:NCONST], const32[:, P:NCONST]).then_inc(const_in, 16)

            def silu_exps():
                av(silu[:, 0, :], cond_sb[:, :], ACT.Exp, scale=-1.0).then_inc(silu_exp, 1)

            def turned(i, bank0, scale, bias, b):
                act.wait_ge(t_done[i], b + 1)
                av(hT[i][:, b * N:(b + 1) * N], PS[:, bank0 + b, 0:N], ACT.Identity, scale=scale,
                   bias=bias).then_inc(h_rdy[i], 1)

            def film0(b):
                act.wait_ge(film_rdy, 1)
                turned(0, 0, fA[0][:, b:b + 1], fB[0][:, b:b + 1], b)

            def film1(b):
                turned(1, 4, fA[1][:, b:b + 1], fB[1][:, b:b + 1], b)

            def affine1(b):
                act.wait_ge(film_rdy, 4)
                turned(2, 4, col("ln1_g"), fB[2][:, b:b + 1], b)

            def bias_qk0(b):
                act.wait_ge(qkv0_mm, b + 1)
                av(qT0[:, b * N:(b + 1) * N], PS[:, 4 + b, 0:N], ACT.Identity, scale=SCALE0, bias=qbs[:, :])
                av(kT0[:, b * N:(b + 1) * N], PS[:, 4 + b, N:2 * N], ACT.Identity,
                   bias=col("k_b")).then_inc(qk0_rdy, 1)

            def exps0(b):
                act.wait_ge(nm0_rdy, b + 1)
                for t in range(TB):
                    last = av(p0[:, b, t, :], PS[:, 4 + b, t * N:(t + 1) * N], ACT.Exp, bias=nm0[:, b, t:t + 1],
                              accum_out=sum0[:, b, t:t + 1])
                last.then_inc(exp0_rdy, 1)

            def bias_v0(b):
                act.wait_ge(o0_mm, b + 1)
                av(oT0[:, b * N:(b + 1) * N], PS[:, 4 + b, 0:N], ACT.Identity, bias=col("v_b")).then_inc(o0_rdy, 1)

            def high_weights():
                act.wait_ge(wc_rdy, 1)
                av(w_half[0], w_all, ACT.Copy, scale=WS).then_inc(w16_rdy, 1)

            def gelu0(b):
                for c in range(FC):
                    if c % 2 == 0:
                        act.wait_ge(up_mm, 2 * b + c // 2 + 1)
                    last = av(gel[:, c, b * N:(b + 1) * N], PS[:, b + 4 * (c // 2), (c % 2) * N:(c % 2 + 1) * N],
                              ACT.Gelu, bias=col("mlp_b1", c))
                last.then_inc(gel_rdy, 1)

            def copy_qkv(p, t):
                g = NT * p + t
                act.wait_ge(qkv_mm, g + 2)
                nt, np_ = (t + 1) % NT, p + (t + 1) // NT
                bank = qkv_bank(p, t)
                if in_range(np_, 0):
                    last = av(qk_raw[:, nt, :], PS[:, bank, 0:2 * P], ACT.Copy)
                if not in_range(p, 0):
                    last.then_inc(qkv_copied, 1)
                    return
                av(vv[:, 0, t, :, 0:HD], PS[:, bank, 2 * P:3 * P].rearrange("p (h c) -> p h c", c=HD),
                   ACT.Copy).then_inc(qkv_copied, 1)

            def exps(p, s):
                u = UP * p + s
                act.wait_ge(nm_rdy, u + 1)
                wait(act, pt_mm, u - 1)
                for t in range(TB):
                    last = av(pr[:, s % 2, t, :], PS[:, s % 2, t * N:(t + 1) * N], ACT.Exp,
                              bias=nm[:, s % 2, t:t + 1])
                last.then_inc(exp_rdy, 1)

            def norm_qk(p, b):
                g = 4 * p + b
                act.wait_ge(qkt_mm, g + 1)
                av(qT[:, b, :], PS[:, 5, 0:N], ACT.Identity, scale=qg8[:, 0:1], bias=qg8[:, 1:2])
                av(kT[:, b, :], PS[:, 5, N:2 * N], ACT.Identity, scale=col("kn_g"),
                   bias=col("kn_b")).then_inc(qk_rdy, 1)

            def copy_out(p, b):
                g = 4 * p + b
                act.wait_ge(ot_mm, g + 1)
                pp = slice(p, p + 1) if isinstance(p, int) else ds(p, 1)
                av(oT[:, pp, b * N:(b + 1) * N], PS[:, 7, 0:N], ACT.Copy).then_inc(ot_rdy, 1)

            def copy_high(p, s):
                u = UP * p + s
                act.wait_ge(pt_mm, u + 1)
                wait(act, pv_mm, u - 1)
                av(pT[:, s % 2, 0, :, :], PS[:, 2 + s % 2, :].rearrange("p (m n) -> p m n", n=N),
                   ACT.Copy).then_inc(ph_rdy, 1)

            def slot_(p, s):
                if has_unit(p, s):
                    copy_high(p, s)
                if has_unit(p, s + 1):
                    exps(p, s + 1)
                if in_range(p, 1):
                    copy_qkv(p + 1, s - 2)
                for s0, dp, b in TURN_SLOTS:
                    if s == s0 and in_range(p, dp):
                        norm_qk(p + dp, b)
                if s in (3, 5, 7, 9) and in_range(p, 0):
                    copy_out(p, (s - 3) // 2)

            def first_slot(s):
                b = s - 2
                if b < B:
                    copy_qkv(0, TB * b)
                    act.wait_ge(qkv_copied, 2 * b + 2)
                    if b:
                        act.wait_ge(var_rdy, b)
                    raw = qk_raw[:, b * TB:(b + 1) * TB, :]
                    av(qk_sq[:, :, :], raw, ACT.Square).then_inc(sq_rdy, 1)
                    if b < B - 1:
                        copy_qkv(0, TB * b + 1)
                elif b == B:
                    copy_qkv(0, NT - 1)
                if 0 <= b - 3 < B - 1:
                    norm_qk(0, b - 3)
                u = s - 5
                if u >= 1:
                    copy_high(-1, u - 1 + UP)
                if u >= 0:
                    exps(-1, u + UP)

            run_layers(act, ((4, film0), (6, bias_qk0), (9, exps0), (14, bias_v0), (20, film1), (22, gelu0),
                             (28, affine1)),
                       {ADA_WAVE - 1: silu_exps, HIGH_WAVE: high_weights,
                        STAGES - 1: lambda: copy_qkv(-1, NT - 1)}, first_slot, slot_)
            for i in range(2):
                act.wait_ge(x3t_mm, i + 1)
                av(x3T[:, 512 * i:512 * (i + 1)], PS[:, 2 + i, :], ACT.Copy).then_inc(x3t_rdy, 1)
            act.wait_ge(lsub_rdy, 1)
            av(lexp[:, :, :], lsub[:, :, :], ACT.Exp).then_inc(lexp_rdy, 1)
            for i in range(2):
                act.wait_ge(gt_mm, i + 1)
                av(V[:, 512 * i:512 * (i + 1)], PS[:, 5 + i, :], ACT.Copy).then_inc(v_rdy, 1)
            act.wait_ge(nmr_rdy, 1)
            for t in range(NT):
                last = av(xn[1][:, t, :], x3[:, t, :], ACT.Identity, scale=rs[3][:, t:t + 1], bias=nmr[:, t:t + 1])
            last.then_inc(xn3_rdy, 1)
            def copy_slots(t):
                act.wait_ge(oht_mm, t + 1)
                av(ohT[:, :, t * P:(t + 1) * P], PS[:, 2 + t % 4, :].bitcast(bf16).rearrange(
                    "p (e n) -> p e n", e=E), ACT.Copy).then_inc(oht_rdy, 1)

            for t in range(NT - 1):
                copy_slots(t)
            for i in range(2):
                act.wait_ge(gath_mm, i + 1)
                av(gT[:, :, i * HC:(i + 1) * HC], PS[:, i, :].rearrange("p (c e) -> p e c", e=E), ACT.Identity,
                   scale=col("mlp_g"), bias=col("mlp_b")).then_inc(g_rdy, 1)
            copy_slots(NT - 1)
            for e in range(E):
                act.wait_ge(fc1_mm, e + 1)
                if e >= 2:
                    act.wait_ge(fc2_mm, e - 1)
                for c in range(EC):
                    last = av(hid[:, e % 2, c, :], PS[:, e % 2, c * CAP:(c + 1) * CAP], ACT.Gelu_apprx_tanh,
                              bias=col("b1s", e * EC + c))
                last.then_inc(hid_rdy, 1)

        @block.vector
        def _(dve):
            ts, tt, stt = nc.vector.tensor_scalar, nc.vector.tensor_tensor, nc.vector.scalar_tensor_tensor
            red, cp = nc.vector.tensor_reduce, nc.vector.tensor_copy
            steps = [0]

            def link(ins):
                ins.then_inc(dve_step, 1)
                steps[0] += 1
                dve.wait_ge(dve_step, steps[0])

            def row_stats(i, src, n):
                link(nc.vector.bn_stats(stats[:, i, n, :], src[:, n, :]))
                return nc.vector.bn_aggr(mv[:, i, n, :], stats[:, i, n, :])

            def squares(i, src, b):
                for t in range(TB):
                    n = b * TB + t
                    last = nc.vector.tensor_tensor_reduce(out=sq[:, t, :], in0=src[:, n, :], in1=src[:, n, :],
                                                          scale=1.0, scalar=0.0, op0=ALU.mult, op1=ALU.add,
                                                          accum_out=ss[i][:, n:n + 1])
                last.then_inc(ss_rdy[i], 1)

            def scaled(i, src, dst, b):
                dve.wait_ge(rs_rdy[i], b + 1)
                for t in range(TB):
                    n = b * TB + t
                    last = ts(dst[:, n, :], src[:, n, :], rs[i][:, n:n + 1], None, ALU.mult)
                last.then_inc(xn_rdy[i], 1)

            def squares0(b):
                dve.wait_ge(x_in[b], 16)
                if b:
                    dve.wait_ge(ss_rdy[0], b)
                squares(0, x0, b)

            def film(i):
                dve.wait_ge(film_mm, i + 1)
                ts(fA[i][:, :], PS[:, 7, 8 * i:8 * i + B], film1c[:, i:i + 1], col(f"norm{i + 1}_w"), ALU.add,
                   ALU.mult)
                ts(fB[i][:, :], PS[:, 7, 8 * i + 4:8 * i + 4 + B], col(f"film{i + 1}_b", 1), None,
                   ALU.add).then_inc(film_rdy, 1)

            def film_first():
                dve.wait_ge(film_in, 48)
                ts(film1c[:, 0:1], col("film1_b", 0), 1.0, None, ALU.add)
                ts(film1c[:, 1:2], col("film2_b", 0), 1.0, None, ALU.add)
                link(ts(qbs[:, :], col("q_b"), SCALE0, None, ALU.mult))
                film(0)

            def shift1():
                dve.wait_ge(silu_exp, 1)
                link(ts(silu[:, 1, :], silu[:, 0, :], 1.0, None, ALU.add))
                link(nc.vector.reciprocal(silu[:, 2, :], silu[:, 1, :]))
                tt(silu[:, 3, :], cond_sb[:, :], silu[:, 2, :], ALU.mult).then_inc(silu_rdy, 1)
                film(1)
                dve.wait_ge(ada_mm, 1)
                ts(fB[2][:, :], PS[:, 7, 0:B], col("b_ada"), col("ln1_b"), ALU.add, ALU.add).then_inc(film_rdy, 1)
                ts(qg8[:, 0:1], col("qn_g"), HD ** -0.5, None, ALU.mult)
                ts(qg8[:, 1:2], col("qn_b"), HD ** -0.5, None, ALU.mult).then_inc(film_rdy, 1)

            def copy_v0(b):
                dve.wait_ge(qkv0_mm, b + 1)
                cp(tiles(v0, b), PS[:, b, 0:N].rearrange("p (t d) -> p t d", d=D)).then_inc(v0_rdy, 1)

            def row_max0(b):
                dve.wait_ge(s0_mm, b + 1)
                red(nm0[:, b, :], PS[:, 4 + b, :].rearrange("p (t m) -> p t m", m=N), AX.X, ALU.max,
                    negate=True).then_inc(nm0_rdy, 1)

            def normalize0(b):
                dve.wait_ge(exp0_rdy, b + 1)
                link(nc.vector.reciprocal(rec0[:, b, :], sum0[:, b, :]))
                for t in range(TB):
                    last = ts(pn0[:, b, t, :], p0[:, b, t, :], rec0[:, b, t:t + 1], None, ALU.mult)
                last.then_inc(pn0_rdy, 1)

            def copy_probs0(b):
                dve.wait_ge(pt0_mm, b + 1)
                cp(pT0[:, b, :, :], PS[:, b, :].rearrange("p (t m) -> p t m", m=N)).then_inc(pt0_rdy, 1)

            def mean_weights():
                dve.wait_ge(qkvw_in, 16)
                link(red(wsum[:, :, :], wqkv_sb[:, :, 0:2, :].rearrange("p a g (h c) -> p a (g h) c", c=HD), AX.X,
                         ALU.add))
                ts(wmean[:, :, :], wsum[:, :, :], -1.0 / HD, None, ALU.mult).then_inc(wsum_rdy, 1)

            def low_weights():
                dve.wait_ge(w16_rdy, 1)
                stt(w_half[1], w_all, WS, w_half[0], ALU.mult, ALU.subtract).then_inc(w16_rdy, 1)

            def residual1(b):
                dve.wait_ge(proj_mm, b + 1)
                dve.wait_ge(xpb_rdy, b + 1)
                tt(tiles(x1, b), PS[:, b, 0:N].rearrange("p (t d) -> p t d", d=D), tiles(xpb, b),
                   ALU.add).then_inc(x1_rdy, 1)
                dve.wait_ge(x1_rdy, b + 1)
                if b:
                    dve.wait_ge(ss_rdy[1], b)
                else:
                    dve.wait_ge(ss_rdy[0], B)
                squares(1, x1, b)

            def residual2(b):
                dve.wait_ge(down_mm, b + 1)
                dve.wait_ge(x1b_rdy, b + 1)
                tt(tiles(x2, b), PS[:, b, 0:N].rearrange("p (t d) -> p t d", d=D), tiles(x1b, b),
                   ALU.add).then_inc(x2_rdy, 1)
                dve.wait_ge(x2_rdy, b + 1)
                for t in range(TB):
                    last = row_stats(0, x2, b * TB + t)
                last.then_inc(ss_rdy[2], 1)

            def normed2(b):
                dve.wait_ge(rs_rdy[2], b + 1)
                dve.wait_ge(t_done[0], b + 1)
                for t in range(TB):
                    n = b * TB + t
                    last = ts(xn[0][:, n, :], x2[:, n, :], mv[:, 0, n, 0:1], rs[2][:, n:n + 1], ALU.subtract,
                              ALU.mult)
                last.then_inc(xn_rdy[2], 1)

            def halve_input(b):
                dve.wait_ge(h_rdy[2], b + 1)
                h = hT[2][:, b * N:(b + 1) * N]
                cp(h16[:, 0, b * N:(b + 1) * N], h).then_inc(h16_rdy, 1)
                dve.wait_ge(h16_rdy, 2 * b + 1)
                tt(h16[:, 1, b * N:(b + 1) * N], h, h16[:, 0, b * N:(b + 1) * N], ALU.subtract).then_inc(h16_rdy, 1)

            def row_max(p, s):
                u = UP * p + s
                dve.wait_ge(s_mm, u + 1)
                wait(dve, exp_rdy, u - 1)
                red(nm[:, s % 2, :], PS[:, s % 2, :].rearrange("p (t m) -> p t m", m=N), AX.X, ALU.max,
                    negate=True).then_inc(nm_rdy, 1)

            def copy_low(p, s):
                u = UP * p + s
                dve.wait_ge(ph_rdy, u + 1)
                tt(pT[:, s % 2, 1, :, :], PS[:, 2 + s % 2, :].rearrange("p (m n) -> p m n", n=N),
                   pT[:, s % 2, 0, :, :], ALU.subtract).then_inc(pt_rdy, 1)

            def copy_v_low(p, t):
                g = NT * p + t
                dve.wait_ge(qkv_copied, g + 2)
                tt(vv[:, 1, t, :, 0:HD], PS[:, qkv_bank(p, t), 2 * P:3 * P].rearrange("p (h c) -> p h c", c=HD),
                   vv[:, 0, t, :, 0:HD], ALU.subtract).then_inc(v_copied, 1)

            def scale_qk(b):
                dve.wait_ge(rs1_rdy, b + 1)
                raw = qk_raw[:, b * TB:(b + 1) * TB, :].rearrange("p t (h c) -> p (t h) c", c=HD)
                tt(raw, raw, qk_rs[:, :].unsqueeze(2).broadcast_to([P, 4 * TB, HD]), ALU.mult).then_inc(qkn_rdy, 1)

            def sum_squares(p, b):
                g = 4 * p + b
                dve.wait_ge(sq_rdy, g + 1)
                red(qk_ss[:, :], qk_sq[:, :, :].rearrange("p t (h c) -> p (t h) c", c=HD), AX.X,
                    ALU.add).then_inc(qkss_rdy, 1)
                dve.wait_ge(qkss_rdy, g + 1)
                wait(dve, rs1_rdy, g)
                ts(qk_var[:, :], qk_ss[:, :], 1.0 / HD, EPS1 * WS * WS, ALU.mult, ALU.add).then_inc(var_rdy, 1)

            def normalize(p, s):
                u, b, hh = UP * p + s, (s % UP) // 2, s % 2
                dve.wait_ge(pv_mm, u + 1)
                o = PS[:, 6, 0:TB * VD].rearrange("p (t c) -> p t c", c=VD)
                nc.vector.reciprocal(rec[:, s % 2, :], o[:, :, HD]).then_inc(rec_rdy, 1)
                dve.wait_ge(rec_rdy, u + 1)
                tt(on[:, b * TB:(b + 1) * TB, hh * HD:(hh + 1) * HD], o[:, :, 0:HD],
                   rec[:, s % 2, :].unsqueeze(2).broadcast_to([P, TB, HD]), ALU.mult).then_inc(o_rdy, 1)

            def first_slot(s):
                b = s - 2
                if b < B:
                    copy_v_low(0, TB * b)
                    sum_squares(0, b)
                    if b < B - 1:
                        copy_v_low(0, TB * b + 1)
                elif b == B:
                    copy_v_low(0, NT - 1)
                if 0 < b <= B:
                    scale_qk(b - 1)
                u = s - 5
                if u >= 0:
                    row_max(-1, u + UP)
                if u >= 2:
                    normalize(-1, u - 2 + UP)
                if u >= 1:
                    copy_low(-1, u - 1 + UP)

            def slot_(p, s):
                if has_unit(p, s + 1):
                    row_max(p, s + 1)
                for s0, dp, b in SUM_SLOTS:
                    if s == s0 and in_range(p, dp):
                        sum_squares(p + dp, b)
                if has_unit(p, s - 1):
                    normalize(p, s - 1)
                if has_unit(p, s):
                    copy_low(p, s)
                if in_range(p, 1):
                    copy_v_low(p + 1, s - 2)

            run_layers(dve, ((0, squares0), (2, lambda b: scaled(0, x0, xn[0], b)), (6, copy_v0), (8, row_max0),
                             (10, normalize0), (12, copy_probs0), (16, residual1),
                             (18, lambda b: scaled(1, x1, xn[1], b)), (24, residual2), (26, normed2),
                             (29, halve_input)),
                       {FILM_WAVE: film_first, ADA_WAVE: shift1, MEAN_WAVE: mean_weights,
                        LOW_WAVE: low_weights}, first_slot, slot_)

            for i in range(2):
                dve.wait_ge(wo_mm, i + 1)
                tt(x3[:, 4 * i:4 * i + 4, :], PS[:, 4 + i, :].rearrange("p (t d) -> p t d", d=D),
                   x2[:, 4 * i:4 * i + 4, :], ALU.add).then_inc(x3_rdy, 1)
            dve.wait_ge(x3_rdy, 2)
            for t in range(NT):
                last = nc.vector.bn_stats(stats[:, 1, t, :], x3[:, t, :])
            link(last)
            for t in range(NT):
                last = nc.vector.bn_aggr(mv[:, 1, t, :], stats[:, 1, t, :])
            last.then_inc(ss_rdy[3], 1)
            dve.wait_ge(lg_mm, 1)
            lg = PS[:, 0, 0:NT * E].rearrange("p (t e) -> p t e", e=E)
            link(red(lmax[:, :], lg, AX.X, ALU.max))
            tt(lsub[:, :, :], lg, lmax[:, :].unsqueeze(2).broadcast_to([P, NT, E]), ALU.subtract).then_inc(lsub_rdy, 1)
            dve.wait_ge(lexp_rdy, 1)
            link(red(lsum[:, :], lexp[:, :, :], AX.X, ALU.add))
            link(nc.vector.reciprocal(lrec[:, :], lsum[:, :]))
            link(tt(gate[:, :, :].rearrange("p e t -> p t e"), lexp[:, :, :],
                    lrec[:, :].unsqueeze(2).broadcast_to([P, NT, E]), ALU.mult))
            cp(gx[:, :, :, :], gate[:, :, :].rearrange("p e t -> p t e").unsqueeze(3).broadcast_to([P, NT, E, GR]))\
                .then_inc(gx_rdy, 1)
            cp(gx2[:, :, :, :], gate[:, :, :].unsqueeze(3).broadcast_to([P, E, NT, 2])).then_inc(gx_rdy, 1)
            cp(g3[:, :, :, 0], gate[:, :, :]).then_inc(g3_rdy, 1)
            dve.wait_ge(g3_rdy, 1)
            link(tt(gr[:, 0, :, :], gate[:, :, :], g3[:, :, :, 0], ALU.subtract))
            cp(g3[:, :, :, 1], gr[:, 0, :, :]).then_inc(g3_rdy, 1)
            dve.wait_ge(g3_rdy, 2)
            link(tt(gr[:, 1, :, :], gr[:, 0, :, :], g3[:, :, :, 1], ALU.subtract))
            cp(g3[:, :, :, 2], gr[:, 1, :, :]).then_inc(g3_rdy, 1)
            dve.wait_ge(const_in, 16)
            cp(iotab[:, :, :], c32[:, P:2 * P].unsqueeze(2).broadcast_to([P, CAP, E])).then_inc(constb_rdy, 1)
            cp(identb[:, :], ident).then_inc(constb_rdy, 1)
            dve.wait_ge(out_in, 64)
            link(cp(blockb[:, :], cm[:, 0, :]))
            dve.wait_ge(rs_rdy[3], 1)
            stt(nmr[:, :], mv[:, 1, :, 0], -1.0, rs[3][:, :], ALU.mult, ALU.mult).then_inc(nmr_rdy, 1)

            dve.wait_ge(gt_mm, 3)
            link(cp(V2[:, :], PS[:, 7, 0:P]))
            nc.vector.memset(digit[:, :], 0)
            link(nc.vector.memset(prefix[:, :], 0))
            cp(thr[:, :], ci[:, 0:1]).then_inc(thr_rdy, 1)
            V16 = V[:, :].bitcast(u16).rearrange("p (n h) -> p n h", h=2)
            for i in range(2):
                dve.wait_ge(v_rdy, i + 1)
                cp(upper[:, 512 * i:512 * (i + 1)], V16[:, 512 * i:512 * (i + 1), 1]).then_inc(upper_rdy, 1)
            dve.wait_ge(upper_rdy, 2)
            for r in range(NR):
                values = upper[:, :].bitcast(bf16) if SHIFTS[r] >= 16 else V[:, :]
                dve.wait_ge(thr_rdy, r + 1)
                ts(ge[:, :], values, thr[:, :].bitcast(f32), None, ALU.is_ge, ALU.add,
                   accum_out=cnt[:, 0:1]).then_inc(cnt_rdy, 1)
                dve.wait_ge(cnt_rdy, r + 1)
                ts(okb[:, :], cnt[:, 0:1], float(CAP), None, ALU.is_ge).then_inc(ok_rdy, 1)
                tt(prefix[:, :], prefix[:, :], digit[:, :], ALU.bitwise_or).then_inc(prefix_rdy, 1)
                dve.wait_ge(prefix_rdy, r + 1)
                tt(trial[:, :], prefix[:, :], ci[:, r + 1:r + 2], ALU.bitwise_or).then_inc(trial_rdy, 1)
                dve.wait_ge(k_mm, r + 1)
                ts(digit[:, :], PS[:, 4, 0:1], -1.0, c32[:, r + 2 * P:r + 2 * P + 1], ALU.add, ALU.mult)\
                    .then_inc(dig_rdy, 1)
                dve.wait_ge(dig_rdy, r + 1)
                dve.wait_ge(trial_rdy, r + 1)
                tt(thr[:, :], trial[:, :], digit[:, :], ALU.bitwise_or).then_inc(thr_rdy, 1)
            dve.wait_ge(thr_rdy, NR + 1)

            kth = thr[:, :].bitcast(f32)
            link(ts(gt[:, :], V2[:, :], kth, None, ALU.is_gt, ALU.add, accum_out=cnt[:, 1:2]))
            ts(eq[:, :], V2[:, :], kth, None, ALU.is_equal, ALU.add, accum_out=cnt[:, 2:3]).then_inc(tie_rdy, 1)
            dve.wait_ge(tie_rdy, 1)
            nc.vector.tensor_tensor_scan(scan1[:, :], eq[:, :], zero[:, :], 0.0, ALU.add, ALU.add)
            dve.wait_ge(tie_mm, 1)
            link(ts(need[:, :], PS[:, 5, 0:1], -1.0, float(CAP), ALU.mult, ALU.add))
            link(stt(sel[:, :], scan1[:, :], need[:, :], eq[:, :], ALU.is_le, ALU.mult))
            stt(mask[:, :], gt[:, :], 0.0, sel[:, :], ALU.add, ALU.add, accum_out=cnt[:, 3:4]).then_inc(off_rdy, 1)
            dve.wait_ge(off_rdy, 1)
            link(nc.vector.tensor_tensor_scan(scan2[:, :], mask[:, :], zero[:, :], 0.0, ALU.add, ALU.add))
            dve.wait_ge(off_mm, 1)
            stt(slot[:, :], scan2[:, :], PS[:, 6, 0:1], mask[:, :], ALU.add, ALU.mult).then_inc(slot_rdy, 1)
            dve.wait_ge(slot_mm, 1)
            link(cp(slotT[:, :, :], PS[:, 7, 0:P].rearrange("p (e t j) -> p t e j", t=NT, j=2)[:, :, :, 0]))
            dve.wait_ge(constb_rdy, 2)
            for t in range(NT):
                tt(OH[:, t, :, :], iotab[:, :, :], slotT[:, t, :].unsqueeze(1).broadcast_to([P, CAP, E]),
                   ALU.is_equal).then_inc(oh_rdy, 1)
            dve.wait_ge(w_mm, 1)
            link(red(wsel[:, :], PS[:, 7, 0:3 * E].rearrange("p (e j) -> p e j", j=3), AX.X, ALU.add))
            dve.wait_ge(fc_in, 48)
            tt(b2_sb[:, :, :], b2_sb[:, :, :], wsel[:, :].unsqueeze(2).broadcast_to([P, E, D]),
               ALU.mult).then_inc(b2w_rdy, 1)
            dve.wait_ge(b2w_rdy, 1)
            for f in range(E):
                y = ys[:, f % 2, :]
                dve.wait_ge(fc2_mm, f + 1)
                if f >= 1:
                    dve.wait_ge(y_rdy, f)
                if f >= 2:
                    dve.wait_ge(sc_mm, f - 1)
                link(stt(y, PS[:, 4 + f % 2, 0:D], wsel[:, f:f + 1], b2_sb[:, f, :], ALU.mult, ALU.add))
                link(cp(y2[:, f % 2, 0, :], y))
                tt(y2[:, f % 2, 1, :], y, y2[:, f % 2, 0, :], ALU.subtract).then_inc(y_rdy, 1)
            for i in range(2):
                dve.wait_ge(sum_mm, i + 1)
                tt(y_out[:, 4 * i:4 * i + 4, :], PS[:, 6 + i, :].rearrange("p (t d) -> p t d", d=D),
                   x3[:, 4 * i:4 * i + 4, :], ALU.add).then_inc(out_rdy, 1)


def kernel(**inputs):
    import numpy as np
    import concourse.bacc as bacc
    from concourse.bass_utils import run_bass_kernel_spmd as run

    a = {k: np.asarray(v) for k, v in inputs.items()}
    g0 = lambda n: a["L0_cond_" + n]
    g1 = lambda n: a["L1_cond_" + n]
    columns = {n: g0(n) for n in ("norm1_w", "film1_b", "q_b", "k_b", "v_b", "norm2_w", "film2_b", "mlp_b1")}
    columns.update({n: g1(n) for n in ("b_ada", "ln1_g", "ln1_b", "mlp_g", "mlp_b", "b1s")})
    for n in ("qn_g", "qn_b", "kn_g", "kn_b"):
        columns[n] = np.tile(g1(n), 2)
    cols = np.concatenate([columns[n].reshape(-1, P).T for n in COLS], axis=1)
    part = np.arange(P)
    const32 = np.concatenate([np.eye(P), np.broadcast_to(part + 1, (P, P)),
                              np.broadcast_to(2.0 ** np.array(SHIFTS), (P, NR))], axis=1).astype(np.float32)
    digits = [np.minimum(part % GR, 4) << 28] + [(part % GR) << s for s in SHIFTS[1:]] + [part * 0]
    consti = np.stack(digits, axis=1).astype(np.int32)
    same = (part[:, None] // GR == part[None, :] // GR)
    tile_of, first = part % GR // 2, (part % 2 == 0)[:, None]
    constm = np.stack([same, same & first, same & first & (tile_of[:, None] < tile_of[None, :])],
                      axis=1).astype(np.float32)
    arrays = {
        "x": a["x"].reshape(TOK, D), "cols": cols, "cond": a["cond_1024"].T, "film1_w": g0("film1_w"),
        "film2_w": g0("film2_w"),
        "wqkvp0": np.stack([g0(n) for n in ("q_w", "k_w", "v_w", "proj_w")], axis=1),
        "w_ada": g1("W_ada").T, "mlp_w1": g0("mlp_w1"), "mlp_w2": g0("mlp_w2").reshape(FC, P, D).transpose(1, 0, 2),
        "rows": np.broadcast_to(np.stack([g0("proj_b"), g0("mlp_b2")]), (P, 2, D)),
        "wqkv": g1("Wqkv").reshape(3, NP, P, D).transpose(3, 1, 0, 2),
        "wout": g1("Wout").reshape(D, NP, P).transpose(2, 1, 0), "wgate": g1("Wgate").T,
        "fc1": g1("fc1s").transpose(2, 0, 1), "fc2": g1("fc2s").reshape(E, D, EC, P).transpose(3, 0, 2, 1),
        "b2s": np.broadcast_to(g1("b2s"), (P, E, D)), "const32": const32, "consti": consti, "constm": constm,
    }
    nc = bacc.Bacc("TRN2", target_bir_lowering=False, num_devices=1)
    arrays = {f"in_{k}": np.ascontiguousarray(v) for k, v in arrays.items()}
    args = [nc.dram_tensor(k, v.shape, mybir.dt.from_np(v.dtype), kind="ExternalInput").ap()
            for k, v in arrays.items()]
    args.append(nc.dram_tensor("out_0", (TOK, D), mybir.dt.float32, kind="ExternalOutput").ap())
    conditioned_sequence_kernel(nc, *args)
    r = run(nc, [arrays], core_ids=[0])
    return r.results[0]["out_0"].reshape(B, N, D)
```
